# Optimizing a Trainium2 kernel written in Bass

```python
import numpy as np
import jax
import jax.numpy as jnp

def _softmax(x, axis=-1):
    return jax.nn.softmax(x, axis=axis)

def _gelu(x):
    return jax.nn.gelu(x, approximate=True)

def _silu(x):
    return jax.nn.silu(x)

def _sigmoid(x):
    return jax.nn.sigmoid(x)

def _layernorm(x, axis=-1, eps=1e-05):
    m = jnp.mean(x, axis=axis, keepdims=True)
    v = jnp.var(x, axis=axis, keepdims=True)
    return (x - m) / jnp.sqrt(v + eps)

def _scatter_add(tgt, idx, src, axis=0):
    return tgt.at[idx].add(src)

def _segment_sum(src, seg, n):
    return jax.ops.segment_sum(src, seg, n)
kernel_name = 'mk_adaln_d1_jaxref_r4_ea2fef'

def setup_inputs(seed: int=0):
    np.random.seed(seed)
    _w = jnp.asarray

    def _L0_attn_setup():
        import jax, jax.numpy as jnp
        import numpy as np
        D_MODEL, D_STATE, D_CONV, EXPAND = (256, 16, 4, 2)
        D_INNER = EXPAND * D_MODEL
        B, L = (2, 1024)
        LN_EPS = 1e-05

        def _layernorm(x, gamma, beta):
            mu = jnp.mean(x, axis=-1, keepdims=True)
            var = jnp.mean(jnp.square(x - mu), axis=-1, keepdims=True)
            return (x - mu) * jax.lax.rsqrt(var + LN_EPS) * gamma + beta

        def _causal_depthwise_conv(xp, conv_w, conv_b):
            lhs = jnp.pad(xp.transpose(0, 2, 1), ((0, 0), (0, 0), (D_CONV - 1, 0)))
            out = jax.lax.conv_general_dilated(lhs, conv_w, window_strides=(1,), padding='VALID', dimension_numbers=('NCH', 'OIH', 'NCH'), feature_group_count=D_INNER)
            return out.transpose(0, 2, 1) + conv_b
        key = jax.random.key(seed)
        ks = jax.random.split(key, 6)
        x = jax.random.normal(ks[0], (B, L, D_MODEL), dtype=jnp.float32)
        ln_gamma = jnp.ones((D_MODEL,), jnp.float32)
        ln_beta = jnp.zeros((D_MODEL,), jnp.float32)
        W_in = jax.random.normal(ks[1], (2 * D_INNER, D_MODEL), jnp.float32) / np.sqrt(D_MODEL).astype(np.float32)
        conv_w = jax.random.normal(ks[2], (D_INNER, 1, D_CONV), jnp.float32) * 0.1
        conv_b = jnp.zeros((D_INNER,), jnp.float32)
        W_out = jax.random.normal(ks[3], (D_MODEL, D_INNER), jnp.float32) / np.sqrt(D_INNER).astype(np.float32)
        A = jnp.eye(D_STATE, dtype=jnp.float32)
        Bm = jax.random.normal(ks[4], (D_STATE, D_INNER), jnp.float32) * 0.01
        Cm = jax.random.normal(ks[5], (D_STATE, D_INNER), jnp.float32) * 0.01
        return dict(x=x, ln_gamma=ln_gamma, ln_beta=ln_beta, W_in=W_in, conv_w=conv_w, conv_b=conv_b, W_out=W_out, A=A, Bm=Bm, Cm=Cm)
    _L0_attn_in = _L0_attn_setup()

    def _L0_ffn_setup():
        import jax, jax.numpy as jnp
        import numpy as np
        E, H, I = (8, 256, 1024)
        B, S = (4, 512)
        key = jax.random.key(seed)
        k0, k1, k2, k3 = jax.random.split(key, 4)
        s = 0.02
        return {'hidden_states': jax.random.normal(k0, (B, S, H), dtype=jnp.float32), 'w1': jax.random.normal(k1, (E, H, I), dtype=jnp.float32) * s, 'b1': jnp.zeros((E, I), dtype=jnp.float32), 'w2': jax.random.normal(k2, (E, I, H), dtype=jnp.float32) * s, 'b2': jnp.zeros((E, H), dtype=jnp.float32), 'wr': jax.random.normal(k3, (H, E), dtype=jnp.float32) * s, 'br': jnp.zeros((E,), dtype=jnp.float32)}
    _L0_ffn_in = _L0_ffn_setup()
    _L0_c = _w((lambda *s: np.random.randn(*s).astype(np.float32) * 0.05)(8, 256))
    _L0_wmod = _w((lambda *s: np.random.randn(*s).astype(np.float32) * 0.05)(256, 6 * 256) * 256 ** (-0.5))
    _d = {'L0_attn_x': _L0_attn_in['x'], 'L0_attn_ln_gamma': _L0_attn_in['ln_gamma'], 'L0_attn_ln_beta': _L0_attn_in['ln_beta'], 'L0_attn_W_in': _L0_attn_in['W_in'], 'L0_attn_conv_w': _L0_attn_in['conv_w'], 'L0_attn_conv_b': _L0_attn_in['conv_b'], 'L0_attn_W_out': _L0_attn_in['W_out'], 'L0_attn_A': _L0_attn_in['A'], 'L0_attn_Bm': _L0_attn_in['Bm'], 'L0_attn_Cm': _L0_attn_in['Cm'], 'L0_ffn_w1': _L0_ffn_in['w1'], 'L0_ffn_b1': _L0_ffn_in['b1'], 'L0_ffn_w2': _L0_ffn_in['w2'], 'L0_ffn_b2': _L0_ffn_in['b2'], 'L0_ffn_wr': _L0_ffn_in['wr'], 'L0_ffn_br': _L0_ffn_in['br'], 'L0_c': _L0_c, 'L0_wmod': _L0_wmod}
    _x0 = _d['L0_attn_x']
    _d['L0_attn_x'] = jax.random.normal(jax.random.fold_in(jax.random.key(seed), 1), (8, 512, 256), dtype=_x0.dtype)
    del _x0
    return _d

def reference(L0_attn_x, L0_attn_ln_gamma, L0_attn_ln_beta, L0_attn_W_in, L0_attn_conv_w, L0_attn_conv_b, L0_attn_W_out, L0_attn_A, L0_attn_Bm, L0_attn_Cm, L0_ffn_w1, L0_ffn_b1, L0_ffn_w2, L0_ffn_b2, L0_ffn_wr, L0_ffn_br, L0_c, L0_wmod):

    def _L0_attn_ref(x, ln_gamma, ln_beta, W_in, conv_w, conv_b, W_out, A, Bm, Cm):
        import jax, jax.numpy as jnp
        import numpy as np
        D_MODEL, D_STATE, D_CONV, EXPAND = (256, 16, 4, 2)
        D_INNER = EXPAND * D_MODEL
        B, L = (2, 1024)
        LN_EPS = 1e-05

        def _layernorm(x, gamma, beta):
            mu = jnp.mean(x, axis=-1, keepdims=True)
            var = jnp.mean(jnp.square(x - mu), axis=-1, keepdims=True)
            return (x - mu) * jax.lax.rsqrt(var + LN_EPS) * gamma + beta

        def _causal_depthwise_conv(xp, conv_w, conv_b):
            lhs = jnp.pad(xp.transpose(0, 2, 1), ((0, 0), (0, 0), (D_CONV - 1, 0)))
            out = jax.lax.conv_general_dilated(lhs, conv_w, window_strides=(1,), padding='VALID', dimension_numbers=('NCH', 'OIH', 'NCH'), feature_group_count=D_INNER)
            return out.transpose(0, 2, 1) + conv_b
        xn = _layernorm(x, ln_gamma, ln_beta)
        xz = jnp.einsum('bld,ed->ble', xn, W_in)
        x_part, z = jnp.split(xz, 2, axis=-1)
        x_conv = jax.nn.silu(_causal_depthwise_conv(x_part, conv_w, conv_b))
        u_seq = x_part.transpose(1, 0, 2)
        xc_seq = x_conv.transpose(1, 0, 2)
        z_seq = z.transpose(1, 0, 2)

        def step(state, inp):
            u_t, xc_t, z_t = inp
            state = state @ A.T + u_t @ Bm.T
            out = (xc_t + state @ Cm) * jax.nn.sigmoid(z_t)
            return (state, out)
        state0 = jnp.zeros((x.shape[0], D_STATE), x.dtype)
        _, ys = jax.lax.scan(step, state0, (u_seq, xc_seq, z_seq))
        y = ys.transpose(1, 0, 2)
        residual = jnp.einsum('bli,di->bld', y, W_out)
        return x + residual

    def _L0_ffn_ref(hidden_states, w1, b1, w2, b2, wr, br):
        import jax, jax.numpy as jnp
        import numpy as np
        E, H, I = (8, 256, 1024)
        B, S = (4, 512)
        b, s, h = hidden_states.shape
        x = hidden_states.reshape(-1, h)
        logits = x @ wr + br
        probs = jax.nn.softmax(logits, axis=-1)
        top_p, top_i = jax.lax.top_k(probs, 2)
        gate = top_p[:, 0] / (top_p[:, 0] + top_p[:, 1])
        top1 = top_i[:, 0]
        out = jnp.zeros_like(x)
        n_experts = w1.shape[0]
        for e in range(n_experts):
            hmid = jax.nn.gelu(x @ w1[e] + b1[e], approximate=False)
            hout = hmid @ w2[e] + b2[e]
            mask = top1 == e
            out = out + jnp.where(mask[:, None], hout * gate[:, None], 0.0)
        return out.reshape(b, s, h)
    x = L0_attn_x
    mod = (_silu(L0_c) @ L0_wmod).reshape(L0_c.shape[0], 6, 1, -1)
    sa, ca, ga, sb, cb, gb = (mod[:, 0], mod[:, 1], mod[:, 2], mod[:, 3], mod[:, 4], mod[:, 5])
    ga = (2 * (ga >= 0) - 1) * jnp.maximum(jnp.abs(ga), 0.25)
    gb = (2 * (gb >= 0) - 1) * jnp.maximum(jnp.abs(gb), 0.25)
    h = _layernorm(x, axis=-1) * (1 + ca) + sa
    x = x + ga * _L0_attn_ref(h, L0_attn_ln_gamma, L0_attn_ln_beta, L0_attn_W_in, L0_attn_conv_w, L0_attn_conv_b, L0_attn_W_out, L0_attn_A, L0_attn_Bm, L0_attn_Cm)
    h = _layernorm(x, axis=-1) * (1 + cb) + sb
    x = x + gb * _L0_ffn_ref(h, L0_ffn_w1, L0_ffn_b1, L0_ffn_w2, L0_ffn_b2, L0_ffn_wr, L0_ffn_br)
    return x

_drawn_inputs = setup_inputs


def setup_inputs(seed=0):
    import zlib

    import numpy as np

    out = dict(_drawn_inputs(seed))
    spreads = {'L0_attn_ln_gamma': (1.0, 0.6),
     'L0_attn_ln_beta': (0.0, 0.1),
     'L0_attn_conv_b': (0.0, 0.8),
     'L0_ffn_b1': (0.0, 0.8),
     'L0_ffn_b2': (0.0, 0.594),
     'L0_ffn_br': (0.0, 0.466)}
    factors = {'L0_attn_conv_w': 3.804, 'L0_ffn_w1': 3.851, 'L0_ffn_w2': 3.584, 'L0_ffn_wr': 3.064}
    for name, (base, spread) in spreads.items():
        noise = np.random.default_rng([zlib.crc32(name.encode()), seed]).standard_normal(out[name].shape)
        drawn = base * np.exp(spread * noise) if base else spread * noise
        out[name] = jnp.asarray(drawn.astype(out[name].dtype))
    for name, factor in factors.items():
        out[name] = (out[name] * factor).astype(out[name].dtype)
    return out
```

```python
from contextlib import ExitStack

import concourse.bass as bass
from concourse import mybir

F32 = mybir.dt.float32
BF16 = mybir.dt.bfloat16
I32 = mybir.dt.int32
ALU = mybir.AluOpType
ACT = mybir.ActivationFunctionType
AX = mybir.AxisListType

P = 128
EPS = 1e-5


class Step:
    TURN = 1

    def __init__(self, turn, place):
        self.turn, self.place = turn, place

    def __add__(self, k):
        n = self.place + k
        return type(self)(self.turn + n // self.TURN, n % self.TURN)

    @property
    def n(self):
        return self.turn * self.TURN + self.place


class Batch(Step):
    TURN = 2


class Tile(Step):
    TURN = 4


def bcast(ap, axis, n):
    ap = ap.unsqueeze(axis)
    shape = list(ap.shape)
    shape[axis] = n
    return ap.to_broadcast(shape)


def adaln_mamba_moe(nc, x, gamma, beta, W_in, W_inT, conv_w, conv_b, W_outT, A, AT, BmT, Cm,
                    w1, b1, w2, b2, wr, br, cT, wmod, out):
    B, L, D = x.shape
    T = B * L
    DI = W_outT.shape[0]
    NS = A.shape[0]
    E, _, FF = w1.shape
    KD = D // P
    KC = DI // P
    KF = FF // P
    JT = L // P
    NT = T // P
    CH = P // NS
    NC = L // CH
    LEVELS = NC.bit_length() - 1
    TAPS = conv_w.shape[2]
    SLOTS = (T - E) // P + E
    NM = wmod.shape[1] // D
    GB = (NM - 1) * D
    WE = KD * FF
    FAR = 2 * T

    table = nc.dram_tensor("token_rows", [T, 3 * D], F32).ap()
    mod_dram = nc.dram_tensor("mod_rows", [B, NM * D], F32).ap()
    gb_dram = nc.dram_tensor("gb_rows", [B, D], F32).ap()
    bias_dram = nc.dram_tensor("bias_parts", [3, E * (FF + D)], BF16).ap()

    ctx = ExitStack()
    with ctx:
        def sb(name, shape, dt=F32):
            return ctx.enter_context(nc.sbuf_tensor(name, shape, dt))

        def sem(name):
            return ctx.enter_context(nc.semaphore(name))

        experts = sb("experts", [P, E, WE + KF * D])
        proj = sb("proj", [P, KD * 2 * DI + KC * D + 2 * JT * D])
        w_in = proj[:, 0:KD * 2 * DI].rearrange("p (k n) -> p k n", k=KD)
        w_out = proj[:, 2048:3072].rearrange("p (k n) -> p k n", k=KC)
        x_sb = proj[:, 3072:5120].rearrange("p (b j d) -> p b j d", b=2, j=JT)
        mods = sb("mods", [P, 2 * 3 * D + 2 * 2 * D + 2 * JT * D])
        mod_in = mods[:, 0:1024].rearrange("p (b v d) -> p b v d", b=2, v=2)
        mod_post = mods[:, 1024:2560].rearrange("p (b v d) -> p b v d", b=2, v=3)
        h_sb = mods[:, 2560:3584].rearrange("p (j d) -> p j d", j=JT)
        xn_sb = mods[:, 3584:4608].rearrange("p (j d) -> p j d", j=JT)
        xh = sb("xh", [P, 2, JT, D])
        trans = sb("trans", [P, 2 * KD * L])
        xnT = trans[:, 0:1024].rearrange("p (k t) -> p k t", k=KD)
        h2T = trans[:, 1024:2048].rearrange("p (k t) -> p k t", k=KD)
        y_sb = sb("y_sb", [P, KC, L])
        rec = sb("rec", [P, JT, 2 * D])
        g_win = sb("g_win", [P, KD, (2 * CH - 1) * NS])
        ident = sb("ident", [P, P])
        l_state = sb("l_state", [P, NC])
        e_state = sb("e_state", [NS, NC])
        logits = sb("logits", [P, NT, E])
        wr_sb = sb("wr_sb", [P, KD, E])
        cols = sb("cols", [P, 2 * KD + (TAPS + 1) * KC])
        gb_col = cols[:, 0:4].rearrange("p (v k) -> p v k", v=2)
        cw = cols[:, 4:20].rearrange("p (j k) -> p j k", j=KC)
        cb = cols[:, 20:24]
        br_sb = sb("br_sb", [P, E])
        powers = sb("powers", [NS, 2, (CH + 1) * NS])
        dbl = sb("dbl", [NS, LEVELS, 2, NS])
        stat = sb("stat", [P, 2, JT, 6])
        stat_c = sb("stat_c", [P, JT, 6])
        mr = sb("mr", [P, 3, 2, JT])
        tmp = sb("tmp", [P, 4, JT])
        const4 = sb("const4", [P, 5, JT])
        half4, inv4, quart4, eps4, mhalf4 = (const4[:, i, :] for i in range(5))
        lt_tok = sb("lt_tok", [P, P], BF16)
        lt_et = sb("lt_et", [P, 2, 2 * P], BF16)
        ones_bf = sb("ones_bf", [P, P], BF16)
        iota = sb("iota", [P, P])
        tok1 = sb("tok1", [P, NT])
        rev = sb("rev", [P, E])
        k128 = sb("k128", [P, NT])
        lt_e = sb("lt_e", [P, E, E])
        conv = experts[:, E - 2, 0:KC * L].rearrange("p (k t) -> p k t", k=KC)
        zg = experts[:, E - 2, KC * L:2 * KC * L].rearrange("p (k t) -> p k t", k=KC)
        cm_z = experts[:, E - 1, :].rearrange("p (t n) -> p t n", t=CH)
        wmod_sb = experts[:, E - 2, 0:KD * NM * D].rearrange("p (k n) -> p k n", k=KD)
        wx_nat = experts[:, E - 2, KD * NM * D:4096].rearrange("p (k d) -> p k d", k=KC)
        mod_sb = xh[0:B, :, :, :].rearrange("p a j d -> p (a j d)")[:, 0:NM * D]
        sgn = y_sb[0:B, 0, :]
        silc = y_sb[:, 1, 0:2 * KD * B].rearrange("p (s k b) -> p s k b", s=2, k=KD)
        bmT = y_sb[:, 3, 0:KC * NS].rearrange("p (k s) -> p k s", k=KC)
        g0 = y_sb[0:NS, 2, 0:D]
        NB = E * (FF + D) // P
        bias_raw = rec[0:NB, 0, 0:P]
        bias_rest = rec[0:NB, 1, 0:2 * P].rearrange("p (s n) -> p s n", s=2)
        bias_3 = rec[0:NB, 2, :].bitcast(BF16)[:, 0:3 * P].rearrange("p (s n) -> p s n", s=3)
        onehot = xnT.rearrange("p k t -> p (k t)")[:, 0:128].bitcast(BF16)
        r_val = xnT.rearrange("p k t -> p (k t)")[:, 256:512].rearrange("p (t e) -> p t e", t=NT)
        r_low = xnT.rearrange("p k t -> p (k t)")[:, 512:768].rearrange("p (t e) -> p t e", t=NT)
        r_cntb = xnT.rearrange("p k t -> p (k t)")[:, 768:896].bitcast(BF16) \
            .rearrange("p (c m) -> p c m", c=2)
        r_sum = h2T.rearrange("p k t -> p (k t)")[:, 0:256].rearrange("p (e t) -> p e t", e=E)
        r_cmp = h2T.rearrange("p k t -> p (k t)")[:, 256:576]
        after_hot = mods[:, 3 * NT * SLOTS:]
        small = after_hot[:, 0:10 * NT].rearrange("p (v t) -> p v t", v=10)
        r_m1, r_mv, r_m2, r_dif, r_gate, r_slot, r_lo, r_hi = (small[:, i, :] for i in range(8))
        r_int = small[:, 8, :].bitcast(I32)
        r_int2 = small[:, 9, :].bitcast(I32)
        r_cnt2 = sb("r_cnt2", [P, 2])
        r_e = sb("r_e", [P, 6, E + 1])
        hot_lo = [y_sb[:, :, :].rearrange("p k t -> p (k t)").rearrange("p (t m) -> p t m", m=P),
                  xh[:, :, :, :].rearrange("p a j d -> p (a j d)").rearrange("p (t m) -> p t m", m=P)]
        hot_hi = mods[:, 0:NT * SLOTS].rearrange("p (t k) -> p t k", t=NT)
        hot_val = mods[:, NT * SLOTS:3 * NT * SLOTS].rearrange("p (t v k) -> p t v k", t=NT, v=2)
        inv = after_hot[:, 320:398].rearrange("p (v k) -> p v k", v=2)
        idx_f = after_hot[:, 398:476].rearrange("p (v k) -> p v k", v=2)
        idx_i = after_hot[:, 476:554].bitcast(I32).rearrange("p (v k) -> p v k", v=2)
        ek = sb("ek", [1, SLOTS], I32)
        ek_f = sb("ek_f", [1, SLOTS])
        idx_k = sb("idx_k", [P, Tile.TURN, 2], I32)
        bias = proj[0:3, :].bitcast(BF16)
        bias1 = bias[:, 0:E * FF].rearrange("p (e n) -> p e n", e=E)
        bias2 = bias[:, E * FF:E * (FF + D)].rearrange("p (e n) -> p e n", e=E)
        rows = mods[:, 0:Tile.TURN * 3 * D].rearrange("p (b n) -> p b n", b=Tile.TURN)
        hT = trans[:, 1536:1792].rearrange("p (k t) -> p k t", k=KD)
        hid = xh[:, :, :, :].rearrange("p a j d -> p a (j d)")
        hidT = y_sb[:, :, :].rearrange("p k t -> p (k t)")[:, 0:1024].rearrange("p (i t) -> p i t", i=KF)
        res = rec[:, 0:2, :].rearrange("p a (b d) -> p (a b) d", b=2)

        banks = [ctx.enter_context(nc.psum_tensor(f"bank{i}", [P, 512], F32)) for i in range(8)]
        ROT, ROTN = 2, 4
        OUT0 = 6
        rot = [banks[ROT + i][:, :] for i in range(ROTN)]
        state_ps = banks[1]

        ld_w, ld_small, ld_wmod = sem("ld_w"), sem("ld_small"), sem("ld_wmod")
        ld_x = [sem(f"ld_x{i}") for i in range(2)]
        ld_mp = [sem(f"ld_mp{i}") for i in range(2)]
        ld_cm = sem("ld_cm")
        ld_ex = [sem(f"ld_ex{i}") for i in range(E)]
        st_mod, st_bias, st_rec = sem("st_mod"), sem("st_bias"), sem("st_rec")
        ld_bias = sem("ld_bias")
        cst = sem("cst")
        cmz = sem("cmz")
        su_d, su_p, su_a = sem("su_d"), sem("su_p"), sem("su_a")
        stats_x, stats_h, stats_p = sem("stats_x"), sem("stats_h"), sem("stats_p")
        norm_x, norm_h, norm_p = sem("norm_x"), sem("norm_h"), sem("norm_p")
        h_done, xn_done, xh_done = sem("h_done"), sem("xn_done"), sem("xh_done")
        xn_trans, xnT_done = sem("xn_trans"), sem("xnT_done")
        loc_ps, loc_done = sem("loc_ps"), sem("loc_done")
        scan_ps, scan_done = sem("scan_ps"), sem("scan_done")
        xz_ps = sem("xz_ps")
        tap0_done, conv_done, zg_done, silu_done = (sem("tap0_done"), sem("conv_done"),
                                                    sem("zg_done"), sem("silu_done"))
        so_ps, t_done, y_done = sem("so_ps"), sem("t_done"), sem("y_done")
        op_ps, op_read, x1_done, h2_done = sem("op_ps"), sem("op_read"), sem("x1_done"), sem("h2_done")
        h2_trans, h2T_done, lg_ps, lg_done = (sem("h2_trans"), sem("h2T_done"), sem("lg_ps"),
                                              sem("lg_done"))
        held = sem("held")
        ro_d, ro_p, ro_a = sem("ro_d"), sem("ro_p"), sem("ro_a")
        idx_done = sem("idx_done")
        got = [sem(f"got{i}") for i in range(Tile.TURN)]
        put = [sem(f"put{i}") for i in range(Tile.TURN)]
        t1_ps, hT_done, f1_ps, hid_done = sem("t1_ps"), sem("hT_done"), sem("f1_ps"), sem("hid_done")
        t2_ps, hidT_a, hidT_d, f2_ps = sem("t2_ps"), sem("hidT_a"), sem("hidT_d"), sem("f2_ps")
        gated, res_done = sem("gated"), sem("res_done")

        def batches(eng, step):
            step(Batch(0, 0), first=True, last=False)
            with eng.Fori(0, B // 2 - 1) as r:
                step(Batch(r, 1), first=False, last=False)
                step(Batch(r + 1, 0), first=False, last=False)
            step(Batch(B // 2 - 1, 1), first=False, last=True)

        def tiles(eng, step):
            turns = (SLOTS - 1) // Tile.TURN
            with eng.Fori(0, turns) as r:
                for p in range(1, Tile.TURN + 1):
                    step(Tile(r, 0) + p)
            for k in range(turns * Tile.TURN + 1, SLOTS):
                step(Tile(0, 0) + k)

        FIRST_TILE, LAST_TILE = Tile(0, 0), Tile(0, 0) + (SLOTS - 1)

        def hold(eng, s, value):
            eng.wait_ge(s, value)
            eng.sem_inc(held, 1)

        AHEAD = 1

        def start_ahead(eng, *sems):
            for s in sems:
                eng.sem_inc(s, AHEAD)

        MOD_READY = 15
        BIAS_READY = 20
        POWERS_READY = 36
        N_CONST = 19
        NORM = 10
        HOT_READY, DIFF_READY, CNTB_READY, LO_READY, INDEX_READY = 5, 8, 11, 32, 40
        SCAN = LEVELS + 3

        block = ctx.enter_context(nc.Block())

        @block.sync
        def _(sp):
            x_v = x.rearrange("b (j p) d -> b p j d", p=P)
            start_ahead(sp, st_rec)

            def load_in(b):
                sp.dma_start(x_sb[:, b.place], x_v[b.n]).then_inc(ld_x[b.place], 16)

            def load_mod_in(b):
                sp.dma_start(mod_in[:, b.place].rearrange("p v d -> p (v d)"),
                             mod_dram[b.n, 0:2 * D].partition_broadcast(P)).then_inc(ld_x[b.place], 16)

            def load_mod_post(b):
                sp.dma_start(mod_post[:, b.place].rearrange("p v d -> p (v d)"),
                             mod_dram[b.n, 2 * D:GB].partition_broadcast(P)).then_inc(ld_mp[b.place], 16)

            def store_rows(b):
                sp.wait_ge(h2_done, 2 * JT * b.n + 2 * JT)
                sp.dma_start(table.rearrange("(b j p) n -> b p j n", p=P, j=JT)[b.n, :, :, 0:2 * D],
                             rec[:, :, :]).then_inc(st_rec, 16)

            sp.dma_start(wmod_sb, wmod.rearrange("(k p) n -> p k n", p=P)).then_inc(ld_wmod, 16)
            sp.dma_start(silc[:, 0], cT.rearrange("(k p) b -> p k b", p=P)).then_inc(ld_wmod, 16)
            sp.dma_start(wx_nat, W_in[0:DI, :].rearrange("(k p) d -> p k d", p=P)).then_inc(ld_small, 16)
            for dst, src in (
                (powers[:, 1, (CH - 1) * NS:CH * NS], A), (powers[:, 0, (CH - 1) * NS:CH * NS], AT),
                (bmT, BmT.rearrange("(k p) s -> p k s", p=P)),
                (bias_raw[0:E * FF // P], b1.rearrange("e (c n) -> (e c) n", n=P)),
                (bias_raw[E * FF // P:NB], b2.rearrange("e (c n) -> (e c) n", n=P)),
                (gb_col[:, 0], gamma),
                (gb_col[:, 1], beta),
                (cw, conv_w),
                (cb, conv_b),
                (wr_sb[:, :, :], wr.rearrange("(k p) e -> p k e", p=P)),
                (br_sb[:, :], br.partition_broadcast(P)),
            ):
                sp.dma_start(dst, src).then_inc(ld_small, 16)
            load_in(Batch(0, 0))
            sp.dma_start(w_in, W_inT.rearrange("(k p) n -> p k n", p=P)).then_inc(ld_w, 16)
            sp.dma_start(w_out, W_outT.rearrange("(k p) n -> p k n", p=P)).then_inc(ld_w, 16)
            load_in(Batch(0, 1))
            sp.wait_ge(cmz, 1)
            for t in range(CH):
                sp.dma_start(cm_z[NS * (CH - 1 - t):NS * (CH - t), t, :], Cm).then_inc(ld_cm, 16)
            sp.wait_ge(su_d, MOD_READY)
            sp.dma_start(mod_dram, mod_sb).then_inc(st_mod, 16)
            sp.dma_start(gb_dram, mod_sb[:, GB:]).then_inc(st_mod, 16)
            sp.wait_ge(st_mod, 32)
            for b in (Batch(0, 0), Batch(0, 1)):
                load_mod_in(b)
                load_mod_post(b)
            for b in range(B):
                sp.dma_start(table[b * L:(b + 1) * L, 2 * D:],
                             gb_dram[b].partition_broadcast(L)).then_inc(st_mod, 16)
            sp.wait_ge(su_d, BIAS_READY)
            sp.dma_start(bias_dram.rearrange("s (r n) -> r s n", n=P), bias_3).then_inc(st_bias, 16)

            def step(i, first, last):
                if first:
                    return
                if not last:
                    sp.wait_ge(xh_done, 2 * i.n)
                    load_in(i + 1)
                    load_mod_in(i + 1)
                store_rows(i + -1)
                if not last:
                    load_mod_post(i + 1)
            batches(sp, step)
            store_rows(Batch(B // 2 - 1, 1))
            sp.wait_ge(y_done, KC * B)
            sp.wait_ge(so_ps, KC * B)
            for e in (E - 2, E - 1):
                sp.dma_start(experts[:, e, 0:WE].rearrange("p (k n) -> p k n", k=KD),
                             w1[e].rearrange("(k p) n -> p k n", p=P)).then_inc(ld_ex[e], 16)
                sp.dma_start(experts[:, e, WE:].rearrange("p (k n) -> p k n", k=KF),
                             w2[e].rearrange("(k p) n -> p k n", p=P)).then_inc(ld_ex[e], 16)
            sp.wait_ge(op_ps, JT * B)
            sp.wait_ge(st_bias, 16)
            sp.dma_start(bias[:, 0:E * (FF + D)], bias_dram).then_inc(ld_bias, 16)

        @block.scalar
        def _(act):
            start_ahead(act, hid_done, hidT_a)
            for e in range(E - 2):
                act.dma_start(experts[:, e, 0:WE].rearrange("p (k n) -> p k n", k=KD),
                              w1[e].rearrange("(k p) n -> p k n", p=P)).then_inc(ld_ex[e], 16)
                act.dma_start(experts[:, e, WE:].rearrange("p (k n) -> p k n", k=KF),
                              w2[e].rearrange("(k p) n -> p k n", p=P)).then_inc(ld_ex[e], 16)
            act.wait_ge(ld_wmod, 32)
            act.activation(silc[:, 1], silc[:, 0], ACT.Sigmoid).then_inc(su_a, 1)
            act.wait_ge(ld_small, 16 * 12)

            def trans_out(b):
                for k in range(KD):
                    act.wait_ge(xn_trans, KD * b.n + k + 1)
                    act.activation(xnT[:, k, :], banks[k][:, :], ACT.Identity, bias=gb_col[:, 1, k:k + 1],
                                   scale=gb_col[:, 0, k:k + 1]).then_inc(xnT_done, 1)

            def h2_out(b):
                for k in range(KD):
                    act.wait_ge(h2_trans, AHEAD + KD * b.n + k + 1)
                    act.activation(h2T[:, k, :], banks[k][:, :], ACT.Copy).then_inc(h2T_done, 1)

            def step(i, first, last):
                trans_out(i)
                for j in range(KC):
                    if not first:
                        act.wait_ge(y_done, KC * (i + -1).n + j + 1)
                    act.wait_ge(xz_ps, 2 * KC * i.n + j + 1)
                    act.activation(zg[:, j, :], rot[j], ACT.Sigmoid).then_inc(zg_done, 1)
                for j in range(KC):
                    act.wait_ge(xz_ps, 2 * KC * i.n + KC + j + 1)
                    act.activation(conv[:, j, :], rot[j], ACT.Identity, bias=cb[:, j:j + 1],
                                   scale=cw[:, j, TAPS - 1:TAPS]).then_inc(tap0_done, 1)
                for j in range(KC):
                    act.wait_ge(conv_done, 3 * KC * i.n + 3 * j + 3)
                    act.activation(conv[:, j, :], conv[:, j, :], ACT.Silu).then_inc(silu_done, 1)
                if not first:
                    h2_out(i + -1)
            batches(act, step)
            h2_out(Batch(B // 2 - 1, 1))

            act.wait_ge(ro_d, DIFF_READY)
            act.activation(r_gate, r_dif, ACT.Sigmoid).then_inc(ro_a, 1)

            def gelu(k):
                for h in range(2):
                    if not k is FIRST_TILE:
                        act.wait_ge(t2_ps, AHEAD + 2 * (k + -1).n)
                    act.wait_ge(f1_ps, 2 * k.n + h + 1)
                    act.activation(hid[:, k.place % 2, 512 * h:512 * h + 512], banks[1 + 2 * (k.place % 2) + h][:, :],
                                   ACT.Gelu).then_inc(hid_done, 1)

            def hidT_low(k):
                act.wait_ge(t2_ps, AHEAD + 2 * k.n + 1)
                act.activation(hidT[:, 0:4, :].rearrange("p i t -> p (i t)"), banks[5][:, :],
                               ACT.Copy).then_inc(hidT_a, 1)

            gelu(FIRST_TILE)

            def tile(k):
                hidT_low(k + -1)
                gelu(k)
            tiles(act, tile)
            hidT_low(LAST_TILE)

        @block.gpsimd
        def _(pool):
            made = [0]

            def const(ins):
                made[0] += 1
                ins.then_inc(cst, 1)
                pool.wait_ge(cst, made[0])

            pool.memset(cm_z, 0.0).then_inc(cmz, 1)
            pool.memset(g_win[:, :, :], 0.0).then_inc(cmz, 1)
            for i, v in enumerate((0.5, 1.0 / D, 0.25, EPS, -0.5)):
                const(pool.memset(const4[:, i, :], v))
            const(pool.memset(ident[:, :], 0.0))
            const(pool.affine_select(out=ident[:, :], in_=ident[:, :], compare_op=ALU.not_equal, fill=1.0,
                                     base=0, pattern=[[-1, P]], channel_multiplier=1))
            const(pool.memset(ones_bf[:, :], 1.0))
            const(pool.memset(lt_tok[:, :], 1.0))
            const(pool.affine_select(out=lt_tok[:, :], in_=lt_tok[:, :], compare_op=ALU.is_gt, fill=0.0,
                                     base=0, pattern=[[1, P]], channel_multiplier=-1))
            const(pool.memset(lt_et[:, :, :], 1.0))
            const(pool.affine_select(out=lt_et[:, :, :], in_=lt_et[:, :, :], compare_op=ALU.is_gt, fill=0.0,
                                     base=0, pattern=[[-P, 2], [1, 2 * P]], channel_multiplier=-1))
            const(pool.memset(lt_e[:, :, :], 1.0))
            const(pool.affine_select(out=lt_e[:, :, :], in_=lt_e[:, :, :], compare_op=ALU.is_gt, fill=0.0,
                                     base=0, pattern=[[1, E], [-1, E]], channel_multiplier=0))
            for dst, pattern, base, mult in ((iota, [[1, P]], 0, 0), (tok1, [[P, NT]], 1, 1),
                                             (rev, [[-1, E]], E, 0), (k128, [[P, NT]], 0, 0)):
                const(pool.iota(dst[:, :], pattern=pattern, base=base, channel_multiplier=mult,
                                allow_small_or_imprecise_dtypes=True))
            const(pool.memset(r_e[:, 0, E:E + 1], float(T)))
            assert made[0] == N_CONST

            def norm(b, st, out, ready, sem):
                me, qe, mo, qo = (st[:, :, c] for c in (1, 2, 4, 5))
                s, d, q, v = (tmp[:, c, :] for c in range(4))
                steps = [0]

                def op(o, a, b_, f):
                    steps[0] += 1
                    pool.tensor_tensor(o, a, b_, f).then_inc(sem, 1)

                def so_far():
                    pool.wait_ge(sem, NORM * b.n + steps[0])

                pool.wait_ge(ready, JT * b.n + JT)
                op(s, me, mo, ALU.add)
                op(d, me, mo, ALU.subtract)
                op(q, qe, qo, ALU.add)
                so_far()
                op(out[:, 0, :], s, half4, ALU.mult)
                op(d, d, d, ALU.mult)
                op(q, q, inv4, ALU.mult)
                so_far()
                op(d, d, quart4, ALU.mult)
                op(q, q, eps4, ALU.add)
                so_far()
                op(v, d, q, ALU.add)
                so_far()
                op(out[:, 1, :], v, mhalf4, ALU.pow)
                so_far()
                assert steps[0] == NORM

            def norms_in(b):
                norm(b, stat[:, 0], mr[:, 0], stats_x, norm_x)
                norm(b, stat[:, 1], mr[:, 1], stats_h, norm_h)

            def residual(b, first):
                pool.wait_ge(ld_mp[b.place], 16 * (b.turn + 1))
                pool.wait_ge(h_done, 2 * JT * b.n + 2 * JT)
                if not first:
                    pool.wait_ge(x1_done, (b + -1).n)
                pool.tensor_tensor(xh[:, b.place], h_sb, bcast(mod_post[:, b.place, 0, :], 1, JT),
                                   ALU.mult).then_inc(xh_done, 1)
                pool.wait_ge(xh_done, 2 * b.n + 1)
                pool.tensor_tensor(xh[:, b.place], xh[:, b.place], x_sb[:, b.place],
                                   ALU.add).then_inc(xh_done, 1)

            norms_in(Batch(0, 0))
            residual(Batch(0, 0), True)

            def step(i, first, last):
                if not last:
                    norms_in(i + 1)
                if not first:
                    norm(i + -1, stat_c, mr[:, 2], stats_p, norm_p)
                pool.wait_ge(op_ps, JT * i.n)
                for j in range(KC):
                    pool.wait_ge(zg_done, KC * i.n + j + 1)
                    pool.wait_ge(t_done, KC * i.n + j + 1)
                    pool.tensor_tensor(y_sb[:, j, :], conv[:, j, :], zg[:, j, :],
                                       ALU.mult).then_inc(y_done, 1)
                if not last:
                    residual(i + 1, first)
            batches(pool, step)
            norm(Batch(B // 2 - 1, 1), stat_c, mr[:, 2], stats_p, norm_p)

            pool.wait_ge(st_rec, AHEAD + 16 * B)
            pool.wait_ge(st_mod, 16 * (2 + B))
            pool.wait_ge(ro_d, INDEX_READY)

            def gather(k):
                pool.tensor_copy(idx_k[:, k.place, :],
                                 idx_i[:, :, bass.ds(k.n, 1)].rearrange("p v o -> p (v o)")).then_inc(idx_done, 1)
                hold(pool, idx_done, k.n + 1)
                pool.indirect_dma_start(
                    out=rows[:, k.place, :], out_offset=None, in_=table,
                    in_offset=bass.IndirectOffsetOnAxis(ap=idx_k[:, k.place, 0:1], axis=0)).then_inc(got[k.place], 16)

            def scatter(k):
                hold(pool, res_done, AHEAD + k.n + 1)
                pool.indirect_dma_start(
                    out=out.rearrange("b l d -> (b l) d"),
                    out_offset=bass.IndirectOffsetOnAxis(ap=idx_k[:, k.place, 1:2], axis=0),
                    in_=res[:, k.place, :], in_offset=None,
                    bounds_check=T - 1, oob_is_err=False).then_inc(put[k.place], 16)

            def turn(k):
                scatter(k)
                hold(pool, put[k.place], 16 * (k.turn + 1))
                gather(k + Tile.TURN)

            for k in range(Tile.TURN):
                gather(Tile(0, k))
            whole = (SLOTS - Tile.TURN) // Tile.TURN
            with pool.Fori(0, whole) as r:
                for p in range(Tile.TURN):
                    turn(Tile(r, p))
            for k in range(whole * Tile.TURN, SLOTS - Tile.TURN):
                turn(Tile(0, 0) + k)
            for k in range(SLOTS - Tile.TURN, SLOTS):
                scatter(Tile(0, 0) + k)
            for p in range(Tile.TURN):
                pool.wait_ge(put[p], 16 * ((SLOTS - p + Tile.TURN - 1) // Tile.TURN))

        @block.vector
        def _(dve):
            chained = [0]

            def link(ins, s=su_d):
                chained[0] += 1
                ins.then_inc(s, 1)
                dve.wait_ge(s, chained[0])

            start_ahead(dve, lg_done, res_done, hidT_d, gated)
            dve.wait_ge(su_a, 1)
            link(dve.tensor_tensor(silc[:, 0], silc[:, 0], silc[:, 1], ALU.mult))
            dve.wait_ge(su_p, 1)
            row = [banks[v // 2][0:B, (v % 2) * D:(v % 2) * D + D] for v in range(NM)]
            dst = [mod_sb[:, v * D:(v + 1) * D] for v in range(NM)]
            for v in (0, 3):
                link(dve.tensor_copy(dst[v], row[v]))
            for v in (1, 4):
                link(dve.tensor_scalar(dst[v], row[v], 1.0, None, ALU.add))
            for v in (2, 5):
                link(dve.tensor_scalar(sgn[:, 0:D], row[v], 0.0, 2.0, ALU.is_ge, ALU.mult))
                link(dve.tensor_copy(dst[v], row[v]))
                link(dve.scalar_tensor_tensor(sgn[:, D:2 * D], dst[v], -1.0, dst[v], ALU.mult, ALU.max))
                link(dve.tensor_scalar(sgn[:, D:2 * D], sgn[:, D:2 * D], 0.25, None, ALU.max))
                link(dve.scalar_tensor_tensor(dst[v], sgn[:, 0:D], -1.0, sgn[:, D:2 * D], ALU.add, ALU.mult))
            assert chained[0] == MOD_READY
            dve.wait_ge(ld_small, 16 * 12)
            link(dve.tensor_copy(bias_3[:, 0], bias_raw))
            link(dve.tensor_tensor(bias_rest[:, 0], bias_raw, bias_3[:, 0], ALU.subtract))
            link(dve.tensor_copy(bias_3[:, 1], bias_rest[:, 0]))
            link(dve.tensor_tensor(bias_rest[:, 1], bias_rest[:, 0], bias_3[:, 1], ALU.subtract))
            link(dve.tensor_copy(bias_3[:, 2], bias_rest[:, 1]))
            assert chained[0] == BIAS_READY
            dve.wait_ge(cst, N_CONST)
            link(dve.tensor_copy(powers[:, 0, CH * NS:], ident[0:NS, 0:NS]))
            dve.wait_ge(su_p, 2)
            link(dve.tensor_copy(g0, banks[3][0:NS, 0:D]))
            two = banks[4][0:NS, 0:2 * NS].rearrange("p (v n) -> p v n", v=2)
            for k in range(2, CH + 1):
                dve.wait_ge(su_p, k + 1)
                link(dve.tensor_copy(powers[:, :, (CH - k) * NS:(CH - k + 1) * NS], two))
            link(dve.tensor_copy(dbl[:, 0], two))
            for lv in range(1, LEVELS):
                dve.wait_ge(su_p, CH + 1 + lv)
                link(dve.tensor_copy(dbl[:, lv], two))
            dve.wait_ge(cmz, 2)
            dve.wait_ge(su_p, CH + LEVELS + 1)
            link(dve.tensor_copy(g_win[:, :, 0:P], banks[5][:, 0:KD * P].rearrange("p (k n) -> p k n", k=KD)))
            assert chained[0] == POWERS_READY

            def stats_in(b):
                dve.wait_ge(ld_x[b.place], 32 * (b.turn + 1))
                for j in range(JT):
                    dve.bn_stats(stat[:, 0, j, :], x_sb[:, b.place, j, :]).then_inc(stats_x, 1)

            def modulate(b):
                dve.wait_ge(xh_done, 2 * b.n)
                dve.wait_ge(norm_x, NORM * (b.n + 1))
                for j in range(JT):
                    dve.scalar_tensor_tensor(h_sb[:, j, :], x_sb[:, b.place, j, :], mr[:, 0, 0, j:j + 1],
                                             mod_in[:, b.place, 1, :], ALU.subtract, ALU.mult).then_inc(h_done, 1)
                for j in range(JT):
                    dve.wait_ge(h_done, 2 * JT * b.n + j + 1)
                    dve.scalar_tensor_tensor(h_sb[:, j, :], h_sb[:, j, :], mr[:, 0, 1, j:j + 1],
                                             mod_in[:, b.place, 0, :], ALU.mult, ALU.add).then_inc(h_done, 1)
                for j in range(JT):
                    dve.wait_ge(h_done, 2 * JT * b.n + JT + j + 1)
                    dve.bn_stats(stat[:, 1, j, :], h_sb[:, j, :]).then_inc(stats_h, 1)

            def normalize(b):
                dve.wait_ge(xn_trans, KD * b.n)
                dve.wait_ge(norm_h, NORM * (b.n + 1))
                for j in range(JT):
                    dve.tensor_scalar(xn_sb[:, j, :], h_sb[:, j, :], mr[:, 1, 0, j:j + 1],
                                      mr[:, 1, 1, j:j + 1], ALU.subtract, ALU.mult).then_inc(xn_done, 1)

            def taps(i, j):
                dve.wait_ge(tap0_done, KC * i.n + j + 1)
                for d in range(1, TAPS):
                    if d > 1:
                        dve.wait_ge(conv_done, 3 * KC * i.n + 3 * j + d - 1)
                    dve.scalar_tensor_tensor(conv[:, j, d:], rot[j][:, 0:L - d],
                                             cw[:, j, TAPS - 1 - d:TAPS - d], conv[:, j, d:],
                                             ALU.mult, ALU.add).then_inc(conv_done, 1)

            def chunk_states(i):
                dve.wait_ge(so_ps, KC * i.n)
                dve.wait_ge(loc_ps, i.n + 1)
                dve.tensor_copy(l_state[:, :], state_ps[:, 0:NC]).then_inc(scan_done, 1)
                dve.tensor_copy(e_state[:, :], state_ps[0:NS, 0:NC]).then_inc(scan_done, 1)

            def double(i, lv):
                m = 1 << lv
                dve.wait_ge(scan_ps, (LEVELS + 1) * i.n + lv + 1)
                dve.tensor_tensor(e_state[:, m:], e_state[:, m:], state_ps[0:NS, NC:2 * NC - m],
                                  ALU.add).then_inc(scan_done, 1)

            def all_states(i):
                dve.wait_ge(scan_ps, (LEVELS + 1) * (i.n + 1))
                dve.tensor_tensor(l_state[:, 1:], l_state[:, 1:], state_ps[:, 2 * NC:3 * NC - 1],
                                  ALU.add).then_inc(scan_done, 1)

            def add_states(i, j):
                dve.wait_ge(silu_done, KC * i.n + j + 1)
                dve.wait_ge(so_ps, KC * i.n + j + 1)
                c = conv[:, j, :].rearrange("p (c t) -> p c t", t=CH)
                dve.tensor_tensor(c, c, rot[j].rearrange("p (t c) -> p c t", t=CH), ALU.add).then_inc(t_done, 1)

            def residual_out(b):
                dve.wait_ge(st_rec, AHEAD + 16 * b.n)
                dve.wait_ge(h2_trans, AHEAD + KD * b.n)
                for j in range(JT):
                    dve.wait_ge(op_ps, JT * b.n + j + 1)
                    dve.tensor_tensor(rec[:, j, D:], banks[OUT0 + j % 2][:, 0:D], mod_post[:, b.place, 0, :],
                                      ALU.mult).then_inc(op_read, 1)
                dve.wait_ge(xh_done, 2 * b.n + 2)
                dve.wait_ge(op_read, JT * b.n + JT)
                dve.tensor_tensor(rec[:, :, D:], rec[:, :, D:], xh[:, b.place], ALU.add).then_inc(x1_done, 1)
                dve.wait_ge(x1_done, b.n + 1)
                for j in range(JT):
                    dve.bn_stats(stat_c[:, j, :], rec[:, j, D:]).then_inc(stats_p, 1)

            def modulate_out(b):
                dve.wait_ge(norm_p, NORM * (b.n + 1))
                for j in range(JT):
                    dve.scalar_tensor_tensor(rec[:, j, 0:D], rec[:, j, D:], mr[:, 2, 0, j:j + 1],
                                             mod_post[:, b.place, 2, :], ALU.subtract, ALU.mult).then_inc(h2_done, 1)
                for j in range(JT):
                    dve.wait_ge(h2_done, 2 * JT * b.n + j + 1)
                    dve.scalar_tensor_tensor(rec[:, j, 0:D], rec[:, j, 0:D], mr[:, 2, 1, j:j + 1],
                                             mod_post[:, b.place, 1, :], ALU.mult, ALU.add).then_inc(h2_done, 1)

            def keep_logits(b):
                dve.wait_ge(lg_ps, b.n + 1)
                dve.tensor_tensor(logits[:, bass.ds(b.n * JT, JT), :],
                                  banks[OUT0][:, 0:JT * E].rearrange("p (j e) -> p j e", j=JT),
                                  bcast(br_sb[:, :], 1, JT), ALU.add).then_inc(lg_done, 1)

            stats_in(Batch(0, 0))
            modulate(Batch(0, 0))
            normalize(Batch(0, 0))
            dve.wait_ge(st_bias, 16)

            def step(i, first, last):
                chunk_states(i)
                if not last:
                    stats_in(i + 1)
                double(i, 0)
                if not last:
                    modulate(i + 1)
                double(i, 1)
                taps(i, 0)
                double(i, 2)
                taps(i, 1)
                double(i, 3)
                if not last:
                    normalize(i + 1)
                double(i, 4)
                taps(i, 2)
                double(i, 5)
                taps(i, 3)
                all_states(i)
                if not first:
                    residual_out(i + -1)
                add_states(i, 0)
                add_states(i, 1)
                if not first:
                    modulate_out(i + -1)
                add_states(i, 2)
                add_states(i, 3)
                if not first:
                    keep_logits(i + -1)
            batches(dve, step)
            residual_out(Batch(B // 2 - 1, 1))
            modulate_out(Batch(B // 2 - 1, 1))
            keep_logits(Batch(B // 2 - 1, 1))

            chained[0] = 0

            def route(ins):
                link(ins, ro_d)

            lg = logits[:, :, :]
            dve.wait_ge(lg_done, AHEAD + B)
            route(dve.tensor_reduce(r_m1, lg, AX.X, ALU.max))
            route(dve.tensor_tensor(r_val, lg, bcast(r_m1, 2, E), ALU.is_equal))
            route(dve.tensor_tensor(r_val, r_val, bcast(rev[:, :], 1, NT), ALU.mult))
            route(dve.tensor_reduce(r_mv, r_val, AX.X, ALU.max))
            hot_te = onehot.rearrange("p (e t) -> p t e", e=E)
            route(dve.tensor_tensor(hot_te, r_val, bcast(r_mv, 2, E), ALU.is_equal))
            assert chained[0] == HOT_READY
            route(dve.scalar_tensor_tensor(r_low, hot_te, -1e30, lg, ALU.mult, ALU.add))
            route(dve.tensor_reduce(r_m2, r_low, AX.X, ALU.max))
            route(dve.tensor_tensor(r_dif, r_m1, r_m2, ALU.subtract))
            assert chained[0] == DIFF_READY
            dve.wait_ge(ro_p, 1)
            route(dve.tensor_copy(r_cnt2[:, :], banks[2][:, 0:2]))
            for c in range(2):
                route(dve.tensor_scalar(r_cntb[:, c, :], ones_bf[:, :], r_cnt2[:, c:c + 1], None, ALU.mult))
            assert chained[0] == CNTB_READY
            dve.wait_ge(ro_p, 2)
            start, count, ntile, first_t, end_t, off = (r_e[:, v, 0:E] for v in range(6))
            route(dve.tensor_copy(start, banks[3][:, 0:2 * P].rearrange("p (e t) -> p e t", e=E)[:, :, 0]))
            route(dve.tensor_tensor(count, r_e[:, 0, 1:E + 1], start, ALU.subtract))
            cmp = r_cmp[:, 0:E * NT].rearrange("p (e t) -> p e t", e=E)
            route(dve.tensor_tensor(cmp, bcast(count, 2, NT), bcast(k128[:, :], 1, E), ALU.is_gt))
            route(dve.tensor_reduce(ntile, cmp, AX.X, ALU.add))
            cmp = r_cmp[:, 0:E * E].rearrange("p (e f) -> p e f", e=E)
            route(dve.tensor_tensor(cmp, lt_e[:, :, :], bcast(ntile, 1, E), ALU.mult))
            route(dve.tensor_reduce(first_t, cmp, AX.X, ALU.add))
            route(dve.tensor_tensor(end_t, first_t, ntile, ALU.add))
            route(dve.scalar_tensor_tensor(off, first_t, float(P), start, ALU.mult, ALU.subtract))
            dve.wait_ge(ro_p, 3)
            route(dve.tensor_tensor(r_sum, banks[4][:, 0:2 * P].rearrange("p (e t) -> p e t", e=E),
                                    bcast(off, 2, NT), ALU.add))
            route(dve.tensor_tensor(r_sum, r_sum, onehot.rearrange("p (e t) -> p e t", e=E), ALU.mult))
            route(dve.tensor_reduce(r_slot, r_sum.rearrange("p e t -> p t e"), AX.X, ALU.add))
            route(dve.tensor_copy(r_int, r_slot))
            route(dve.tensor_scalar(r_int2, r_int, P - 1, None, ALU.bitwise_and))
            route(dve.tensor_copy(r_lo, r_int2))
            route(dve.tensor_scalar(r_int2, r_int, P.bit_length() - 1, None, ALU.arith_shift_right))
            route(dve.tensor_copy(r_hi, r_int2))
            route(dve.tensor_tensor(hot_hi, bcast(iota[:, 0:SLOTS], 1, NT), bcast(r_hi, 2, SLOTS), ALU.is_equal))
            route(dve.tensor_tensor(hot_val[:, :, 0, :], hot_hi, bcast(tok1[:, :], 2, SLOTS), ALU.mult))
            dve.wait_ge(ro_a, 1)
            route(dve.tensor_tensor(hot_val[:, :, 1, :], hot_hi, bcast(r_gate, 2, SLOTS), ALU.mult))
            half = NT // 2
            for c in range(2):
                route(dve.tensor_tensor(hot_lo[c], bcast(iota[:, :], 1, half),
                                        bcast(r_lo[:, c * half:(c + 1) * half], 2, P), ALU.is_equal))
            assert chained[0] == LO_READY
            cmp = r_cmp[0:1, 0:SLOTS * E].rearrange("p (k e) -> p k e", k=SLOTS)
            route(dve.tensor_tensor(cmp, bcast(iota[0:1, 0:SLOTS], 2, E), bcast(end_t[0:1, :], 1, SLOTS), ALU.is_ge))
            route(dve.tensor_reduce(ek_f[:, :], cmp, AX.X, ALU.add))
            route(dve.tensor_scalar(ek[:, :], ek_f[:, :], float(E - 1), None, ALU.min))
            dve.wait_ge(ro_p, 4)
            route(dve.tensor_copy(inv[:, :, :], banks[5][:, 0:2 * SLOTS].rearrange("p (v k) -> p v k", v=2)))
            route(dve.tensor_scalar(idx_f[:, 0, :], inv[:, 0, :], -1.0, 0.0, ALU.add, ALU.max))
            route(dve.tensor_copy(idx_i[:, 0, :], idx_f[:, 0, :]))
            route(dve.tensor_scalar(idx_f[:, 1, :], inv[:, 0, :], 0.0, float(FAR), ALU.is_equal, ALU.mult))
            route(dve.scalar_tensor_tensor(idx_i[:, 1, :], idx_f[:, 1, :], -1.0, inv[:, 0, :], ALU.add, ALU.add))
            assert chained[0] == INDEX_READY

            def hT_out(k):
                dve.wait_ge(t1_ps, k.n + 1)
                dve.tensor_copy(hT[:, :, :].rearrange("p k t -> p (k t)"), banks[0][:, 0:D]).then_inc(hT_done, 1)

            def hidT_high(k):
                dve.wait_ge(t2_ps, AHEAD + 2 * k.n + 2)
                dve.tensor_copy(hidT[:, 4:8, :].rearrange("p i t -> p (i t)"), banks[6][:, :]).then_inc(hidT_d, 1)

            def finish(k):
                dve.wait_ge(f2_ps, k.n + 1)
                dve.scalar_tensor_tensor(res[:, k.place, :], banks[7][:, 0:D], inv[:, 1, bass.ds(k.n, 1)],
                                         rows[:, k.place, 2 * D:], ALU.mult, ALU.mult).then_inc(gated, 1)
                dve.wait_ge(gated, AHEAD + k.n + 1)
                dve.tensor_tensor(res[:, k.place, :], res[:, k.place, :], rows[:, k.place, D:2 * D],
                                  ALU.add).then_inc(res_done, 1)

            hT_out(FIRST_TILE)

            def tile(k):
                hT_out(k)
                hidT_high(k + -1)
                finish(k + -1)
            tiles(dve, tile)
            hidT_high(LAST_TILE)
            finish(LAST_TILE)

        @block.tensor
        def _(pe):
            start_ahead(pe, h2_trans, t2_ps)
            pe.wait_ge(su_d, 1)
            for v in range(NM // 2):
                for k in range(KD):
                    mm = pe.matmul(banks[v][0:B, :], silc[:, 0, k, :], wmod_sb[:, k, v * 512:(v + 1) * 512],
                                   start=(k == 0), stop=(k == KD - 1))
            mm.then_inc(su_p, 1)
            pe.wait_ge(ld_small, 16 * 12)
            for k in range(KC):
                mm = pe.matmul(banks[3][0:NS, 0:D], bmT[:, k, :], wx_nat[:, k, :], start=(k == 0), stop=(k == KC - 1))
            mm.then_inc(su_p, 1)
            at_pow = [powers[:, 0, j * NS:(j + 1) * NS] for j in range(CH + 1)]
            a_pow = [powers[:, 1, j * NS:(j + 1) * NS] for j in range(CH)]
            for k in range(2, CH + 1):
                pe.wait_ge(su_d, BIAS_READY + k)
                pe.matmul(banks[4][0:NS, 0:NS], a_pow[CH - 1], at_pow[CH - k + 1], start=True, stop=True)
                pe.matmul(banks[4][0:NS, NS:2 * NS], at_pow[CH - 1], a_pow[CH - k + 1],
                          start=True, stop=True).then_inc(su_p, 1)
            for lv in range(1, LEVELS):
                pe.wait_ge(su_d, BIAS_READY + CH + 1 + lv)
                pe.matmul(banks[4][0:NS, 0:NS], dbl[:, lv - 1, 1], dbl[:, lv - 1, 0], start=True, stop=True)
                pe.matmul(banks[4][0:NS, NS:2 * NS], dbl[:, lv - 1, 0], dbl[:, lv - 1, 1],
                          start=True, stop=True).then_inc(su_p, 1)
            for k in range(KD):
                mm = pe.matmul(banks[5][:, k * P:(k + 1) * P], g0[:, k * P:(k + 1) * P], powers[:, 0, NS:],
                               start=True, stop=True)
            mm.then_inc(su_p, 1)
            pe.wait_ge(su_d, POWERS_READY)
            pe.wait_ge(ld_w, 32)
            pe.wait_ge(ld_cm, 16 * CH)
            pe.wait_ge(cst, N_CONST)

            def xn_transpose(b):
                for k in range(KD):
                    for j in range(JT):
                        if k == 0:
                            pe.wait_ge(xn_done, JT * b.n + j + 1)
                        tr = pe.transpose(banks[k][:, j * P:(j + 1) * P], xn_sb[:, j, k * P:(k + 1) * P], ident[:, :])
                    tr.then_inc(xn_trans, 1)

            def local_states(b):
                pe.wait_ge(xnT_done, KD * (b.n + 1))
                for s in range(CH):
                    for k in range(KD):
                        mm = pe.matmul(state_ps[:, 0:NC], g_win[:, k, s * NS:s * NS + P], xnT[:, k, s::CH],
                                       start=(s == 0 and k == 0), stop=(s == CH - 1 and k == KD - 1))
                mm.then_inc(loc_ps, 1)

            def project(b, j, is_x):
                c = j * P + (0 if is_x else DI)
                for k in range(KD):
                    mm = pe.matmul(rot[j], w_in[:, k, c:c + P], xnT[:, k, :], start=(k == 0), stop=(k == KD - 1))
                mm.then_inc(xz_ps, 1)

            def double(i, lv):
                m = 1 << lv
                hold(pe, scan_done, SCAN * i.n + 2 + lv)
                pe.matmul(state_ps[0:NS, NC:2 * NC - m], dbl[:, lv, 0], e_state[:, 0:NC - m],
                          start=True, stop=True).then_inc(scan_ps, 1)

            def carry_states(i):
                pe.wait_ge(scan_done, SCAN * i.n + 2 + LEVELS)
                pe.matmul(state_ps[:, 2 * NC:3 * NC - 1], powers[:, 0, 0:CH * NS], e_state[:, 0:NC - 1],
                          start=True, stop=True).then_inc(scan_ps, 1)

            def state_out(i, j):
                if j == 0:
                    pe.wait_ge(scan_done, SCAN * (i.n + 1))
                pe.wait_ge(conv_done, 3 * KC * i.n + 3 * j + 3)
                for t in range(CH):
                    mm = pe.matmul(rot[j][:, t * NC:(t + 1) * NC], cm_z[:, t, j * P:(j + 1) * P], l_state[:, :],
                                   start=True, stop=True)
                mm.then_inc(so_ps, 1)

            def project_out(b, j):
                if j == 0:
                    pe.wait_ge(y_done, KC * (b.n + 1))
                    pe.wait_ge(lg_done, AHEAD + b.n)
                if j >= 2:
                    pe.wait_ge(op_read, JT * b.n + j - 1)
                for k in range(KC):
                    mm = pe.matmul(banks[OUT0 + j % 2][:, 0:D], y_sb[:, k, j * P:(j + 1) * P], w_out[:, k, :],
                                   start=(k == 0), stop=(k == KC - 1))
                mm.then_inc(op_ps, 1)

            def router(b):
                pe.wait_ge(h2_done, 2 * JT * (b.n + 1))
                for k in range(KD):
                    for j in range(JT):
                        tr = pe.transpose(banks[k][:, j * P:(j + 1) * P], rec[:, j, k * P:(k + 1) * P], ident[:, :])
                    tr.then_inc(h2_trans, 1)
                pe.wait_ge(h2T_done, KD * (b.n + 1))
                for j in range(JT):
                    for k in range(KD):
                        mm = pe.matmul(banks[OUT0][:, j * E:(j + 1) * E], h2T[:, k, j * P:(j + 1) * P], wr_sb[:, k, :],
                                       start=(k == 0), stop=(k == KD - 1))
                mm.then_inc(lg_ps, 1)

            def step(i, first, last):
                xn_transpose(i)
                local_states(i)
                for j in range(KC):
                    if not first:
                        pe.wait_ge(t_done, KC * (i + -1).n + j + 1)
                    project(i, j, False)
                    if j == 1:
                        double(i, 0)
                double(i, 1)
                for j in range(KC):
                    pe.wait_ge(zg_done, KC * i.n + j + 1)
                    project(i, j, True)
                    if j >= 1:
                        double(i, j + 1)
                for j in range(JT):
                    if not first:
                        project_out(i + -1, j)
                    if j == 1:
                        double(i, 5)
                        carry_states(i)
                for j in range(KC):
                    state_out(i, j)
                if not first:
                    router(i + -1)
            batches(pe, step)
            for j in range(JT):
                project_out(Batch(B // 2 - 1, 1), j)
            router(Batch(B // 2 - 1, 1))

            pe.wait_ge(ro_d, HOT_READY)
            for c in range(2):
                mm = pe.matmul(banks[2][:, c:c + 1], onehot[:, c * P:(c + 1) * P], ones_bf[:, 0:1], start=True, stop=True)
            mm.then_inc(ro_p, 1)
            pe.wait_ge(ro_d, CNTB_READY)
            for c in range(2):
                mm = pe.matmul(banks[3][:, 0:2 * P], r_cntb[:, c, :], lt_et[:, c, :], start=(c == 0), stop=(c == 1))
            mm.then_inc(ro_p, 1)
            pe.matmul(banks[4][:, 0:2 * P], lt_tok[:, :], onehot, start=True, stop=False)
            for c in range(2):
                mm = pe.matmul(banks[4][:, 0:2 * P], r_cntb[:, c, :], lt_et[:, c, :], start=False, stop=(c == 1))
            mm.then_inc(ro_p, 1)
            for t in range(NT):
                if t % (NT // 2) == 0:
                    pe.wait_ge(ro_d, LO_READY - 1 + t // (NT // 2))
                mm = pe.matmul(banks[5][:, 0:2 * SLOTS], hot_lo[t // (NT // 2)][:, t % (NT // 2), :],
                               hot_val[:, t, :, :].rearrange("p v k -> p (v k)"), start=(t == 0), stop=(t == NT - 1))
            mm.then_inc(ro_p, 1)

            for e in range(E):
                pe.wait_ge(ld_ex[e], 32)
            pe.wait_ge(ld_bias, 16)
            pe.wait_ge(ro_d, INDEX_READY)

            def expert(k):
                return pe.value_load(ek[0:1, bass.ds(k.n, 1)], min_val=0, max_val=E - 1)

            def turn_in(k):
                if k is not FIRST_TILE:
                    pe.wait_ge(hT_done, k.n)
                pe.wait_ge(got[k.place], 16 * (k.turn + 1))
                for c in range(KD):
                    tr = pe.transpose(banks[0][:, c * P:(c + 1) * P], rows[:, k.place, c * P:(c + 1) * P], ident[:, :])
                tr.then_inc(t1_ps, 1)

            def up(k):
                e = expert(k)
                if k is not FIRST_TILE:
                    pe.wait_ge(hid_done, AHEAD + 2 * (k + -1).n)
                pe.wait_ge(hT_done, k.n + 1)
                w = experts[:, bass.ds(e, 1), :].rearrange("p o n -> p (o n)")
                bw = bias1[:, bass.ds(e, 1), :].rearrange("p o n -> p (o n)")
                for h in range(2):
                    bank = banks[1 + 2 * (k.place % 2) + h][:, :]
                    for c in range(KD):
                        pe.matmul(bank, hT[:, c, :], w[:, c * FF + 512 * h:c * FF + 512 * h + 512],
                                  start=(c == 0), stop=False)
                    pe.matmul(bank, ones_bf[0:3, :], bw[:, 512 * h:512 * h + 512],
                              start=False, stop=True).then_inc(f1_ps, 1)

            def turn_hidden(k):
                hold(pe, hid_done, AHEAD + 2 * (k.n + 1))
                for i in range(KF):
                    if i % 4 == 0:
                        pe.wait_ge(hidT_a if i == 0 else hidT_d, AHEAD + k.n)
                    tr = pe.transpose(banks[5 + i // 4][:, (i % 4) * P:(i % 4 + 1) * P],
                                      hid[:, k.place % 2, i * P:(i + 1) * P], ident[:, :])
                    if i % 4 == 3:
                        tr.then_inc(t2_ps, 1)

            def down(k):
                e = expert(k)
                hold(pe, gated, AHEAD + k.n)
                hold(pe, hidT_d, AHEAD + k.n + 1)
                pe.wait_ge(hidT_a, AHEAD + k.n + 1)
                w = experts[:, bass.ds(e, 1), :].rearrange("p o n -> p (o n)")
                bw = bias2[:, bass.ds(e, 1), :].rearrange("p o n -> p (o n)")
                for i in range(KF):
                    pe.matmul(banks[7][:, 0:D], hidT[:, i, :], w[:, WE + i * D:WE + (i + 1) * D],
                              start=(i == 0), stop=False)
                pe.matmul(banks[7][:, 0:D], ones_bf[0:3, :], bw, start=False, stop=True).then_inc(f2_ps, 1)

            turn_in(FIRST_TILE)
            up(FIRST_TILE)

            def tile(k):
                turn_in(k)
                turn_hidden(k + -1)
                up(k)
                down(k + -1)
            tiles(pe, tile)
            turn_hidden(LAST_TILE)
            down(LAST_TILE)


_INS = ['x', 'ln_gamma', 'ln_beta', 'W_in', 'W_inT', 'conv_w', 'conv_b', 'W_outT', 'A', 'AT', 'BmT', 'Cm',
        'w1', 'b1', 'w2', 'b2', 'wr', 'br', 'cT', 'wmod']
_OUTS = [((8, 512, 256), 'float32')]


def kernel(**inputs):
    import numpy as _np
    import concourse.bacc as _bacc
    from concourse import mybir as _mybir
    from concourse.bass_utils import run_bass_kernel_spmd as _run

    given = {n.replace('L0_attn_', '').replace('L0_ffn_', '').replace('L0_', ''): _np.asarray(a)
             for n, a in inputs.items()}
    for name, of in (('W_inT', 'W_in'), ('W_outT', 'W_out'), ('AT', 'A'), ('BmT', 'Bm'), ('cT', 'c')):
        given[name] = given[of].T
    for name in ('ln_gamma', 'ln_beta', 'conv_b', 'conv_w'):
        a = given[name]
        given[name] = a.reshape((a.shape[0] // P, P) + a.shape[2:]).swapaxes(0, 1)
    nc = _bacc.Bacc("TRN2", target_bir_lowering=False, num_devices=1)
    arrays, args = {}, []
    for name in _INS:
        a = _np.ascontiguousarray(given[name])
        arrays[f"in_{name}_dram"] = a
        args.append(nc.dram_tensor(f"in_{name}_dram", a.shape, _mybir.dt.from_np(a.dtype), kind="ExternalInput").ap())
    for i, (shape, dtype) in enumerate(_OUTS):
        dt = _mybir.dt.from_np(_np.dtype(dtype))
        args.append(nc.dram_tensor(f"out_{i}_dram", shape, dt, kind="ExternalOutput").ap())
    adaln_mamba_moe(nc, *args)
    r = _run(nc, [arrays], core_ids=[0])
    return r.results[0]["out_0_dram"]
```

```python
from contextlib import ExitStack

import concourse.bass as bass
from concourse import mybir

F32 = mybir.dt.float32
BF16 = mybir.dt.bfloat16
I32 = mybir.dt.int32
ALU = mybir.AluOpType
ACT = mybir.ActivationFunctionType
AX = mybir.AxisListType

P = 128
EPS = 1e-5


class Step:
    TURN = 1

    def __init__(self, turns, plus):
        self.turns, self.plus = turns, plus
        self.place = plus % self.TURN
        self.turn = turns + plus // self.TURN if plus >= self.TURN else turns
        self.n = turns * self.TURN + plus

    def __add__(self, k):
        return type(self)(self.turns, self.plus + k)


class Batch(Step):
    TURN = 2


class Tile(Step):
    TURN = 4


def bcast(ap, axis, n):
    ap = ap.unsqueeze(axis)
    shape = list(ap.shape)
    shape[axis] = n
    return ap.to_broadcast(shape)


def adaln_mamba_moe(nc, x, gamma, beta, W_in, W_inT, conv_w, conv_b, W_outT, A, AT, BmT, Cm,
                    w1, b1, w2, b2, wr, br, cT, wmod, out):
    B, L, D = x.shape
    T = B * L
    DI = W_outT.shape[0]
    NS = A.shape[0]
    E, _, FF = w1.shape
    KD = D // P
    KC = DI // P
    KF = FF // P
    JT = L // P
    NT = T // P
    CH = P // NS
    NC = L // CH
    LEVELS = NC.bit_length() - 1
    TAPS = conv_w.shape[2]
    SLOTS = (T - E) // P + E
    NM = wmod.shape[1] // D
    GB = (NM - 1) * D
    WE = KD * FF
    FAR = 2 * T

    table = nc.dram_tensor("token_rows", [T, 3 * D], F32).ap()
    mod_dram = nc.dram_tensor("mod_rows", [B, NM * D], F32).ap()
    gb_dram = nc.dram_tensor("gb_rows", [B, D], F32).ap()
    bias_dram = nc.dram_tensor("bias_parts", [3, E * (FF + D)], BF16).ap()

    ctx = ExitStack()
    with ctx:
        def sb(name, shape, dt=F32):
            return ctx.enter_context(nc.sbuf_tensor(name, shape, dt))

        def sem(name):
            return ctx.enter_context(nc.semaphore(name))

        experts = sb("experts", [P, E, WE + KF * D])
        proj = sb("proj", [P, KD * 2 * DI + KC * D + 2 * JT * D])
        w_in = proj[:, 0:KD * 2 * DI].rearrange("p (k n) -> p k n", k=KD)
        w_out = proj[:, 2048:3072].rearrange("p (k n) -> p k n", k=KC)
        x_sb = proj[:, 3072:5120].rearrange("p (b j d) -> p b j d", b=2, j=JT)
        mods = sb("mods", [P, 2 * 3 * D + 2 * 2 * D + 2 * JT * D])
        mod_in = mods[:, 0:1536].rearrange("p (b v d) -> p b v d", b=2, v=3)
        mod_post = mods[:, 1536:2560].rearrange("p (b v d) -> p b v d", b=2, v=2)
        h_sb = mods[:, 2560:3584].rearrange("p (j d) -> p j d", j=JT)
        xn_sb = mods[:, 3584:4608].rearrange("p (j d) -> p j d", j=JT)
        xh = sb("xh", [P, 2, JT, D])
        trans = sb("trans", [P, 2 * KD * L])
        xnT = trans[:, 0:1024].rearrange("p (k t) -> p k t", k=KD)
        h2T = trans[:, 1024:2048].rearrange("p (k t) -> p k t", k=KD)
        y_sb = sb("y_sb", [P, KC, L])
        rec = sb("rec", [P, JT, 2 * D])
        g_in = sb("g_in", [P, KD, NS])
        own_row = sb("own_row", [P, CH])
        ident = sb("ident", [P, P])
        l_state = sb("l_state", [P, NC])
        e_state = sb("e_state", [NS, NC])
        logits = sb("logits", [P, NT, E])
        wr_sb = sb("wr_sb", [P, KD, E])
        cols = sb("cols", [P, 2 * KD + (TAPS + 1) * KC])
        gb_col = cols[:, 0:4].rearrange("p (v k) -> p v k", v=2)
        cw = cols[:, 4:20].rearrange("p (j k) -> p j k", j=KC)
        cb = cols[:, 20:24]
        br_sb = sb("br_sb", [P, E])
        powers = sb("powers", [NS, 2, 2 * CH * NS])
        dbl = sb("dbl", [NS, LEVELS, 2, NS])
        stat = sb("stat", [P, 2, JT, 6])
        stat_c = sb("stat_c", [P, JT, 6])
        mr = sb("mr", [P, 3, 2, JT])
        shift_h = sb("shift_h", [P, 2, JT])
        tmp = sb("tmp", [P, 4, JT])
        const4 = sb("const4", [P, 6, JT])
        half4, inv4, quart4, eps4, mhalf4, zero4 = (const4[:, i, :] for i in range(6))
        lt_tok = sb("lt_tok", [P, P], BF16)
        lt_et = sb("lt_et", [P, 2, 2 * P], BF16)
        ones_bf = sb("ones_bf", [P, P], BF16)
        iota = sb("iota", [P, P])
        tok1 = sb("tok1", [P, NT])
        rev = sb("rev", [P, E])
        k128 = sb("k128", [P, NT])
        lt_e = sb("lt_e", [P, E, E])
        conv = experts[:, E - 2, 0:KC * L].rearrange("p (k t) -> p k t", k=KC)
        zg = experts[:, E - 2, KC * L:2 * KC * L].rearrange("p (k t) -> p k t", k=KC)
        cm_t = experts[:, E - 1, 0:DI]
        w_ga = experts[:, E - 1, DI + 2 * L:DI + 2 * L + KC * D].rearrange("p (k n) -> p k n", k=KC)
        v_sb = experts[0:NS, E - 1, DI:DI + L]
        spread = experts[:, E - 1, DI + L:DI + 2 * L]
        wmod_sb = experts[:, E - 2, 0:KD * NM * D].rearrange("p (k n) -> p k n", k=KD)
        wx_nat = experts[:, E - 2, KD * NM * D:4096].rearrange("p (k d) -> p k d", k=KC)
        mod_sb = xh[0:B, :, :, :].rearrange("p a j d -> p (a j d)")[:, 0:NM * D]
        sgn = y_sb[0:B, 0, :]
        silc = y_sb[:, 1, 0:2 * KD * B].rearrange("p (s k b) -> p s k b", s=2, k=KD)
        bmT = y_sb[:, 3, 0:KC * NS].rearrange("p (k s) -> p k s", k=KC)
        NB = E * (FF + D) // P
        bias_raw = rec[0:NB, 0, 0:P]
        bias_rest = rec[0:NB, 1, 0:2 * P].rearrange("p (s n) -> p s n", s=2)
        bias_3 = rec[0:NB, 2, :].bitcast(BF16)[:, 0:3 * P].rearrange("p (s n) -> p s n", s=3)
        onehot = xnT.rearrange("p k t -> p (k t)")[:, 0:128].bitcast(BF16)
        r_val = xnT.rearrange("p k t -> p (k t)")[:, 256:512].rearrange("p (t e) -> p t e", t=NT)
        r_low = xnT.rearrange("p k t -> p (k t)")[:, 512:768].rearrange("p (t e) -> p t e", t=NT)
        r_cntb = xnT.rearrange("p k t -> p (k t)")[:, 768:896].bitcast(BF16) \
            .rearrange("p (c m) -> p c m", c=2)
        r_sum = h2T.rearrange("p k t -> p (k t)")[:, 0:256].rearrange("p (e t) -> p e t", e=E)
        r_cmp = h2T.rearrange("p k t -> p (k t)")[:, 256:576]
        after_hot = mods[:, 3 * NT * SLOTS:]
        small = after_hot[:, 0:10 * NT].rearrange("p (v t) -> p v t", v=10)
        r_m1, r_mv, r_m2, r_dif, r_gate, r_slot, r_lo, r_hi = (small[:, i, :] for i in range(8))
        r_int = small[:, 8, :].bitcast(I32)
        r_int2 = small[:, 9, :].bitcast(I32)
        r_cnt2 = sb("r_cnt2", [P, 2])
        r_e = sb("r_e", [P, 6, E + 1])
        hot_lo = [y_sb[:, :, :].rearrange("p k t -> p (k t)").rearrange("p (t m) -> p t m", m=P),
                  xh[:, :, :, :].rearrange("p a j d -> p (a j d)").rearrange("p (t m) -> p t m", m=P)]
        hot_hi = mods[:, 0:NT * SLOTS].rearrange("p (t k) -> p t k", t=NT)
        hot_val = mods[:, NT * SLOTS:3 * NT * SLOTS].rearrange("p (t v k) -> p t v k", t=NT, v=2)
        inv = after_hot[:, 320:398].rearrange("p (v k) -> p v k", v=2)
        idx_f = after_hot[:, 398:476].rearrange("p (v k) -> p v k", v=2)
        idx_i = after_hot[:, 476:554].bitcast(I32).rearrange("p (v k) -> p v k", v=2)
        ek = sb("ek", [1, SLOTS], I32)
        ek_f = sb("ek_f", [1, SLOTS])
        idx_k = sb("idx_k", [P, Tile.TURN, 2], I32)
        bias = proj[0:3, :].bitcast(BF16)
        bias1 = bias[:, 0:E * FF].rearrange("p (e n) -> p e n", e=E)
        bias2 = bias[:, E * FF:E * (FF + D)].rearrange("p (e n) -> p e n", e=E)
        rows = mods[:, 0:Tile.TURN * 3 * D].rearrange("p (b n) -> p b n", b=Tile.TURN)
        hT = trans[:, 1536:2048].rearrange("p (b k t) -> p b k t", b=2, k=KD)
        hid = xh[:, :, :, :].rearrange("p a j d -> p a (j d)")
        hidT = y_sb[:, :, :].rearrange("p k t -> p (k t)")[:, 0:1024].rearrange("p (i t) -> p i t", i=KF)
        res = rec[:, 0:2, :].rearrange("p a (b d) -> p (a b) d", b=2)

        banks = [ctx.enter_context(nc.psum_tensor(f"bank{i}", [P, 512], F32)) for i in range(8)]
        ROT, ROTN = 2, 4
        OUT0 = 6
        TR = (0, 7)
        rot = [banks[ROT + i][:, :] for i in range(ROTN)]
        state_ps = banks[1]

        ld_w, ld_small, ld_wmod = sem("ld_w"), sem("ld_small"), sem("ld_wmod")
        ld_x = [sem(f"ld_x{i}") for i in range(2)]
        ld_mp = [sem(f"ld_mp{i}") for i in range(2)]
        ld_cm = sem("ld_cm")
        ld_ex = [sem(f"ld_ex{i}") for i in range(E)]
        st_mod, st_bias, st_rec = sem("st_mod"), sem("st_bias"), sem("st_rec")
        ld_bias = sem("ld_bias")
        cst = sem("cst")
        su_d, su_p, su_a = sem("su_d"), sem("su_p"), sem("su_a")
        stats_x, stats_h, stats_p = sem("stats_x"), sem("stats_h"), sem("stats_p")
        norm_x, norm_h, norm_p = sem("norm_x"), sem("norm_h"), sem("norm_p")
        h_done, xn_done, xh_done = sem("h_done"), sem("xn_done"), sem("xh_done")
        xn_trans, xnT_done = sem("xn_trans"), sem("xnT_done")
        v_ps, v_done, loc_ps = sem("v_ps"), sem("v_done"), sem("loc_ps")
        scan_ps, scan_done = sem("scan_ps"), sem("scan_done")
        xz_ps = sem("xz_ps")
        tap0_done, conv_done, zg_done, silu_done = (sem("tap0_done"), sem("conv_done"),
                                                    sem("zg_done"), sem("silu_done"))
        so_ps, t_done, y_done = sem("so_ps"), sem("t_done"), sem("y_done")
        w_ga_done, op_ps, x1_done, h2_done = sem("w_ga_done"), sem("op_ps"), sem("x1_done"), sem("h2_done")
        h2_trans, h2T_done, lg_ps, lg_done = (sem("h2_trans"), sem("h2T_done"), sem("lg_ps"),
                                              sem("lg_done"))
        held = sem("held")
        ro_d, ro_p, ro_a = sem("ro_d"), sem("ro_p"), sem("ro_a")
        idx_done = sem("idx_done")
        got = [sem(f"got{i}") for i in range(Tile.TURN)]
        put = [sem(f"put{i}") for i in range(Tile.TURN)]
        t1_ps, hT_done, f1_ps, hid_done = sem("t1_ps"), sem("hT_done"), sem("f1_ps"), sem("hid_done")
        t2_ps, hidT_a, hidT_d, f2_ps = sem("t2_ps"), sem("hidT_a"), sem("hidT_d"), sem("f2_ps")
        gated, res_done = sem("gated"), sem("res_done")

        def batches(eng, step):
            step(Batch(0, 0), first=True, last=False)
            with eng.Fori(0, B // 2 - 1) as r:
                step(Batch(r, 1), first=False, last=False)
                step(Batch(r, 2), first=False, last=False)
            step(Batch(B // 2 - 1, 1), first=False, last=True)

        def tiles(eng, step):
            turns = (SLOTS - 1) // Tile.TURN
            with eng.Fori(0, turns) as r:
                for p in range(1, Tile.TURN + 1):
                    step(Tile(r, 0) + p)
            for k in range(turns * Tile.TURN + 1, SLOTS):
                step(Tile(0, 0) + k)

        def is_last(k):
            return isinstance(k.n, int) and k.n == SLOTS - 1

        FIRST_TILE, LAST_TILE = Tile(0, 0), Tile(0, 0) + (SLOTS - 1)

        def hold(eng, s, value):
            eng.wait_ge(s, value)
            eng.sem_inc(held, 1)

        AHEAD = 1

        def start_ahead(eng, *sems):
            for s in sems:
                eng.sem_inc(s, AHEAD)

        MOD_READY = 15
        BIAS_READY = 20
        POWERS_READY = 35
        N_CONST = 24
        NORM = 10
        NORM_H = NORM + 2
        HOT_READY, DIFF_READY, CNTB_READY, LO_READY, INDEX_READY = 5, 8, 11, 32, 40
        SCAN = LEVELS + 4

        block = ctx.enter_context(nc.Block())

        @block.sync
        def _(sp):
            x_v = x.rearrange("b (j p) d -> b p j d", p=P)
            start_ahead(sp, st_rec)

            def load_in(b):
                sp.dma_start(x_sb[:, b.place], x_v[b.n]).then_inc(ld_x[b.place], 16)

            def load_mod_in(b):
                sp.dma_start(mod_in[:, b.place].rearrange("p v d -> p (v d)"),
                             mod_dram[b.n, 0:3 * D].partition_broadcast(P)).then_inc(ld_x[b.place], 16)

            def load_mod_post(b):
                sp.dma_start(mod_post[:, b.place].rearrange("p v d -> p (v d)"),
                             mod_dram[b.n, 3 * D:GB].partition_broadcast(P)).then_inc(ld_mp[b.place], 16)

            def store_rows(b):
                sp.wait_ge(h2_done, 2 * JT * b.n + 2 * JT)
                sp.dma_start(table.rearrange("(b j p) n -> b p j n", p=P, j=JT)[b.n, :, :, 0:2 * D],
                             rec[:, :, :]).then_inc(st_rec, 16)

            sp.dma_start(wmod_sb, wmod.rearrange("(k p) n -> p k n", p=P)).then_inc(ld_wmod, 16)
            sp.dma_start(silc[:, 0], cT.rearrange("(k p) b -> p k b", p=P)).then_inc(ld_wmod, 16)
            sp.dma_start(wx_nat, W_in[0:DI, :].rearrange("(k p) d -> p k d", p=P)).then_inc(ld_small, 16)
            for dst, src in (
                (powers[:, 1, (CH - 1) * NS:CH * NS], A), (powers[:, 0, (CH - 1) * NS:CH * NS], AT),
                (bmT, BmT.rearrange("(k p) s -> p k s", p=P)),
                (bias_raw[0:E * FF // P], b1.rearrange("e (c n) -> (e c) n", n=P)),
                (bias_raw[E * FF // P:NB], b2.rearrange("e (c n) -> (e c) n", n=P)),
                (gb_col[:, 0], gamma),
                (gb_col[:, 1], beta),
                (cw, conv_w),
                (cb, conv_b),
                (wr_sb[:, :, :], wr.rearrange("(k p) e -> p k e", p=P)),
                (br_sb[:, :], br.partition_broadcast(P)),
            ):
                sp.dma_start(dst, src).then_inc(ld_small, 16)
            load_in(Batch(0, 0))
            sp.dma_start(w_in, W_inT.rearrange("(k p) n -> p k n", p=P)).then_inc(ld_w, 16)
            sp.dma_start(w_out, W_outT.rearrange("(k p) n -> p k n", p=P)).then_inc(ld_w, 16)
            load_in(Batch(0, 1))
            for t in range(CH):
                sp.dma_start(cm_t[NS * t:NS * (t + 1), :], Cm).then_inc(ld_cm, 16)
            sp.wait_ge(su_d, MOD_READY)
            sp.dma_start(mod_dram, mod_sb).then_inc(st_mod, 16)
            sp.dma_start(gb_dram, mod_sb[:, GB:]).then_inc(st_mod, 16)
            sp.wait_ge(st_mod, 32)
            for b in (Batch(0, 0), Batch(0, 1)):
                load_mod_in(b)
                load_mod_post(b)
            for b in range(B):
                sp.dma_start(table[b * L:(b + 1) * L, 2 * D:],
                             gb_dram[b].partition_broadcast(L)).then_inc(st_mod, 16)
            sp.wait_ge(su_d, BIAS_READY)
            sp.dma_start(bias_dram.rearrange("s (r n) -> r s n", n=P), bias_3).then_inc(st_bias, 16)

            def step(i, first, last):
                if first:
                    return
                if not last:
                    sp.wait_ge(xh_done, 2 * i.n)
                    sp.wait_ge(w_ga_done, i.n)
                    load_in(i + 1)
                    load_mod_in(i + 1)
                store_rows(i + -1)
                if not last:
                    load_mod_post(i + 1)
            batches(sp, step)
            store_rows(Batch(B // 2 - 1, 1))
            sp.wait_ge(y_done, KC * B)
            sp.wait_ge(so_ps, KC * B)
            for e in (E - 2, E - 1):
                sp.dma_start(experts[:, e, 0:WE].rearrange("p (k n) -> p k n", k=KD),
                             w1[e].rearrange("(k p) n -> p k n", p=P)).then_inc(ld_ex[e], 16)
                sp.dma_start(experts[:, e, WE:].rearrange("p (k n) -> p k n", k=KF),
                             w2[e].rearrange("(k p) n -> p k n", p=P)).then_inc(ld_ex[e], 16)
            sp.wait_ge(op_ps, 2 * B)
            sp.wait_ge(st_bias, 16)
            sp.dma_start(bias[:, 0:E * (FF + D)], bias_dram).then_inc(ld_bias, 16)

        @block.scalar
        def _(act):
            start_ahead(act, hid_done, hidT_a)
            for e in range(E - 2):
                act.dma_start(experts[:, e, 0:WE].rearrange("p (k n) -> p k n", k=KD),
                              w1[e].rearrange("(k p) n -> p k n", p=P)).then_inc(ld_ex[e], 16)
                act.dma_start(experts[:, e, WE:].rearrange("p (k n) -> p k n", k=KF),
                              w2[e].rearrange("(k p) n -> p k n", p=P)).then_inc(ld_ex[e], 16)
            act.wait_ge(ld_wmod, 32)
            act.activation(silc[:, 1], silc[:, 0], ACT.Sigmoid).then_inc(su_a, 1)
            act.wait_ge(ld_small, 16 * 12)

            def trans_out(b):
                for k in range(KD):
                    act.wait_ge(xn_trans, KD * b.n + k + 1)
                    act.activation(xnT[:, k, :], banks[TR[k]][:, :], ACT.Identity, bias=gb_col[:, 1, k:k + 1],
                                   scale=gb_col[:, 0, k:k + 1]).then_inc(xnT_done, 1)

            def v_out(b):
                act.wait_ge(v_ps, b.n + 1)
                act.activation(v_sb, banks[TR[1]][0:NS, :], ACT.Copy).then_inc(v_done, 1)

            def h2_out(b):
                for k in range(KD):
                    act.wait_ge(h2_trans, AHEAD + KD * b.n + k + 1)
                    act.activation(h2T[:, k, :], banks[TR[k]][:, :], ACT.Copy).then_inc(h2T_done, 1)

            def normalize(b, first):
                if not first:
                    act.wait_ge(xn_trans, KD * b.n)
                act.wait_ge(norm_h, NORM_H * (b.n + 1))
                for j in range(JT):
                    act.activation(xn_sb[:, j, :], h_sb[:, j, :], ACT.Identity, bias=shift_h[:, 1, j:j + 1],
                                   scale=mr[:, 1, 1, j:j + 1]).then_inc(xn_done, 1)

            normalize(Batch(0, 0), True)
            trans_out(Batch(0, 0))
            v_out(Batch(0, 0))

            def step(i, first, last):
                for j in range(KC):
                    if not first:
                        act.wait_ge(y_done, KC * (i + -1).n + j + 1)
                    act.wait_ge(xz_ps, 2 * KC * i.n + j + 1)
                    act.activation(zg[:, j, :], rot[j], ACT.Sigmoid).then_inc(zg_done, 1)
                for j in range(KC):
                    if j == 2 and not last:
                        normalize(i + 1, False)
                    act.wait_ge(xz_ps, 2 * KC * i.n + KC + j + 1)
                    act.activation(conv[:, j, :], rot[j], ACT.Identity, bias=cb[:, j:j + 1],
                                   scale=cw[:, j, TAPS - 1:TAPS]).then_inc(tap0_done, 1)
                if not last:
                    trans_out(i + 1)
                for j in range(KC):
                    if j == 2:
                        if not last:
                            v_out(i + 1)
                        if not first:
                            h2_out(i + -1)
                    act.wait_ge(conv_done, 3 * KC * i.n + 3 * j + 3)
                    act.activation(conv[:, j, :], conv[:, j, :], ACT.Silu).then_inc(silu_done, 1)
            batches(act, step)
            h2_out(Batch(B // 2 - 1, 1))

            act.wait_ge(ro_d, DIFF_READY)
            act.activation(r_gate, r_dif, ACT.Sigmoid).then_inc(ro_a, 1)

            def gelu(k):
                for h in range(2):
                    if not k is FIRST_TILE:
                        act.wait_ge(t2_ps, AHEAD + 2 * (k + -1).n)
                    act.wait_ge(f1_ps, 2 * k.n + h + 1)
                    act.activation(hid[:, k.place % 2, 512 * h:512 * h + 512], banks[1 + 2 * (k.place % 2) + h][:, :],
                                   ACT.Gelu).then_inc(hid_done, 1)

            def hidT_low(k):
                act.wait_ge(t2_ps, AHEAD + 2 * k.n + 1)
                act.activation(hidT[:, 0:4, :].rearrange("p i t -> p (i t)"), banks[5][:, :],
                               ACT.Copy).then_inc(hidT_a, 1)

            gelu(FIRST_TILE)

            def tile(k):
                hidT_low(k + -1)
                gelu(k)
            tiles(act, tile)
            hidT_low(LAST_TILE)

        @block.gpsimd
        def _(pool):
            made = [0]

            def const(ins):
                made[0] += 1
                ins.then_inc(cst, 1)
                pool.wait_ge(cst, made[0])

            const(pool.memset(powers[:, 0, (CH + 1) * NS:], 0.0))
            const(pool.memset(own_row[:, :], 1.0))
            const(pool.affine_select(out=own_row[:, :], in_=own_row[:, :], compare_op=ALU.is_ge, fill=0.0,
                                     base=-NS * (CH - 1), pattern=[[NS, CH]], channel_multiplier=1))
            const(pool.affine_select(out=own_row[:, :], in_=own_row[:, :], compare_op=ALU.is_ge, fill=0.0,
                                     base=NS * CH - 1, pattern=[[-NS, CH]], channel_multiplier=-1))
            for i, v in enumerate((0.5, 1.0 / D, 0.25, EPS, -0.5, 0.0)):
                const(pool.memset(const4[:, i, :], v))
            const(pool.memset(ident[:, :], 0.0))
            const(pool.affine_select(out=ident[:, :], in_=ident[:, :], compare_op=ALU.not_equal, fill=1.0,
                                     base=0, pattern=[[-1, P]], channel_multiplier=1))
            const(pool.memset(ones_bf[:, :], 1.0))
            const(pool.memset(lt_tok[:, :], 1.0))
            const(pool.affine_select(out=lt_tok[:, :], in_=lt_tok[:, :], compare_op=ALU.is_gt, fill=0.0,
                                     base=0, pattern=[[1, P]], channel_multiplier=-1))
            const(pool.memset(lt_et[:, :, :], 1.0))
            const(pool.affine_select(out=lt_et[:, :, :], in_=lt_et[:, :, :], compare_op=ALU.is_gt, fill=0.0,
                                     base=0, pattern=[[-P, 2], [1, 2 * P]], channel_multiplier=-1))
            const(pool.memset(lt_e[:, :, :], 1.0))
            const(pool.affine_select(out=lt_e[:, :, :], in_=lt_e[:, :, :], compare_op=ALU.is_gt, fill=0.0,
                                     base=0, pattern=[[1, E], [-1, E]], channel_multiplier=0))
            for dst, pattern, base, mult in ((iota, [[1, P]], 0, 0), (tok1, [[P, NT]], 1, 1),
                                             (rev, [[-1, E]], E, 0), (k128, [[P, NT]], 0, 0)):
                const(pool.iota(dst[:, :], pattern=pattern, base=base, channel_multiplier=mult,
                                allow_small_or_imprecise_dtypes=True))
            const(pool.memset(r_e[:, 0, E:E + 1], float(T)))
            assert made[0] == N_CONST

            def norm(b, st, out, ready, sem, total=NORM):
                me, qe, mo, qo = (st[:, :, c] for c in (1, 2, 4, 5))
                s, d, q, v = (tmp[:, c, :] for c in range(4))
                steps = [0]

                def op(o, a, b_, f):
                    steps[0] += 1
                    pool.tensor_tensor(o, a, b_, f).then_inc(sem, 1)

                def so_far():
                    pool.wait_ge(sem, total * b.n + steps[0])

                pool.wait_ge(ready, JT * b.n + JT)
                op(s, me, mo, ALU.add)
                op(d, me, mo, ALU.subtract)
                op(q, qe, qo, ALU.add)
                so_far()
                op(out[:, 0, :], s, half4, ALU.mult)
                op(d, d, d, ALU.mult)
                op(q, q, inv4, ALU.mult)
                so_far()
                op(d, d, quart4, ALU.mult)
                op(q, q, eps4, ALU.add)
                so_far()
                op(v, d, q, ALU.add)
                so_far()
                op(out[:, 1, :], v, mhalf4, ALU.pow)
                so_far()
                if total == NORM_H:
                    op(shift_h[:, 0, :], out[:, 0, :], out[:, 1, :], ALU.mult)
                    so_far()
                    op(shift_h[:, 1, :], zero4, shift_h[:, 0, :], ALU.subtract)
                    so_far()
                assert steps[0] == total

            def norms_in(b):
                norm(b, stat[:, 0], mr[:, 0], stats_x, norm_x)
                norm(b, stat[:, 1], mr[:, 1], stats_h, norm_h, NORM_H)

            def residual(b, first):
                pool.wait_ge(ld_x[b.place], 32 * (b.turn + 1))
                pool.wait_ge(h_done, 2 * JT * b.n + 2 * JT)
                if not first:
                    pool.wait_ge(x1_done, 2 * (b + -1).n)
                pool.tensor_tensor(xh[:, b.place], h_sb, bcast(mod_in[:, b.place, 2, :], 1, JT),
                                   ALU.mult).then_inc(xh_done, 1)
                pool.wait_ge(xh_done, 2 * b.n + 1)
                pool.tensor_tensor(xh[:, b.place], xh[:, b.place], x_sb[:, b.place],
                                   ALU.add).then_inc(xh_done, 1)

            norms_in(Batch(0, 0))
            pool.wait_ge(ld_w, 32)
            residual(Batch(0, 0), True)

            def step(i, first, last):
                if not last:
                    norms_in(i + 1)
                if not first:
                    norm(i + -1, stat_c, mr[:, 2], stats_p, norm_p)
                if not first:
                    pool.wait_ge(op_ps, 2 * i.n)
                pool.tensor_tensor(w_ga, w_out, bcast(mod_in[:, i.place, 2, :], 1, KC),
                                   ALU.mult).then_inc(w_ga_done, 1)
                if not last:
                    residual(i + 1, first)
                for j in range(KC):
                    pool.wait_ge(zg_done, KC * i.n + j + 1)
                    pool.wait_ge(t_done, KC * i.n + j + 1)
                    pool.tensor_tensor(y_sb[:, j, :], conv[:, j, :], zg[:, j, :],
                                       ALU.mult).then_inc(y_done, 1)
            batches(pool, step)
            norm(Batch(B // 2 - 1, 1), stat_c, mr[:, 2], stats_p, norm_p)

            pool.wait_ge(st_rec, AHEAD + 16 * B)
            pool.wait_ge(st_mod, 16 * (2 + B))
            pool.wait_ge(ro_d, INDEX_READY)

            def gather(k):
                pool.tensor_copy(idx_k[:, k.place, :],
                                 idx_i[:, :, bass.ds(k.n, 1)].rearrange("p v o -> p (v o)")).then_inc(idx_done, 1)
                hold(pool, idx_done, k.n + 1)
                pool.indirect_dma_start(
                    out=rows[:, k.place, :], out_offset=None, in_=table,
                    in_offset=bass.IndirectOffsetOnAxis(ap=idx_k[:, k.place, 0:1], axis=0)).then_inc(got[k.place], 16)

            def scatter(k):
                hold(pool, res_done, AHEAD + k.n + 1)
                pool.indirect_dma_start(
                    out=out.rearrange("b l d -> (b l) d"),
                    out_offset=bass.IndirectOffsetOnAxis(ap=idx_k[:, k.place, 1:2], axis=0),
                    in_=res[:, k.place, :], in_offset=None,
                    bounds_check=T - 1, oob_is_err=False).then_inc(put[k.place], 16)

            def turn(k):
                scatter(k)
                hold(pool, put[k.place], 16 * (k.turn + 1))
                gather(k + Tile.TURN)

            for k in range(Tile.TURN):
                gather(Tile(0, k))
            whole = (SLOTS - Tile.TURN) // Tile.TURN
            with pool.Fori(0, whole) as r:
                for p in range(Tile.TURN):
                    turn(Tile(r, p))
            for k in range(whole * Tile.TURN, SLOTS - Tile.TURN):
                turn(Tile(0, 0) + k)
            for k in range(SLOTS - Tile.TURN, SLOTS):
                scatter(Tile(0, 0) + k)
            for p in range(Tile.TURN):
                pool.wait_ge(put[p], 16 * ((SLOTS - p + Tile.TURN - 1) // Tile.TURN))

        @block.vector
        def _(dve):
            chained = [0]

            def link(ins, s=su_d):
                chained[0] += 1
                ins.then_inc(s, 1)
                dve.wait_ge(s, chained[0])

            start_ahead(dve, lg_done, res_done, hidT_d, gated)
            dve.wait_ge(su_a, 1)
            link(dve.tensor_tensor(silc[:, 0], silc[:, 0], silc[:, 1], ALU.mult))
            dve.wait_ge(su_p, 1)
            row = [banks[v // 2][0:B, (v % 2) * D:(v % 2) * D + D] for v in range(NM)]
            dst = [mod_sb[:, v * D:(v + 1) * D] for v in range(NM)]
            for v in (0, 3):
                link(dve.tensor_copy(dst[v], row[v]))
            for v in (1, 4):
                link(dve.tensor_scalar(dst[v], row[v], 1.0, None, ALU.add))
            for v in (2, 5):
                link(dve.tensor_scalar(sgn[:, 0:D], row[v], 0.0, 2.0, ALU.is_ge, ALU.mult))
                link(dve.tensor_copy(dst[v], row[v]))
                link(dve.scalar_tensor_tensor(sgn[:, D:2 * D], dst[v], -1.0, dst[v], ALU.mult, ALU.max))
                link(dve.tensor_scalar(sgn[:, D:2 * D], sgn[:, D:2 * D], 0.25, None, ALU.max))
                link(dve.scalar_tensor_tensor(dst[v], sgn[:, 0:D], -1.0, sgn[:, D:2 * D], ALU.add, ALU.mult))
            assert chained[0] == MOD_READY
            dve.wait_ge(ld_small, 16 * 12)
            link(dve.tensor_copy(bias_3[:, 0], bias_raw))
            link(dve.tensor_tensor(bias_rest[:, 0], bias_raw, bias_3[:, 0], ALU.subtract))
            link(dve.tensor_copy(bias_3[:, 1], bias_rest[:, 0]))
            link(dve.tensor_tensor(bias_rest[:, 1], bias_rest[:, 0], bias_3[:, 1], ALU.subtract))
            link(dve.tensor_copy(bias_3[:, 2], bias_rest[:, 1]))
            assert chained[0] == BIAS_READY
            dve.wait_ge(cst, N_CONST)
            link(dve.tensor_copy(powers[:, 0, CH * NS:(CH + 1) * NS], ident[0:NS, 0:NS]))
            dve.wait_ge(su_p, 2)
            link(dve.tensor_copy(g_in[:, :, :], banks[3][:, 0:KD * NS].rearrange("p (k n) -> p k n", k=KD)))
            two = banks[4][0:NS, 0:2 * NS].rearrange("p (v n) -> p v n", v=2)
            for k in range(2, CH + 1):
                dve.wait_ge(su_p, k + 1)
                link(dve.tensor_copy(powers[:, :, (CH - k) * NS:(CH - k + 1) * NS], two))
            link(dve.tensor_copy(dbl[:, 0], two))
            for lv in range(1, LEVELS):
                dve.wait_ge(su_p, CH + 1 + lv)
                link(dve.tensor_copy(dbl[:, lv], two))
            assert chained[0] == POWERS_READY

            def stats_in(b):
                dve.wait_ge(ld_x[b.place], 32 * (b.turn + 1))
                for j in range(JT):
                    dve.bn_stats(stat[:, 0, j, :], x_sb[:, b.place, j, :]).then_inc(stats_x, 1)

            def modulate_scale(b):
                dve.wait_ge(xh_done, 2 * b.n)
                dve.wait_ge(xn_done, JT * b.n)
                dve.wait_ge(norm_x, NORM * (b.n + 1))
                for j in range(JT):
                    dve.scalar_tensor_tensor(h_sb[:, j, :], x_sb[:, b.place, j, :], mr[:, 0, 0, j:j + 1],
                                             mod_in[:, b.place, 1, :], ALU.subtract, ALU.mult).then_inc(h_done, 1)

            def modulate_shift(b):
                for j in range(JT):
                    dve.wait_ge(h_done, 2 * JT * b.n + j + 1)
                    dve.scalar_tensor_tensor(h_sb[:, j, :], h_sb[:, j, :], mr[:, 0, 1, j:j + 1],
                                             mod_in[:, b.place, 0, :], ALU.mult, ALU.add).then_inc(h_done, 1)

            def stats_h_in(b):
                for j in range(JT):
                    dve.wait_ge(h_done, 2 * JT * b.n + JT + j + 1)
                    dve.bn_stats(stat[:, 1, j, :], h_sb[:, j, :]).then_inc(stats_h, 1)

            def taps(i, j):
                dve.wait_ge(tap0_done, KC * i.n + j + 1)
                for d in range(1, TAPS):
                    if d > 1:
                        dve.wait_ge(conv_done, 3 * KC * i.n + 3 * j + d - 1)
                    dve.scalar_tensor_tensor(conv[:, j, d:], rot[j][:, 0:L - d],
                                             cw[:, j, TAPS - 1 - d:TAPS - d], conv[:, j, d:],
                                             ALU.mult, ALU.add).then_inc(conv_done, 1)

            def chunk_states(i):
                dve.wait_ge(so_ps, KC * i.n)
                dve.wait_ge(loc_ps, i.n + 1)
                dve.tensor_copy(l_state[:, :], state_ps[:, 0:NC]).then_inc(scan_done, 1)
                dve.tensor_copy(e_state[:, :], state_ps[0:NS, 0:NC]).then_inc(scan_done, 1)

            def double(i, lv):
                m = 1 << lv
                dve.wait_ge(scan_ps, (LEVELS + 1) * i.n + lv + 1)
                dve.tensor_tensor(e_state[:, m:], e_state[:, m:], state_ps[0:NS, NC:2 * NC - m],
                                  ALU.add).then_inc(scan_done, 1)

            def all_states(i):
                dve.wait_ge(scan_ps, (LEVELS + 1) * (i.n + 1))
                dve.tensor_tensor(l_state[:, 1:], l_state[:, 1:], state_ps[:, 2 * NC:3 * NC - 1],
                                  ALU.add).then_inc(scan_done, 1)
                dve.wait_ge(scan_done, SCAN * i.n + LEVELS + 3)
                dve.tensor_tensor(spread.rearrange("p (c t) -> p c t", t=CH), bcast(l_state[:, :], 2, CH),
                                  bcast(own_row[:, :], 1, NC), ALU.mult).then_inc(scan_done, 1)

            def add_states(i, j):
                dve.wait_ge(silu_done, KC * i.n + j + 1)
                dve.wait_ge(so_ps, KC * i.n + j + 1)
                dve.tensor_tensor(conv[:, j, :], conv[:, j, :], rot[j], ALU.add).then_inc(t_done, 1)

            def residual_out(b):
                dve.wait_ge(st_rec, AHEAD + 16 * b.n)
                dve.wait_ge(h2_trans, AHEAD + KD * b.n)
                dve.wait_ge(xh_done, 2 * b.n + 2)
                for h in range(2):
                    dve.wait_ge(op_ps, 2 * b.n + h + 1)
                    dve.tensor_tensor(rec[:, 2 * h:2 * h + 2, D:], banks[OUT0 + h][:, :].rearrange("p (j d) -> p j d", j=2),
                                      xh[:, b.place, 2 * h:2 * h + 2, :], ALU.add).then_inc(x1_done, 1)
                for h in range(2):
                    dve.wait_ge(x1_done, 2 * b.n + h + 1)
                    for j in (2 * h, 2 * h + 1):
                        dve.bn_stats(stat_c[:, j, :], rec[:, j, D:]).then_inc(stats_p, 1)

            def modulate_out(b):
                dve.wait_ge(ld_mp[b.place], 16 * (b.turn + 1))
                dve.wait_ge(norm_p, NORM * (b.n + 1))
                for j in range(JT):
                    dve.scalar_tensor_tensor(rec[:, j, 0:D], rec[:, j, D:], mr[:, 2, 0, j:j + 1],
                                             mod_post[:, b.place, 1, :], ALU.subtract, ALU.mult).then_inc(h2_done, 1)
                for j in range(JT):
                    dve.wait_ge(h2_done, 2 * JT * b.n + j + 1)
                    dve.scalar_tensor_tensor(rec[:, j, 0:D], rec[:, j, 0:D], mr[:, 2, 1, j:j + 1],
                                             mod_post[:, b.place, 0, :], ALU.mult, ALU.add).then_inc(h2_done, 1)

            def keep_logits(b):
                dve.wait_ge(lg_ps, b.n + 1)
                dve.tensor_tensor(logits[:, bass.ds(b.n * JT, JT), :],
                                  banks[OUT0][:, 0:JT * E].rearrange("p (j e) -> p j e", j=JT),
                                  bcast(br_sb[:, :], 1, JT), ALU.add).then_inc(lg_done, 1)

            stats_in(Batch(0, 0))
            modulate_scale(Batch(0, 0))
            modulate_shift(Batch(0, 0))
            stats_h_in(Batch(0, 0))
            dve.wait_ge(st_bias, 16)

            def step(i, first, last):
                chunk_states(i)
                if not last:
                    stats_in(i + 1)
                double(i, 0)
                double(i, 1)
                if not last:
                    modulate_scale(i + 1)
                double(i, 2)
                if not last:
                    modulate_shift(i + 1)
                double(i, 3)
                if not last:
                    stats_h_in(i + 1)
                double(i, 4)
                taps(i, 0)
                double(i, 5)
                taps(i, 1)
                all_states(i)
                if not first:
                    residual_out(i + -1)
                taps(i, 2)
                if not first:
                    modulate_out(i + -1)
                taps(i, 3)
                for j in range(KC):
                    add_states(i, j)
                if not first:
                    keep_logits(i + -1)
            batches(dve, step)
            residual_out(Batch(B // 2 - 1, 1))
            modulate_out(Batch(B // 2 - 1, 1))
            keep_logits(Batch(B // 2 - 1, 1))

            chained[0] = 0

            def route(ins):
                link(ins, ro_d)

            lg = logits[:, :, :]
            dve.wait_ge(lg_done, AHEAD + B)
            route(dve.tensor_reduce(r_m1, lg, AX.X, ALU.max))
            route(dve.tensor_tensor(r_val, lg, bcast(r_m1, 2, E), ALU.is_equal))
            route(dve.tensor_tensor(r_val, r_val, bcast(rev[:, :], 1, NT), ALU.mult))
            route(dve.tensor_reduce(r_mv, r_val, AX.X, ALU.max))
            hot_te = onehot.rearrange("p (e t) -> p t e", e=E)
            route(dve.tensor_tensor(hot_te, r_val, bcast(r_mv, 2, E), ALU.is_equal))
            assert chained[0] == HOT_READY
            route(dve.scalar_tensor_tensor(r_low, hot_te, -1e30, lg, ALU.mult, ALU.add))
            route(dve.tensor_reduce(r_m2, r_low, AX.X, ALU.max))
            route(dve.tensor_tensor(r_dif, r_m1, r_m2, ALU.subtract))
            assert chained[0] == DIFF_READY
            dve.wait_ge(ro_p, 1)
            route(dve.tensor_copy(r_cnt2[:, :], banks[2][:, 0:2]))
            for c in range(2):
                route(dve.tensor_scalar(r_cntb[:, c, :], ones_bf[:, :], r_cnt2[:, c:c + 1], None, ALU.mult))
            assert chained[0] == CNTB_READY
            dve.wait_ge(ro_p, 2)
            start, count, ntile, first_t, end_t, off = (r_e[:, v, 0:E] for v in range(6))
            route(dve.tensor_copy(start, banks[3][:, 0:2 * P].rearrange("p (e t) -> p e t", e=E)[:, :, 0]))
            route(dve.tensor_tensor(count, r_e[:, 0, 1:E + 1], start, ALU.subtract))
            cmp = r_cmp[:, 0:E * NT].rearrange("p (e t) -> p e t", e=E)
            route(dve.tensor_tensor(cmp, bcast(count, 2, NT), bcast(k128[:, :], 1, E), ALU.is_gt))
            route(dve.tensor_reduce(ntile, cmp, AX.X, ALU.add))
            cmp = r_cmp[:, 0:E * E].rearrange("p (e f) -> p e f", e=E)
            route(dve.tensor_tensor(cmp, lt_e[:, :, :], bcast(ntile, 1, E), ALU.mult))
            route(dve.tensor_reduce(first_t, cmp, AX.X, ALU.add))
            route(dve.tensor_tensor(end_t, first_t, ntile, ALU.add))
            route(dve.scalar_tensor_tensor(off, first_t, float(P), start, ALU.mult, ALU.subtract))
            dve.wait_ge(ro_p, 3)
            route(dve.tensor_tensor(r_sum, banks[4][:, 0:2 * P].rearrange("p (e t) -> p e t", e=E),
                                    bcast(off, 2, NT), ALU.add))
            route(dve.tensor_tensor(r_sum, r_sum, onehot.rearrange("p (e t) -> p e t", e=E), ALU.mult))
            route(dve.tensor_reduce(r_slot, r_sum.rearrange("p e t -> p t e"), AX.X, ALU.add))
            route(dve.tensor_copy(r_int, r_slot))
            route(dve.tensor_scalar(r_int2, r_int, P - 1, None, ALU.bitwise_and))
            route(dve.tensor_copy(r_lo, r_int2))
            route(dve.tensor_scalar(r_int2, r_int, P.bit_length() - 1, None, ALU.arith_shift_right))
            route(dve.tensor_copy(r_hi, r_int2))
            route(dve.tensor_tensor(hot_hi, bcast(iota[:, 0:SLOTS], 1, NT), bcast(r_hi, 2, SLOTS), ALU.is_equal))
            route(dve.tensor_tensor(hot_val[:, :, 0, :], hot_hi, bcast(tok1[:, :], 2, SLOTS), ALU.mult))
            dve.wait_ge(ro_a, 1)
            route(dve.tensor_tensor(hot_val[:, :, 1, :], hot_hi, bcast(r_gate, 2, SLOTS), ALU.mult))
            half = NT // 2
            for c in range(2):
                route(dve.tensor_tensor(hot_lo[c], bcast(iota[:, :], 1, half),
                                        bcast(r_lo[:, c * half:(c + 1) * half], 2, P), ALU.is_equal))
            assert chained[0] == LO_READY
            cmp = r_cmp[0:1, 0:SLOTS * E].rearrange("p (k e) -> p k e", k=SLOTS)
            route(dve.tensor_tensor(cmp, bcast(iota[0:1, 0:SLOTS], 2, E), bcast(end_t[0:1, :], 1, SLOTS), ALU.is_ge))
            route(dve.tensor_reduce(ek_f[:, :], cmp, AX.X, ALU.add))
            route(dve.tensor_scalar(ek[:, :], ek_f[:, :], float(E - 1), None, ALU.min))
            dve.wait_ge(ro_p, 4)
            route(dve.tensor_copy(inv[:, :, :], banks[5][:, 0:2 * SLOTS].rearrange("p (v k) -> p v k", v=2)))
            route(dve.tensor_scalar(idx_f[:, 0, :], inv[:, 0, :], -1.0, 0.0, ALU.add, ALU.max))
            route(dve.tensor_copy(idx_i[:, 0, :], idx_f[:, 0, :]))
            route(dve.tensor_scalar(idx_f[:, 1, :], inv[:, 0, :], 0.0, float(FAR), ALU.is_equal, ALU.mult))
            route(dve.scalar_tensor_tensor(idx_i[:, 1, :], idx_f[:, 1, :], -1.0, inv[:, 0, :], ALU.add, ALU.add))
            assert chained[0] == INDEX_READY

            def hT_out(k):
                dve.wait_ge(t1_ps, k.n + 1)
                dve.tensor_copy(hT[:, k.place % 2].rearrange("p k t -> p (k t)"), banks[0][:, 0:D]).then_inc(hT_done, 1)

            def hidT_high(k):
                dve.wait_ge(t2_ps, AHEAD + 2 * k.n + 2)
                dve.tensor_copy(hidT[:, 4:8, :].rearrange("p i t -> p (i t)"), banks[6][:, :]).then_inc(hidT_d, 1)

            def finish(k):
                dve.wait_ge(f2_ps, k.n + 1)
                dve.scalar_tensor_tensor(res[:, k.place, :], banks[7][:, 0:D], inv[:, 1, bass.ds(k.n, 1)],
                                         rows[:, k.place, 2 * D:], ALU.mult, ALU.mult).then_inc(gated, 1)
                dve.wait_ge(gated, AHEAD + k.n + 1)
                dve.tensor_tensor(res[:, k.place, :], res[:, k.place, :], rows[:, k.place, D:2 * D],
                                  ALU.add).then_inc(res_done, 1)

            hT_out(FIRST_TILE)
            hT_out(FIRST_TILE + 1)

            def tile(k):
                hidT_high(k + -1)
                if not is_last(k):
                    hT_out(k + 1)
                finish(k + -1)
            tiles(dve, tile)
            hidT_high(LAST_TILE)
            finish(LAST_TILE)

        @block.tensor
        def _(pe):
            start_ahead(pe, h2_trans, t2_ps)
            pe.wait_ge(su_d, 1)
            for v in range(NM // 2):
                for k in range(KD):
                    mm = pe.matmul(banks[v][0:B, :], silc[:, 0, k, :], wmod_sb[:, k, v * 512:(v + 1) * 512],
                                   start=(k == 0), stop=(k == KD - 1))
            mm.then_inc(su_p, 1)
            pe.wait_ge(ld_small, 16 * 12)
            for c in range(KD):
                for k in range(KC):
                    mm = pe.matmul(banks[3][:, c * NS:(c + 1) * NS], wx_nat[:, k, c * P:(c + 1) * P], bmT[:, k, :],
                                   start=(k == 0), stop=(k == KC - 1))
            mm.then_inc(su_p, 1)
            at_pow = [powers[:, 0, j * NS:(j + 1) * NS] for j in range(CH + 1)]
            a_pow = [powers[:, 1, j * NS:(j + 1) * NS] for j in range(CH)]
            for k in range(2, CH + 1):
                pe.wait_ge(su_d, BIAS_READY + k)
                pe.matmul(banks[4][0:NS, 0:NS], a_pow[CH - 1], at_pow[CH - k + 1], start=True, stop=True)
                pe.matmul(banks[4][0:NS, NS:2 * NS], at_pow[CH - 1], a_pow[CH - k + 1],
                          start=True, stop=True).then_inc(su_p, 1)
            for lv in range(1, LEVELS):
                pe.wait_ge(su_d, BIAS_READY + CH + 1 + lv)
                pe.matmul(banks[4][0:NS, 0:NS], dbl[:, lv - 1, 1], dbl[:, lv - 1, 0], start=True, stop=True)
                pe.matmul(banks[4][0:NS, NS:2 * NS], dbl[:, lv - 1, 0], dbl[:, lv - 1, 1],
                          start=True, stop=True).then_inc(su_p, 1)
            pe.wait_ge(su_d, POWERS_READY)
            pe.wait_ge(ld_w, 32)
            pe.wait_ge(ld_cm, 16 * CH)
            pe.wait_ge(cst, N_CONST)

            def xn_transpose(b, first):
                for k in range(KD):
                    if k == 1 and not first:
                        pe.wait_ge(x1_done, 2 * (b + -1).n)
                    for j in range(JT):
                        if k == 0:
                            pe.wait_ge(xn_done, JT * b.n + j + 1)
                        tr = pe.transpose(banks[TR[k]][:, j * P:(j + 1) * P], xn_sb[:, j, k * P:(k + 1) * P], ident[:, :])
                    tr.then_inc(xn_trans, 1)

            def state_inputs(b):
                pe.wait_ge(xnT_done, KD * (b.n + 1))
                for k in range(KD):
                    mm = pe.matmul(banks[TR[1]][0:NS, :], g_in[:, k, :], xnT[:, k, :], start=(k == 0), stop=(k == KD - 1))
                mm.then_inc(v_ps, 1)

            def local_states(b):
                pe.wait_ge(v_done, b.n + 1)
                for s in range(CH):
                    mm = pe.matmul(state_ps[:, 0:NC], powers[:, 0, (s + 1) * NS:(s + 1) * NS + P], v_sb[:, s::CH],
                                   start=(s == 0), stop=(s == CH - 1))
                mm.then_inc(loc_ps, 1)

            def project(b, j, is_x):
                c = j * P + (0 if is_x else DI)
                for k in range(KD):
                    mm = pe.matmul(rot[j], w_in[:, k, c:c + P], xnT[:, k, :], start=(k == 0), stop=(k == KD - 1))
                mm.then_inc(xz_ps, 1)

            def double(i, lv):
                m = 1 << lv
                hold(pe, scan_done, SCAN * i.n + 2 + lv)
                pe.matmul(state_ps[0:NS, NC:2 * NC - m], dbl[:, lv, 0], e_state[:, 0:NC - m],
                          start=True, stop=True).then_inc(scan_ps, 1)

            def carry_states(i):
                pe.wait_ge(scan_done, SCAN * i.n + 2 + LEVELS)
                pe.matmul(state_ps[:, 2 * NC:3 * NC - 1], powers[:, 0, 0:CH * NS], e_state[:, 0:NC - 1],
                          start=True, stop=True).then_inc(scan_ps, 1)

            def state_out(i, j):
                if j == 0:
                    pe.wait_ge(scan_done, SCAN * (i.n + 1))
                pe.wait_ge(conv_done, 3 * KC * i.n + 3 * j + 3)
                pe.matmul(rot[j], cm_t[:, j * P:(j + 1) * P], spread, start=True, stop=True).then_inc(so_ps, 1)

            def project_out(b, j):
                if j == 0:
                    pe.wait_ge(y_done, KC * (b.n + 1))
                    pe.wait_ge(w_ga_done, b.n + 1)
                    pe.wait_ge(lg_done, AHEAD + b.n)
                for k in range(KC):
                    mm = pe.matmul(banks[OUT0 + j // 2][:, (j % 2) * D:(j % 2 + 1) * D],
                                   y_sb[:, k, j * P:(j + 1) * P], w_ga[:, k, :], start=(k == 0), stop=(k == KC - 1))
                if j % 2 == 1:
                    mm.then_inc(op_ps, 1)

            def h2_transpose(b, v_left):
                pe.wait_ge(h2_done, 2 * JT * (b.n + 1))
                for k in range(KD):
                    if k == 1:
                        pe.wait_ge(v_done, v_left)
                    for j in range(JT):
                        tr = pe.transpose(banks[TR[k]][:, j * P:(j + 1) * P], rec[:, j, k * P:(k + 1) * P], ident[:, :])
                    tr.then_inc(h2_trans, 1)

            def router(b):
                pe.wait_ge(h2T_done, KD * (b.n + 1))
                for j in range(JT):
                    for k in range(KD):
                        mm = pe.matmul(banks[OUT0][:, j * E:(j + 1) * E], h2T[:, k, j * P:(j + 1) * P], wr_sb[:, k, :],
                                       start=(k == 0), stop=(k == KD - 1))
                mm.then_inc(lg_ps, 1)

            xn_transpose(Batch(0, 0), True)
            state_inputs(Batch(0, 0))
            local_states(Batch(0, 0))

            def step(i, first, last):
                def project_x(j):
                    pe.wait_ge(zg_done, KC * i.n + j + 1)
                    project(i, j, True)

                for j in range(KC):
                    if not first:
                        pe.wait_ge(t_done, KC * (i + -1).n + j + 1)
                    project(i, j, False)
                    if j >= 1:
                        double(i, j - 1)
                for j in range(2):
                    project_x(j)
                    double(i, j + 3)
                for j in range(JT):
                    if not first:
                        project_out(i + -1, j)
                    if j == 0:
                        double(i, LEVELS - 1)
                    if j == 1:
                        carry_states(i)
                for j in range(2, KC):
                    project_x(j)
                if not last:
                    xn_transpose(i + 1, first)
                state_out(i, 0)
                state_out(i, 1)
                state_out(i, 2)
                if not last:
                    state_inputs(i + 1)
                if not first:
                    h2_transpose(i + -1, i.n + (1 if last else 2))
                if not last:
                    local_states(i + 1)
                if not first:
                    router(i + -1)
                state_out(i, 3)
            batches(pe, step)
            for j in range(JT):
                project_out(Batch(B // 2 - 1, 1), j)
            h2_transpose(Batch(B // 2 - 1, 1), B)
            router(Batch(B // 2 - 1, 1))

            pe.wait_ge(ro_d, HOT_READY)
            for c in range(2):
                mm = pe.matmul(banks[2][:, c:c + 1], onehot[:, c * P:(c + 1) * P], ones_bf[:, 0:1], start=True, stop=True)
            mm.then_inc(ro_p, 1)
            pe.wait_ge(ro_d, CNTB_READY)
            for c in range(2):
                mm = pe.matmul(banks[3][:, 0:2 * P], r_cntb[:, c, :], lt_et[:, c, :], start=(c == 0), stop=(c == 1))
            mm.then_inc(ro_p, 1)
            pe.matmul(banks[4][:, 0:2 * P], lt_tok[:, :], onehot, start=True, stop=False)
            for c in range(2):
                mm = pe.matmul(banks[4][:, 0:2 * P], r_cntb[:, c, :], lt_et[:, c, :], start=False, stop=(c == 1))
            mm.then_inc(ro_p, 1)
            for t in range(NT):
                if t % (NT // 2) == 0:
                    pe.wait_ge(ro_d, LO_READY - 1 + t // (NT // 2))
                mm = pe.matmul(banks[5][:, 0:2 * SLOTS], hot_lo[t // (NT // 2)][:, t % (NT // 2), :],
                               hot_val[:, t, :, :].rearrange("p v k -> p (v k)"), start=(t == 0), stop=(t == NT - 1))
            mm.then_inc(ro_p, 1)

            for e in range(E):
                pe.wait_ge(ld_ex[e], 32)
            pe.wait_ge(ld_bias, 16)
            pe.wait_ge(ro_d, INDEX_READY)

            def expert(k):
                return pe.value_load(ek[0:1, bass.ds(k.n, 1)], min_val=0, max_val=E - 1)

            def turn_in(k):
                if k is not FIRST_TILE:
                    pe.wait_ge(hT_done, k.n)
                pe.wait_ge(got[k.place], 16 * (k.turn + 1))
                for c in range(KD):
                    tr = pe.transpose(banks[0][:, c * P:(c + 1) * P], rows[:, k.place, c * P:(c + 1) * P], ident[:, :])
                tr.then_inc(t1_ps, 1)

            def up(k):
                e = expert(k)
                if k is not FIRST_TILE:
                    pe.wait_ge(hid_done, AHEAD + 2 * (k + -1).n)
                pe.wait_ge(hT_done, k.n + 1)
                w = experts[:, bass.ds(e, 1), :].rearrange("p o n -> p (o n)")
                bw = bias1[:, bass.ds(e, 1), :].rearrange("p o n -> p (o n)")
                for h in range(2):
                    bank = banks[1 + 2 * (k.place % 2) + h][:, :]
                    for c in range(KD):
                        pe.matmul(bank, hT[:, k.place % 2, c, :], w[:, c * FF + 512 * h:c * FF + 512 * h + 512],
                                  start=(c == 0), stop=False)
                    pe.matmul(bank, ones_bf[0:3, :], bw[:, 512 * h:512 * h + 512],
                              start=False, stop=True).then_inc(f1_ps, 1)

            def turn_hidden(k):
                hold(pe, hid_done, AHEAD + 2 * (k.n + 1))
                for i in range(KF):
                    if i % 4 == 0:
                        pe.wait_ge(hidT_a if i == 0 else hidT_d, AHEAD + k.n)
                    tr = pe.transpose(banks[5 + i // 4][:, (i % 4) * P:(i % 4 + 1) * P],
                                      hid[:, k.place % 2, i * P:(i + 1) * P], ident[:, :])
                    if i % 4 == 3:
                        tr.then_inc(t2_ps, 1)

            def down(k):
                e = expert(k)
                hold(pe, gated, AHEAD + k.n)
                hold(pe, hidT_d, AHEAD + k.n + 1)
                pe.wait_ge(hidT_a, AHEAD + k.n + 1)
                w = experts[:, bass.ds(e, 1), :].rearrange("p o n -> p (o n)")
                bw = bias2[:, bass.ds(e, 1), :].rearrange("p o n -> p (o n)")
                for i in range(KF):
                    pe.matmul(banks[7][:, 0:D], hidT[:, i, :], w[:, WE + i * D:WE + (i + 1) * D],
                              start=(i == 0), stop=False)
                pe.matmul(banks[7][:, 0:D], ones_bf[0:3, :], bw, start=False, stop=True).then_inc(f2_ps, 1)

            turn_in(FIRST_TILE)
            turn_in(FIRST_TILE + 1)
            up(FIRST_TILE)

            def tile(k):
                turn_hidden(k + -1)
                if not is_last(k):
                    turn_in(k + 1)
                up(k)
                down(k + -1)
            tiles(pe, tile)
            turn_hidden(LAST_TILE)
            down(LAST_TILE)


_INS = ['x', 'ln_gamma', 'ln_beta', 'W_in', 'W_inT', 'conv_w', 'conv_b', 'W_outT', 'A', 'AT', 'BmT', 'Cm',
        'w1', 'b1', 'w2', 'b2', 'wr', 'br', 'cT', 'wmod']
_OUTS = [((8, 512, 256), 'float32')]


def kernel(**inputs):
    import numpy as _np
    import concourse.bacc as _bacc
    from concourse import mybir as _mybir
    from concourse.bass_utils import run_bass_kernel_spmd as _run

    given = {n.replace('L0_attn_', '').replace('L0_ffn_', '').replace('L0_', ''): _np.asarray(a)
             for n, a in inputs.items()}
    for name, of in (('W_inT', 'W_in'), ('W_outT', 'W_out'), ('AT', 'A'), ('BmT', 'Bm'), ('cT', 'c')):
        given[name] = given[of].T
    for name in ('ln_gamma', 'ln_beta', 'conv_b', 'conv_w'):
        a = given[name]
        given[name] = a.reshape((a.shape[0] // P, P) + a.shape[2:]).swapaxes(0, 1)
    nc = _bacc.Bacc("TRN2", target_bir_lowering=False, num_devices=1)
    arrays, args = {}, []
    for name in _INS:
        a = _np.ascontiguousarray(given[name])
        arrays[f"in_{name}_dram"] = a
        args.append(nc.dram_tensor(f"in_{name}_dram", a.shape, _mybir.dt.from_np(a.dtype), kind="ExternalInput").ap())
    for i, (shape, dtype) in enumerate(_OUTS):
        dt = _mybir.dt.from_np(_np.dtype(dtype))
        args.append(nc.dram_tensor(f"out_{i}_dram", shape, dt, kind="ExternalOutput").ap())
    adaln_mamba_moe(nc, *args)
    r = _run(nc, [arrays], core_ids=[0])
    return r.results[0]["out_0_dram"]
```

```python
from contextlib import ExitStack

import concourse.bass as bass
from concourse import mybir

F32 = mybir.dt.float32
F32R = mybir.dt.float32r
BF16 = mybir.dt.bfloat16
I32 = mybir.dt.int32
ALU = mybir.AluOpType
ACT = mybir.ActivationFunctionType
AX = mybir.AxisListType

P = 128
EPS = 1e-5


class Step:
    TURN = 1

    def __init__(self, turns, plus):
        self.turns, self.plus = turns, plus
        self.place = plus % self.TURN
        self.turn = turns + plus // self.TURN if plus >= self.TURN else turns
        self.n = turns * self.TURN + plus

    def __add__(self, k):
        return type(self)(self.turns, self.plus + k)


class Batch(Step):
    TURN = 2


class Tile(Step):
    TURN = 4


def bcast(ap, axis, n):
    ap = ap.unsqueeze(axis)
    shape = list(ap.shape)
    shape[axis] = n
    return ap.to_broadcast(shape)


def adaln_mamba_moe(nc, x, gamma, beta, W_in, W_inT, conv_w, conv_b, W_outT, A, AT, BmT, Cm,
                    w1, b1, w2, b2, wr, br, cT, wmod, out):
    B, L, D = x.shape
    T = B * L
    DI = W_outT.shape[0]
    NS = A.shape[0]
    E, _, FF = w1.shape
    KD = D // P
    KC = DI // P
    KF = FF // P
    JT = L // P
    NT = T // P
    CH = P // NS
    NC = L // CH
    LEVELS = NC.bit_length() - 1
    TAPS = conv_w.shape[2]
    SLOTS = (T - E) // P + E
    NM = wmod.shape[1] // D
    GB = (NM - 1) * D
    WE = KD * FF
    FAR = 2 * T

    table = nc.dram_tensor("token_rows", [T, 3 * D], F32).ap()
    mod_dram = nc.dram_tensor("mod_rows", [B, NM * D], F32).ap()
    gb_dram = nc.dram_tensor("gb_rows", [B, D], F32).ap()
    bias_dram = nc.dram_tensor("bias_parts", [3, E * (FF + D)], BF16).ap()

    ctx = ExitStack()
    with ctx:
        def sb(name, shape, dt=F32):
            return ctx.enter_context(nc.sbuf_tensor(name, shape, dt))

        def sem(name):
            return ctx.enter_context(nc.semaphore(name))

        raw = sb("raw", [P, 2, WE + KF * D])
        stage = sb("stage", [P, WE + KF * D])
        w_parts = sb("w_parts", [P, 2, 2, WE + KF * D], F32R)
        hT = sb("hT", [P, 2, 2, D], F32R)
        hidT = sb("hidT", [P, 2, FF], F32R)
        proj = sb("proj", [P, KD * 2 * DI + KC * D + 2 * JT * D])
        w_in = proj[:, 0:KD * 2 * DI].rearrange("p (k n) -> p k n", k=KD)
        w_out = proj[:, 2048:3072].rearrange("p (k n) -> p k n", k=KC)
        x_sb = proj[:, 3072:5120].rearrange("p (b j d) -> p b j d", b=2, j=JT)
        mods = sb("mods", [P, 2 * 3 * D + 2 * 2 * D + 2 * JT * D])
        mod_in = mods[:, 0:1536].rearrange("p (b v d) -> p b v d", b=2, v=3)
        mod_post = mods[:, 1536:2560].rearrange("p (b v d) -> p b v d", b=2, v=2)
        h_sb = mods[:, 2560:3584].rearrange("p (j d) -> p j d", j=JT)
        xn_sb = mods[:, 3584:4608].rearrange("p (j d) -> p j d", j=JT)
        xh = sb("xh", [P, 2, JT, D])
        trans = sb("trans", [P, 2 * KD * L])
        xnT = trans[:, 0:1024].rearrange("p (k t) -> p k t", k=KD)
        h2T = trans[:, 1024:2048].rearrange("p (k t) -> p k t", k=KD)
        y_sb = sb("y_sb", [P, KC, L])
        rec = sb("rec", [P, JT, 2 * D])
        g_in = sb("g_in", [P, KD, NS])
        own_row = sb("own_row", [P, CH])
        ident = sb("ident", [P, P])
        l_state = sb("l_state", [P, NC])
        e_state = sb("e_state", [NS, NC])
        logits = sb("logits", [P, NT, E])
        wr_sb = sb("wr_sb", [P, KD, E])
        cols = sb("cols", [P, 2 * KD + (TAPS + 1) * KC])
        gb_col = cols[:, 0:4].rearrange("p (v k) -> p v k", v=2)
        cw = cols[:, 4:20].rearrange("p (j k) -> p j k", j=KC)
        cb = cols[:, 20:24]
        br_sb = sb("br_sb", [P, E])
        powers = sb("powers", [NS, 2, 2 * CH * NS])
        dbl = sb("dbl", [NS, LEVELS, 2, NS])
        stat = sb("stat", [P, 2, JT, 6])
        stat_c = sb("stat_c", [P, JT, 6])
        mr = sb("mr", [P, 3, 2, JT])
        shift_h = sb("shift_h", [P, 2, JT])
        tmp = sb("tmp", [P, 4, JT])
        const4 = sb("const4", [P, 6, JT])
        half4, inv4, quart4, eps4, mhalf4, zero4 = (const4[:, i, :] for i in range(6))
        lt_tok = sb("lt_tok", [P, P], BF16)
        lt_et = sb("lt_et", [P, 2, 2 * P], BF16)
        ones_bf = sb("ones_bf", [P, P], BF16)
        iota = sb("iota", [P, P])
        tile1 = sb("tile1", [P, NT])
        place_tok = sb("place_tok", [P, 1])
        rev = sb("rev", [P, E])
        k128 = sb("k128", [P, NT])
        lt_e = sb("lt_e", [P, E, E])
        conv = raw[:, 0, 0:KC * L].rearrange("p (k t) -> p k t", k=KC)
        zg = raw[:, 0, KC * L:2 * KC * L].rearrange("p (k t) -> p k t", k=KC)
        cm_t = raw[:, 1, 0:DI]
        w_ga = raw[:, 1, DI + 2 * L:DI + 2 * L + KC * D].rearrange("p (k n) -> p k n", k=KC)
        v_sb = raw[0:NS, 1, DI:DI + L]
        spread = raw[:, 1, DI + L:DI + 2 * L]
        w_in_parts = w_parts[:, 1, :, 0:KD * 2 * DI].rearrange("p v (k n) -> p v k n", k=KD)
        xnT_parts = w_parts[:, 1, :, KD * 2 * DI:KD * 2 * DI + KD * L].rearrange("p v (k t) -> p v k t", k=KD)
        wmod_sb = raw[:, 0, 0:KD * NM * D].rearrange("p (k n) -> p k n", k=KD)
        wx_nat = raw[:, 0, KD * NM * D:4096].rearrange("p (k d) -> p k d", k=KC)
        mod_sb = xh[0:B, :, :, :].rearrange("p a j d -> p (a j d)")[:, 0:NM * D]
        sgn = y_sb[0:B, 0, :]
        silc = y_sb[:, 1, 0:2 * KD * B].rearrange("p (s k b) -> p s k b", s=2, k=KD)
        bmT = y_sb[:, 3, 0:KC * NS].rearrange("p (k s) -> p k s", k=KC)
        NB = E * (FF + D) // P
        bias_raw = rec[0:NB, 0, 0:P]
        bias_rest = rec[0:NB, 1, 0:2 * P].rearrange("p (s n) -> p s n", s=2)
        bias_3 = rec[0:NB, 2, :].bitcast(BF16)[:, 0:3 * P].rearrange("p (s n) -> p s n", s=3)
        onehot = xnT.rearrange("p k t -> p (k t)")[:, 0:128].bitcast(BF16)
        r_val = xnT.rearrange("p k t -> p (k t)")[:, 256:512].rearrange("p (t e) -> p t e", t=NT)
        r_low = xnT.rearrange("p k t -> p (k t)")[:, 512:768].rearrange("p (t e) -> p t e", t=NT)
        r_cntb = xnT.rearrange("p k t -> p (k t)")[:, 768:896].bitcast(BF16) \
            .rearrange("p (c m) -> p c m", c=2)
        r_sum = h2T.rearrange("p k t -> p (k t)")[:, 0:256].rearrange("p (e t) -> p e t", e=E)
        r_cmp = h2T.rearrange("p k t -> p (k t)")[:, 256:576]
        after_rows = mods[:, Tile.TURN * 3 * D:]
        small = after_rows[:, 0:10 * NT].rearrange("p (v t) -> p v t", v=10)
        r_m1, r_mv, r_m2, r_dif, r_gate, r_slot_f = (small[:, i, :] for i in range(6))
        r_slot, r_lo, r_hi = (small[:, i, :].bitcast(I32) for i in range(6, 9))
        r_cnt2 = sb("r_cnt2", [P, 2])
        r_e = sb("r_e", [P, 6, E + 1])
        hot_lo = y_sb[:, :, :].rearrange("p k t -> p (k t)").bitcast(BF16).rearrange("p (t m) -> p t m", m=P)
        hot = stage[:, 0:3 * NT * SLOTS].bitcast(BF16).rearrange("p (v t k) -> p v t k", v=6, k=SLOTS)
        hot_hi = hot[:, 0]
        gate_3 = h2T.rearrange("p k t -> p (k t)")[:, 640:640 + 3 * NT // 2].bitcast(BF16) \
            .rearrange("p (v t) -> p v t", v=3)
        gate_rest = h2T.rearrange("p k t -> p (k t)")[:, 704:704 + 2 * NT].rearrange("p (v t) -> p v t", v=2)
        inv = after_rows[:, 320:398].rearrange("p (v k) -> p v k", v=2)
        inv_2 = r_cmp[:, 0:2 * SLOTS].rearrange("p (v k) -> p v k", v=2)
        idx_f = after_rows[:, 398:476].rearrange("p (v k) -> p v k", v=2)
        idx_i = after_rows[:, 476:554].bitcast(I32).rearrange("p (v k) -> p v k", v=2)
        tile_tab = sb("tile_tab", [1, 4, SLOTS], I32)
        EXPERT, PLACE, OTHER, PART = range(4)
        ek_f = sb("ek_f", [1, 2, SLOTS])
        idx_k = sb("idx_k", [P, 2, Tile.TURN], I32)
        bias = proj[0:3, :].bitcast(BF16)
        bias1 = bias[:, 0:E * FF].rearrange("p (e n) -> p e n", e=E)
        bias2 = bias[:, E * FF:E * (FF + D)].rearrange("p (e n) -> p e n", e=E)
        rows = mods[:, 0:Tile.TURN * 3 * D].rearrange("p (b n) -> p b n", b=Tile.TURN)
        hid = xh[:, :, :, :].rearrange("p a j d -> p a (j d)")
        res = rec[:, 0:2, :].rearrange("p a (b d) -> p (a b) d", b=2)

        banks = [ctx.enter_context(nc.psum_tensor(f"bank{i}", [P, 512], F32)) for i in range(8)]
        ROT, ROTN = 2, 4
        OUT0 = 6
        TR = (0, 7)
        rot = [banks[ROT + i][:, :] for i in range(ROTN)]
        state_ps = banks[1]

        ld_w, ld_small, ld_wmod = sem("ld_w"), sem("ld_small"), sem("ld_wmod")
        ld_x = [sem(f"ld_x{i}") for i in range(2)]
        ld_mi = [sem(f"ld_mi{i}") for i in range(2)]
        ld_mp = [sem(f"ld_mp{i}") for i in range(2)]
        ld_cm = sem("ld_cm")
        w_in_hi, w_in_lo, xn_hi, xn_lo = sem("w_in_hi"), sem("w_in_lo"), sem("xn_hi"), sem("xn_lo")
        ld_stage, ld_raw, w_hi, w_lo = sem("ld_stage"), sem("ld_raw"), sem("w_hi"), sem("w_lo")
        st_mod, st_bias, st_rec = sem("st_mod"), sem("st_bias"), sem("st_rec")
        ld_bias = sem("ld_bias")
        cst = sem("cst")
        su_d, su_p, su_a = sem("su_d"), sem("su_p"), sem("su_a")
        su_m, su_w = sem("su_m"), sem("su_w")
        stats_x, stats_h, stats_p = sem("stats_x"), sem("stats_h"), sem("stats_p")
        norm_x, norm_h, norm_p = sem("norm_x"), sem("norm_h"), sem("norm_p")
        h_done, xn_done, xh_done = sem("h_done"), sem("xn_done"), sem("xh_done")
        xn_trans, xnT_done = sem("xn_trans"), sem("xnT_done")
        v_ps, v_done, loc_ps = sem("v_ps"), sem("v_done"), sem("loc_ps")
        scan_ps, scan_done = sem("scan_ps"), sem("scan_done")
        xz_ps = sem("xz_ps")
        tap0_done, conv_done, zg_done, silu_done = (sem("tap0_done"), sem("conv_done"),
                                                    sem("zg_done"), sem("silu_done"))
        so_ps, t_done, y_done = sem("so_ps"), sem("t_done"), sem("y_done")
        w_ga_done, op_ps, x1_done, h2_done = sem("w_ga_done"), sem("op_ps"), sem("x1_done"), sem("h2_done")
        h2_trans, h2T_done, lg_ps, lg_done = (sem("h2_trans"), sem("h2T_done"), sem("lg_ps"),
                                              sem("lg_done"))
        held = sem("held")
        ro_d, ro_p, ro_a = sem("ro_d"), sem("ro_p"), sem("ro_a")
        hot_done = sem("hot_done")
        idx_done = sem("idx_done")
        got = [sem(f"got{i}") for i in range(Tile.TURN)]
        put = [sem(f"put{i}") for i in range(Tile.TURN)]
        t1_ps, hT_hi, hT_lo = sem("t1_ps"), sem("hT_hi"), sem("hT_lo")
        f1_ps, hid_done = sem("f1_ps"), sem("hid_done")
        t2_ps, hidT_hi, hidT_lo, f2_ps = sem("t2_ps"), sem("hidT_hi"), sem("hidT_lo"), sem("f2_ps")
        gated, res_done = sem("gated"), sem("res_done")

        def batches(eng, step):
            step(Batch(0, 0), first=True, last=False)
            with eng.Fori(0, B // 2 - 1) as r:
                step(Batch(r, 1), first=False, last=False)
                step(Batch(r, 2), first=False, last=False)
            step(Batch(B // 2 - 1, 1), first=False, last=True)

        def tiles(eng, step):
            steps = 2 * Tile.TURN
            with eng.Fori(0, (SLOTS - 1) // steps) as r:
                for p in range(1, steps + 1):
                    step(Tile(2 * r, 0) + p)
            for k in range((SLOTS - 1) // steps * steps + 1, SLOTS):
                step(Tile(0, 0) + k)

        def is_last(k):
            return isinstance(k.n, int) and k.n == SLOTS - 1

        FIRST_TILE, LAST_TILE = Tile(0, 0), Tile(0, 0) + (SLOTS - 1)

        def hold(eng, s, value):
            eng.wait_ge(s, value)
            eng.sem_inc(held, 1)

        def load_expert(eng, dst, e, done):
            eng.dma_start(dst[:, 0:WE].rearrange("p (k n) -> p k n", k=KD),
                          w1[e].rearrange("(k p) n -> p k n", p=P)).then_inc(done, 16)
            eng.dma_start(dst[:, WE:].rearrange("p (k n) -> p k n", k=KF),
                          w2[e].rearrange("(k p) n -> p k n", p=P)).then_inc(done, 16)

        def at(ap, i):
            return ap[:, bass.ds(i, 1)].rearrange("p o n -> p (o n)")

        def lookup(eng, what, k):
            return eng.value_load(tile_tab[0:1, what, bass.ds(k.n, 1)], min_val=0, max_val=(E - 1 if what == EXPERT else 1))

        AHEAD = 1

        def start_ahead(eng, *sems):
            for s in sems:
                eng.sem_inc(s, AHEAD)

        MOD_IN_READY = 8
        MOD_READY = 15
        BIAS_READY = 20
        POWERS_READY = 15
        N_CONST = 25
        NORM = 10
        NORM_H = NORM + 2
        HOT_READY, DIFF_READY, CNTB_READY, HI_READY, LO_READY, INDEX_READY, TABLE_READY, GATES_READY = 5, 8, 11, 27, 31, 41, 51, 54
        LO_CUTS = 4
        SCAN = LEVELS + 4

        block = ctx.enter_context(nc.Block())

        @block.sync
        def _(sp):
            x_v = x.rearrange("b (j p) d -> b p j d", p=P)
            start_ahead(sp, st_rec)

            def load_in(b):
                sp.dma_start(x_sb[:, b.place], x_v[b.n]).then_inc(ld_x[b.place], 16)

            def load_mod_in(b):
                sp.dma_start(mod_in[:, b.place].rearrange("p v d -> p (v d)"),
                             mod_dram[b.n, 0:3 * D].partition_broadcast(P)).then_inc(ld_mi[b.place], 16)

            def load_mod_post(b):
                sp.dma_start(mod_post[:, b.place].rearrange("p v d -> p (v d)"),
                             mod_dram[b.n, 3 * D:GB].partition_broadcast(P)).then_inc(ld_mp[b.place], 16)

            def store_rows(b):
                sp.wait_ge(h2_done, 2 * JT * b.n + 2 * JT)
                sp.dma_start(table.rearrange("(b j p) n -> b p j n", p=P, j=JT)[b.n, :, :, 0:2 * D],
                             rec[:, :, :]).then_inc(st_rec, 16)

            sp.dma_start(wmod_sb, wmod.rearrange("(k p) n -> p k n", p=P)).then_inc(ld_wmod, 16)
            sp.dma_start(silc[:, 0], cT.rearrange("(k p) b -> p k b", p=P)).then_inc(ld_wmod, 16)
            sp.dma_start(wx_nat, W_in[0:DI, :].rearrange("(k p) d -> p k d", p=P)).then_inc(ld_small, 16)
            for dst, src in (
                (powers[:, 1, (CH - 1) * NS:CH * NS], A), (powers[:, 0, (CH - 1) * NS:CH * NS], AT),
                (bmT, BmT.rearrange("(k p) s -> p k s", p=P)),
                (bias_raw[0:E * FF // P], b1.rearrange("e (c n) -> (e c) n", n=P)),
                (bias_raw[E * FF // P:NB], b2.rearrange("e (c n) -> (e c) n", n=P)),
                (gb_col[:, 0], gamma),
                (gb_col[:, 1], beta),
                (cw, conv_w),
                (cb, conv_b),
                (wr_sb[:, :, :], wr.rearrange("(k p) e -> p k e", p=P)),
                (br_sb[:, :], br.partition_broadcast(P)),
            ):
                sp.dma_start(dst, src).then_inc(ld_small, 16)
            load_in(Batch(0, 0))
            sp.dma_start(w_in, W_inT.rearrange("(k p) n -> p k n", p=P)).then_inc(ld_w, 16)
            sp.dma_start(w_out, W_outT.rearrange("(k p) n -> p k n", p=P)).then_inc(ld_w, 16)
            load_in(Batch(0, 1))
            for t in range(CH):
                sp.dma_start(cm_t[NS * t:NS * (t + 1), :], Cm).then_inc(ld_cm, 16)
            sp.wait_ge(su_d, MOD_IN_READY)
            sp.dma_start(mod_dram[:, 0:3 * D], mod_sb[:, 0:3 * D]).then_inc(st_mod, 16)
            sp.wait_ge(st_mod, 16)
            load_mod_in(Batch(0, 0))
            load_mod_in(Batch(0, 1))
            sp.wait_ge(su_d, MOD_READY)
            sp.dma_start(mod_dram[:, 3 * D:], mod_sb[:, 3 * D:]).then_inc(st_mod, 16)
            sp.dma_start(gb_dram, mod_sb[:, GB:]).then_inc(st_mod, 16)
            sp.wait_ge(st_mod, 48)
            load_mod_post(Batch(0, 0))
            load_mod_post(Batch(0, 1))
            for b in range(B):
                sp.dma_start(table[b * L:(b + 1) * L, 2 * D:],
                             gb_dram[b].partition_broadcast(L)).then_inc(st_mod, 16)
            sp.wait_ge(su_d, BIAS_READY)
            sp.dma_start(bias_dram.rearrange("s (r n) -> r s n", n=P), bias_3).then_inc(st_bias, 16)

            def step(i, first, last):
                if first:
                    return
                if not last:
                    sp.wait_ge(xh_done, 2 * i.n)
                    sp.wait_ge(w_ga_done, i.n)
                    load_in(i + 1)
                    load_mod_in(i + 1)
                else:
                    sp.wait_ge(w_lo, 2)
                    load_expert(sp, stage[:, :], 1, ld_stage)
                store_rows(i + -1)
                if not last:
                    load_mod_post(i + 1)
            batches(sp, step)
            store_rows(Batch(B // 2 - 1, 1))
            sp.wait_ge(y_done, KC * B)
            load_expert(sp, raw[:, 0], 2, ld_raw)
            sp.wait_ge(op_ps, 2 * B)
            sp.wait_ge(st_bias, 16)
            sp.dma_start(bias[:, 0:E * (FF + D)], bias_dram).then_inc(ld_bias, 16)
            for e in range(3, E):
                sp.wait_ge(ld_raw, 32 * (e - 2))
                if e >= 4:
                    sp.wait_ge(w_lo, 2 * (e - 1))
                load_expert(sp, raw[:, e % 2], e, ld_raw)

        @block.scalar
        def _(act):
            start_ahead(act, hid_done)
            load_expert(act, stage[:, :], 0, ld_stage)
            act.wait_ge(ld_wmod, 32)
            act.activation(silc[:, 1], silc[:, 0], ACT.Sigmoid).then_inc(su_a, 1)

            def first_hi(e):
                act.wait_ge(ld_stage, 32 * (e + 1))
                for h in range(2):
                    act.activation(w_parts[:, e, 0, h * WE:(h + 1) * WE], stage[:, h * WE:(h + 1) * WE],
                                   ACT.Copy).then_inc(w_hi, 1)

            act.wait_ge(ld_w, 32)
            act.activation(w_in_parts[:, 0], w_in, ACT.Copy).then_inc(w_in_hi, 1)
            act.wait_ge(ld_small, 16 * 12)

            def trans_out(b):
                for k in range(KD):
                    act.wait_ge(xn_trans, KD * b.n + k + 1)
                    act.activation(xnT[:, k, :], banks[TR[k]][:, :], ACT.Identity, bias=gb_col[:, 1, k:k + 1],
                                   scale=gb_col[:, 0, k:k + 1]).then_inc(xnT_done, 1)
                for k in range(KD):
                    act.wait_ge(xnT_done, KD * b.n + k + 1)
                    act.activation(xnT_parts[:, 0, k, :], xnT[:, k, :], ACT.Copy).then_inc(xn_hi, 1)

            def v_out(b):
                act.wait_ge(v_ps, b.n + 1)
                act.activation(v_sb, banks[TR[1]][0:NS, :], ACT.Copy).then_inc(v_done, 1)

            def h2_out(b):
                for k in range(KD):
                    act.wait_ge(h2_trans, AHEAD + KD * b.n + k + 1)
                    act.activation(h2T[:, k, :], banks[TR[k]][:, :], ACT.Copy).then_inc(h2T_done, 1)

            def normalize(b, first):
                if not first:
                    act.wait_ge(xn_trans, KD * b.n)
                act.wait_ge(norm_h, NORM_H * (b.n + 1))
                for j in range(JT):
                    act.activation(xn_sb[:, j, :], h_sb[:, j, :], ACT.Identity, bias=shift_h[:, 1, j:j + 1],
                                   scale=mr[:, 1, 1, j:j + 1]).then_inc(xn_done, 1)

            normalize(Batch(0, 0), True)
            trans_out(Batch(0, 0))
            v_out(Batch(0, 0))

            def step(i, first, last):
                for j in range(KC):
                    if not first:
                        act.wait_ge(y_done, KC * (i + -1).n + j + 1)
                    act.wait_ge(xz_ps, 2 * KC * i.n + j + 1)
                    act.activation(zg[:, j, :], rot[j], ACT.Sigmoid).then_inc(zg_done, 1)
                for j in range(KC):
                    if j == 2 and not last:
                        normalize(i + 1, False)
                    act.wait_ge(xz_ps, 2 * KC * i.n + KC + j + 1)
                    act.activation(conv[:, j, :], rot[j], ACT.Identity, bias=cb[:, j:j + 1],
                                   scale=cw[:, j, TAPS - 1:TAPS]).then_inc(tap0_done, 1)
                if not last:
                    trans_out(i + 1)
                for j in range(KC):
                    if j == 2:
                        if not last:
                            v_out(i + 1)
                        if not first:
                            h2_out(i + -1)
                    act.wait_ge(conv_done, 3 * KC * i.n + 3 * j + 3)
                    act.activation(conv[:, j, :], conv[:, j, :], ACT.Silu).then_inc(silu_done, 1)
                if first:
                    first_hi(0)
            batches(act, step)
            act.wait_ge(xz_ps, 2 * KC * B)
            first_hi(1)
            h2_out(Batch(B // 2 - 1, 1))

            act.wait_ge(ro_d, DIFF_READY)
            act.activation(r_gate, r_dif, ACT.Sigmoid).then_inc(ro_a, 1)
            act.wait_ge(ro_d, HI_READY)
            act.activation(hot[:, 2], hot_hi, ACT.Copy, scale=place_tok[:, :]).then_inc(ro_a, 1)

            def gelu(k):
                for h in range(2):
                    if not k is FIRST_TILE:
                        act.wait_ge(t2_ps, AHEAD + 2 * (k + -1).n)
                    act.wait_ge(f1_ps, 2 * k.n + h + 1)
                    act.activation(hid[:, k.place % 2, 512 * h:512 * h + 512], banks[1 + 2 * (k.place % 2) + h][:, :],
                                   ACT.Gelu).then_inc(hid_done, 1)

            def hT_out(k):
                act.wait_ge(t1_ps, k.n + 1)
                act.activation(hT[:, k.place % 2, 0, :], banks[0][:, 0:D], ACT.Copy).then_inc(hT_hi, 1)

            def hidT_out(k):
                for h in range(2):
                    act.wait_ge(t2_ps, AHEAD + 2 * k.n + h + 1)
                    act.activation(hidT[:, 0, 512 * h:512 * h + 512], banks[5 + h][:, :], ACT.Copy).then_inc(hidT_hi, 1)

            def part(k, h):
                with act.If(lookup(act, PART, k) > 0):
                    e, other = lookup(act, EXPERT, k), lookup(act, OTHER, k)
                    if h == 0:
                        act.wait_ge(f1_ps, 2 * k.n)
                    else:
                        act.wait_ge(f2_ps, k.n)
                    act.wait_ge(ld_raw, 32 * e)
                    act.activation(at(w_parts[:, :, 0, h * WE:(h + 1) * WE], other),
                                   at(raw[:, :, h * WE:(h + 1) * WE], other), ACT.Copy).then_inc(w_hi, 1)

            hT_out(FIRST_TILE)
            hT_out(FIRST_TILE + 1)
            gelu(FIRST_TILE)

            def tile(k):
                hidT_out(k + -1)
                if not is_last(k):
                    hT_out(k + 1)
                part(k + -1, 1)
                part(k, 0)
                gelu(k)
            tiles(act, tile)
            hidT_out(LAST_TILE)

        @block.gpsimd
        def _(pool):
            made = [0]

            def const(ins):
                made[0] += 1
                ins.then_inc(cst, 1)
                pool.wait_ge(cst, made[0])

            const(pool.memset(powers[:, 0, (CH + 1) * NS:], 0.0))
            const(pool.memset(own_row[:, :], 1.0))
            const(pool.affine_select(out=own_row[:, :], in_=own_row[:, :], compare_op=ALU.is_ge, fill=0.0,
                                     base=-NS * (CH - 1), pattern=[[NS, CH]], channel_multiplier=1))
            const(pool.affine_select(out=own_row[:, :], in_=own_row[:, :], compare_op=ALU.is_ge, fill=0.0,
                                     base=NS * CH - 1, pattern=[[-NS, CH]], channel_multiplier=-1))
            for i, v in enumerate((0.5, 1.0 / D, 0.25, EPS, -0.5, 0.0)):
                const(pool.memset(const4[:, i, :], v))
            const(pool.memset(ident[:, :], 0.0))
            const(pool.affine_select(out=ident[:, :], in_=ident[:, :], compare_op=ALU.not_equal, fill=1.0,
                                     base=0, pattern=[[-1, P]], channel_multiplier=1))
            const(pool.memset(ones_bf[:, :], 1.0))
            const(pool.memset(lt_tok[:, :], 1.0))
            const(pool.affine_select(out=lt_tok[:, :], in_=lt_tok[:, :], compare_op=ALU.is_gt, fill=0.0,
                                     base=0, pattern=[[1, P]], channel_multiplier=-1))
            const(pool.memset(lt_et[:, :, :], 1.0))
            const(pool.affine_select(out=lt_et[:, :, :], in_=lt_et[:, :, :], compare_op=ALU.is_gt, fill=0.0,
                                     base=0, pattern=[[-P, 2], [1, 2 * P]], channel_multiplier=-1))
            const(pool.memset(lt_e[:, :, :], 1.0))
            const(pool.affine_select(out=lt_e[:, :, :], in_=lt_e[:, :, :], compare_op=ALU.is_gt, fill=0.0,
                                     base=0, pattern=[[1, E], [-1, E]], channel_multiplier=0))
            for dst, pattern, base, mult in ((iota[:, :], [[1, P]], 0, 0), (tile1[:, :], [[1, NT]], 1, 0),
                                             (place_tok[:, :], [[0, 1]], 0, 1), (rev[:, :], [[-1, E]], E, 0), (k128[:, :], [[P, NT]], 0, 0)):
                const(pool.iota(dst, pattern=pattern, base=base, channel_multiplier=mult,
                                allow_small_or_imprecise_dtypes=True))
            const(pool.memset(r_e[:, 0, E:E + 1], float(T)))
            assert made[0] == N_CONST

            def norm(b, st, out, ready, sem, total=NORM):
                me, qe, mo, qo = (st[:, :, c] for c in (1, 2, 4, 5))
                s, d, q, v = (tmp[:, c, :] for c in range(4))
                steps = [0]

                def op(o, a, b_, f):
                    steps[0] += 1
                    pool.tensor_tensor(o, a, b_, f).then_inc(sem, 1)

                def so_far():
                    pool.wait_ge(sem, total * b.n + steps[0])

                pool.wait_ge(ready, JT * b.n + JT)
                op(s, me, mo, ALU.add)
                op(d, me, mo, ALU.subtract)
                op(q, qe, qo, ALU.add)
                so_far()
                op(out[:, 0, :], s, half4, ALU.mult)
                op(d, d, d, ALU.mult)
                op(q, q, inv4, ALU.mult)
                so_far()
                op(d, d, quart4, ALU.mult)
                op(q, q, eps4, ALU.add)
                so_far()
                op(v, d, q, ALU.add)
                so_far()
                op(out[:, 1, :], v, mhalf4, ALU.pow)
                so_far()
                if total == NORM_H:
                    op(shift_h[:, 0, :], out[:, 0, :], out[:, 1, :], ALU.mult)
                    so_far()
                    op(shift_h[:, 1, :], zero4, shift_h[:, 0, :], ALU.subtract)
                    so_far()
                assert steps[0] == total

            def norm_of_x(b):
                norm(b, stat[:, 0], mr[:, 0], stats_x, norm_x)

            def norm_of_h(b):
                norm(b, stat[:, 1], mr[:, 1], stats_h, norm_h, NORM_H)

            def residual(b, first):
                pool.wait_ge(ld_x[b.place], 16 * (b.turn + 1))
                pool.wait_ge(ld_mi[b.place], 16 * (b.turn + 1))
                pool.wait_ge(h_done, 2 * JT * b.n + 2 * JT)
                if not first:
                    pool.wait_ge(x1_done, 2 * (b + -1).n)
                pool.tensor_tensor(xh[:, b.place], h_sb, bcast(mod_in[:, b.place, 2, :], 1, JT),
                                   ALU.mult).then_inc(xh_done, 1)
                pool.wait_ge(xh_done, 2 * b.n + 1)
                pool.tensor_tensor(xh[:, b.place], xh[:, b.place], x_sb[:, b.place],
                                   ALU.add).then_inc(xh_done, 1)

            def first_lo(e):
                for h in range(2):
                    pool.wait_ge(w_hi, 2 * e + h + 1)
                    pool.tensor_tensor(w_parts[:, e, 1, h * WE:(h + 1) * WE], stage[:, h * WE:(h + 1) * WE],
                                       w_parts[:, e, 0, h * WE:(h + 1) * WE].bitcast(F32),
                                       ALU.subtract).then_inc(w_lo, 1)

            norm_of_x(Batch(0, 0))
            pool.wait_ge(w_in_hi, 1)
            pool.tensor_tensor(w_in_parts[:, 1], w_in, w_in_parts[:, 0].bitcast(F32), ALU.subtract).then_inc(w_in_lo, 1)
            norm_of_h(Batch(0, 0))
            pool.wait_ge(ld_w, 32)
            pool.wait_ge(st_mod, 48)
            residual(Batch(0, 0), True)

            def step(i, first, last):
                if not last:
                    norm_of_x(i + 1)
                    norm_of_h(i + 1)
                if not first:
                    norm(i + -1, stat_c, mr[:, 2], stats_p, norm_p)
                if not first:
                    pool.wait_ge(op_ps, 2 * i.n)
                pool.tensor_tensor(w_ga, w_out, bcast(mod_in[:, i.place, 2, :], 1, KC),
                                   ALU.mult).then_inc(w_ga_done, 1)
                if not last:
                    residual(i + 1, first)
                for j in range(1 if last else KC):
                    pool.wait_ge(zg_done, KC * i.n + j + 1)
                    pool.wait_ge(t_done, KC * i.n + j + 1)
                    pool.tensor_tensor(y_sb[:, j, :], conv[:, j, :], zg[:, j, :],
                                       ALU.mult).then_inc(y_done, 1)
                if first:
                    first_lo(0)
            batches(pool, step)
            first_lo(1)
            norm(Batch(B // 2 - 1, 1), stat_c, mr[:, 2], stats_p, norm_p)

            pool.wait_ge(ro_d, HI_READY)
            pool.tensor_tensor(hot[:, 1], hot_hi, bcast(tile1[:, :], 2, SLOTS), ALU.mult).then_inc(hot_done, 1)

            pool.wait_ge(st_rec, AHEAD + 16 * B)
            pool.wait_ge(st_mod, 16 * (3 + B))
            pool.wait_ge(ro_d, INDEX_READY)

            GATHER, SCATTER = 0, 1

            def pick(what, k):
                pool.tensor_copy(idx_k[:, what, k.place:k.place + 1], idx_i[:, what, bass.ds(k.n, 1)]).then_inc(idx_done, 1)

            def gather(k):
                pool.indirect_dma_start(
                    out=rows[:, k.place, :], out_offset=None, in_=table,
                    in_offset=bass.IndirectOffsetOnAxis(ap=idx_k[:, GATHER, k.place:k.place + 1], axis=0)
                ).then_inc(got[k.place], 16)

            def scatter(k):
                pool.indirect_dma_start(
                    out=out.rearrange("b l d -> (b l) d"),
                    out_offset=bass.IndirectOffsetOnAxis(ap=idx_k[:, SCATTER, k.place:k.place + 1], axis=0),
                    in_=res[:, k.place, :], in_offset=None,
                    bounds_check=T - 1, oob_is_err=False).then_inc(put[k.place], 16)

            def turn(k, first=False):
                if not first:
                    before = k + -1
                    hold(pool, put[before.place], 16 * (before.turn + 1))
                hold(pool, res_done, AHEAD + k.n + 1)
                pick(GATHER, k + Tile.TURN)
                pick(SCATTER, k)
                hold(pool, idx_done, 2 * k.n + Tile.TURN + 2)
                gather(k + Tile.TURN)
                scatter(k)

            def leave(k):
                pool.wait_ge(put[k.place], 16 * k.turn)
                pick(SCATTER, k)
                pool.wait_ge(res_done, AHEAD + k.n + 1)
                pool.wait_ge(idx_done, k.n + 1 + SLOTS)
                scatter(k)

            for k in range(Tile.TURN):
                pick(GATHER, Tile(0, k))
                pool.wait_ge(idx_done, k + 1)
                gather(Tile(0, k))
            turn(FIRST_TILE, first=True)
            whole = (SLOTS - Tile.TURN - 1) // Tile.TURN
            with pool.Fori(0, whole) as r:
                for p in range(1, Tile.TURN + 1):
                    turn(Tile(r, p))
            for k in range(whole * Tile.TURN + 1, SLOTS - Tile.TURN):
                turn(Tile(0, 0) + k)
            for k in range(SLOTS - Tile.TURN, SLOTS):
                leave(Tile(0, 0) + k)
            for p in range(Tile.TURN):
                pool.wait_ge(put[p], 16 * ((SLOTS - p + Tile.TURN - 1) // Tile.TURN))

        @block.vector
        def _(dve):
            def chain(done):
                steps = [0]

                def link(ins):
                    steps[0] += 1
                    ins.then_inc(done, 1)
                    dve.wait_ge(done, steps[0])
                return link, steps

            def stats_in(b):
                dve.wait_ge(ld_x[b.place], 16 * (b.turn + 1))
                for j in range(JT):
                    dve.bn_stats(stat[:, 0, j, :], x_sb[:, b.place, j, :]).then_inc(stats_x, 1)

            def modulate_scale(b):
                dve.wait_ge(xh_done, 2 * b.n)
                dve.wait_ge(xn_done, JT * b.n)
                dve.wait_ge(ld_mi[b.place], 16 * (b.turn + 1))
                dve.wait_ge(norm_x, NORM * (b.n + 1))
                for j in range(JT):
                    dve.scalar_tensor_tensor(h_sb[:, j, :], x_sb[:, b.place, j, :], mr[:, 0, 0, j:j + 1],
                                             mod_in[:, b.place, 1, :], ALU.subtract, ALU.mult).then_inc(h_done, 1)

            def modulate_shift(b):
                for j in range(JT):
                    dve.wait_ge(h_done, 2 * JT * b.n + j + 1)
                    dve.scalar_tensor_tensor(h_sb[:, j, :], h_sb[:, j, :], mr[:, 0, 1, j:j + 1],
                                             mod_in[:, b.place, 0, :], ALU.mult, ALU.add).then_inc(h_done, 1)

            def stats_h_in(b):
                for j in range(JT):
                    dve.wait_ge(h_done, 2 * JT * b.n + JT + j + 1)
                    dve.bn_stats(stat[:, 1, j, :], h_sb[:, j, :]).then_inc(stats_h, 1)

            start_ahead(dve, lg_done, res_done, gated)
            link, chained = chain(su_d)
            dve.wait_ge(su_a, 1)
            link(dve.tensor_tensor(silc[:, 0], silc[:, 0], silc[:, 1], ALU.mult))
            row = [banks[v // 2][0:B, (v % 2) * D:(v % 2) * D + D] for v in range(NM)]
            dst = [mod_sb[:, v * D:(v + 1) * D] for v in range(NM)]
            for v in range(NM):
                if v == 3:
                    assert chained[0] == MOD_IN_READY
                    stats_in(Batch(0, 0))
                dve.wait_ge(su_m, v // 2 + 1)
                if v % 3 == 0:
                    link(dve.tensor_copy(dst[v], row[v]))
                elif v % 3 == 1:
                    link(dve.tensor_scalar(dst[v], row[v], 1.0, None, ALU.add))
                else:
                    link(dve.tensor_scalar(sgn[:, 0:D], row[v], 0.0, 2.0, ALU.is_ge, ALU.mult))
                    link(dve.tensor_copy(dst[v], row[v]))
                    link(dve.scalar_tensor_tensor(sgn[:, D:2 * D], dst[v], -1.0, dst[v], ALU.mult, ALU.max))
                    link(dve.tensor_scalar(sgn[:, D:2 * D], sgn[:, D:2 * D], 0.25, None, ALU.max))
                    link(dve.scalar_tensor_tensor(dst[v], sgn[:, 0:D], -1.0, sgn[:, D:2 * D], ALU.add, ALU.mult))
            assert chained[0] == MOD_READY
            link_w, powers_made = chain(su_w)
            dve.wait_ge(cst, N_CONST)
            dve.wait_ge(ld_small, 16 * 12)
            link_w(dve.tensor_copy(powers[:, 0, CH * NS:(CH + 1) * NS], ident[0:NS, 0:NS]))
            dve.wait_ge(su_p, 1)
            link_w(dve.tensor_copy(g_in[:, :, :], banks[3][:, 0:KD * NS].rearrange("p (k n) -> p k n", k=KD)))
            two = banks[4][0:NS, 0:2 * NS].rearrange("p (v n) -> p v n", v=2)
            for k in range(2, CH + 1):
                if k == CH - 1:
                    modulate_scale(Batch(0, 0))
                    modulate_shift(Batch(0, 0))
                    stats_h_in(Batch(0, 0))
                dve.wait_ge(su_p, k)
                link_w(dve.tensor_copy(powers[:, :, (CH - k) * NS:(CH - k + 1) * NS], two))
            link_w(dve.tensor_copy(dbl[:, 0], two))
            for lv in range(1, LEVELS):
                dve.wait_ge(su_p, CH + lv)
                link_w(dve.tensor_copy(dbl[:, lv], two))
            assert powers_made[0] == POWERS_READY

            def taps(i, j):
                dve.wait_ge(tap0_done, KC * i.n + j + 1)
                for d in range(1, TAPS):
                    if d > 1:
                        dve.wait_ge(conv_done, 3 * KC * i.n + 3 * j + d - 1)
                    dve.scalar_tensor_tensor(conv[:, j, d:], rot[j][:, 0:L - d],
                                             cw[:, j, TAPS - 1 - d:TAPS - d], conv[:, j, d:],
                                             ALU.mult, ALU.add).then_inc(conv_done, 1)

            def xn_low(b):
                dve.wait_ge(xn_hi, KD * (b.n + 1))
                dve.tensor_tensor(xnT_parts[:, 1], xnT, xnT_parts[:, 0].bitcast(F32), ALU.subtract).then_inc(xn_lo, 1)

            def chunk_states(i):
                dve.wait_ge(so_ps, KC * i.n)
                dve.wait_ge(loc_ps, i.n + 1)
                dve.tensor_copy(l_state[:, :], state_ps[:, 0:NC]).then_inc(scan_done, 1)
                dve.tensor_copy(e_state[:, :], state_ps[0:NS, 0:NC]).then_inc(scan_done, 1)

            def double(i, lv):
                m = 1 << lv
                dve.wait_ge(scan_ps, (LEVELS + 1) * i.n + lv + 1)
                dve.tensor_tensor(e_state[:, m:], e_state[:, m:], state_ps[0:NS, NC:2 * NC - m],
                                  ALU.add).then_inc(scan_done, 1)

            def all_states(i):
                dve.wait_ge(scan_ps, (LEVELS + 1) * (i.n + 1))
                dve.tensor_tensor(l_state[:, 1:], l_state[:, 1:], state_ps[:, 2 * NC:3 * NC - 1],
                                  ALU.add).then_inc(scan_done, 1)
                dve.wait_ge(scan_done, SCAN * i.n + LEVELS + 3)
                dve.tensor_tensor(spread.rearrange("p (c t) -> p c t", t=CH), bcast(l_state[:, :], 2, CH),
                                  bcast(own_row[:, :], 1, NC), ALU.mult).then_inc(scan_done, 1)

            def add_states(i, j):
                dve.wait_ge(silu_done, KC * i.n + j + 1)
                dve.wait_ge(so_ps, KC * i.n + j + 1)
                dve.tensor_tensor(conv[:, j, :], conv[:, j, :], rot[j], ALU.add).then_inc(t_done, 1)

            def residual_out(b):
                dve.wait_ge(st_rec, AHEAD + 16 * b.n)
                dve.wait_ge(h2_trans, AHEAD + KD * b.n)
                dve.wait_ge(xh_done, 2 * b.n + 2)
                for h in range(2):
                    dve.wait_ge(op_ps, 2 * b.n + h + 1)
                    dve.tensor_tensor(rec[:, 2 * h:2 * h + 2, D:], banks[OUT0 + h][:, :].rearrange("p (j d) -> p j d", j=2),
                                      xh[:, b.place, 2 * h:2 * h + 2, :], ALU.add).then_inc(x1_done, 1)
                for h in range(2):
                    dve.wait_ge(x1_done, 2 * b.n + h + 1)
                    for j in (2 * h, 2 * h + 1):
                        dve.bn_stats(stat_c[:, j, :], rec[:, j, D:]).then_inc(stats_p, 1)

            def modulate_out(b):
                dve.wait_ge(ld_mp[b.place], 16 * (b.turn + 1))
                dve.wait_ge(norm_p, NORM * (b.n + 1))
                for j in range(JT):
                    dve.scalar_tensor_tensor(rec[:, j, 0:D], rec[:, j, D:], mr[:, 2, 0, j:j + 1],
                                             mod_post[:, b.place, 1, :], ALU.subtract, ALU.mult).then_inc(h2_done, 1)
                for j in range(JT):
                    dve.wait_ge(h2_done, 2 * JT * b.n + j + 1)
                    dve.scalar_tensor_tensor(rec[:, j, 0:D], rec[:, j, 0:D], mr[:, 2, 1, j:j + 1],
                                             mod_post[:, b.place, 0, :], ALU.mult, ALU.add).then_inc(h2_done, 1)

            def keep_logits(b):
                dve.wait_ge(lg_ps, b.n + 1)
                dve.tensor_tensor(logits[:, bass.ds(b.n * JT, JT), :],
                                  banks[OUT0][:, 0:JT * E].rearrange("p (j e) -> p j e", j=JT),
                                  bcast(br_sb[:, :], 1, JT), ALU.add).then_inc(lg_done, 1)

            xn_low(Batch(0, 0))
            link(dve.tensor_copy(bias_3[:, 0], bias_raw))
            link(dve.tensor_tensor(bias_rest[:, 0], bias_raw, bias_3[:, 0], ALU.subtract))
            link(dve.tensor_copy(bias_3[:, 1], bias_rest[:, 0]))
            link(dve.tensor_tensor(bias_rest[:, 1], bias_rest[:, 0], bias_3[:, 1], ALU.subtract))
            link(dve.tensor_copy(bias_3[:, 2], bias_rest[:, 1]))
            assert chained[0] == BIAS_READY

            def step(i, first, last):
                chunk_states(i)
                if not last:
                    stats_in(i + 1)
                double(i, 0)
                double(i, 1)
                if not last:
                    modulate_scale(i + 1)
                double(i, 2)
                if not last:
                    modulate_shift(i + 1)
                double(i, 3)
                if not last:
                    stats_h_in(i + 1)
                double(i, 4)
                taps(i, 0)
                double(i, 5)
                taps(i, 1)
                all_states(i)
                if not first:
                    residual_out(i + -1)
                taps(i, 2)
                if not first:
                    modulate_out(i + -1)
                taps(i, 3)
                if not last:
                    xn_low(i + 1)
                for j in range(KC):
                    add_states(i, j)
                if first:
                    dve.wait_ge(st_bias, 16)
                if last:
                    for j in range(1, KC):
                        dve.wait_ge(t_done, KC * i.n + j + 1)
                        dve.tensor_tensor(y_sb[:, j, :], conv[:, j, :], zg[:, j, :], ALU.mult).then_inc(y_done, 1)
                if not first:
                    keep_logits(i + -1)
            batches(dve, step)
            residual_out(Batch(B // 2 - 1, 1))
            modulate_out(Batch(B // 2 - 1, 1))
            keep_logits(Batch(B // 2 - 1, 1))

            route, chained = chain(ro_d)
            lg = logits[:, :, :]
            dve.wait_ge(lg_done, AHEAD + B)
            route(dve.tensor_reduce(r_m1, lg, AX.X, ALU.max))
            route(dve.tensor_tensor(r_val, lg, bcast(r_m1, 2, E), ALU.is_equal))
            route(dve.tensor_tensor(r_val, r_val, bcast(rev[:, :], 1, NT), ALU.mult))
            route(dve.tensor_reduce(r_mv, r_val, AX.X, ALU.max))
            hot_te = onehot.rearrange("p (e t) -> p t e", e=E)
            route(dve.tensor_tensor(hot_te, r_val, bcast(r_mv, 2, E), ALU.is_equal))
            assert chained[0] == HOT_READY
            route(dve.scalar_tensor_tensor(r_low, hot_te, -1e30, lg, ALU.mult, ALU.add))
            route(dve.tensor_reduce(r_m2, r_low, AX.X, ALU.max))
            route(dve.tensor_tensor(r_dif, r_m1, r_m2, ALU.subtract))
            assert chained[0] == DIFF_READY
            dve.wait_ge(ro_p, 1)
            route(dve.tensor_copy(r_cnt2[:, :], banks[2][:, 0:2]))
            for c in range(2):
                route(dve.tensor_scalar(r_cntb[:, c, :], ones_bf[:, :], r_cnt2[:, c:c + 1], None, ALU.mult))
            assert chained[0] == CNTB_READY
            dve.wait_ge(ro_p, 2)
            start, count, ntile, first_t, end_t, off = (r_e[:, v, 0:E] for v in range(6))
            route(dve.tensor_copy(start, banks[3][:, 0:2 * P].rearrange("p (e t) -> p e t", e=E)[:, :, 0]))
            route(dve.tensor_tensor(count, r_e[:, 0, 1:E + 1], start, ALU.subtract))
            cmp = r_cmp[:, 0:E * NT].rearrange("p (e t) -> p e t", e=E)
            route(dve.tensor_tensor(cmp, bcast(count, 2, NT), bcast(k128[:, :], 1, E), ALU.is_gt))
            route(dve.tensor_reduce(ntile, cmp, AX.X, ALU.add))
            route(dve.tensor_scalar(ntile, ntile, 1.0, None, ALU.max))
            cmp = r_cmp[:, 0:E * E].rearrange("p (e f) -> p e f", e=E)
            route(dve.tensor_tensor(cmp, lt_e[:, :, :], bcast(ntile, 1, E), ALU.mult))
            route(dve.tensor_reduce(first_t, cmp, AX.X, ALU.add))
            route(dve.tensor_tensor(end_t, first_t, ntile, ALU.add))
            route(dve.scalar_tensor_tensor(off, first_t, float(P), start, ALU.mult, ALU.subtract))
            dve.wait_ge(ro_p, 3)
            route(dve.tensor_tensor(r_sum, banks[4][:, 0:2 * P].rearrange("p (e t) -> p e t", e=E),
                                    bcast(off, 2, NT), ALU.add))
            route(dve.tensor_tensor(r_sum, r_sum, onehot.rearrange("p (e t) -> p e t", e=E), ALU.mult))
            route(dve.tensor_reduce(r_slot_f, r_sum.rearrange("p e t -> p t e"), AX.X, ALU.add))
            route(dve.tensor_copy(r_slot, r_slot_f))
            route(dve.tensor_scalar(r_lo, r_slot, P - 1, None, ALU.bitwise_and))
            route(dve.tensor_scalar(r_hi, r_slot, P.bit_length() - 1, None, ALU.arith_shift_right))
            route(dve.tensor_tensor(hot_hi, bcast(iota[:, 0:SLOTS], 1, NT), bcast(r_hi, 2, SLOTS), ALU.is_equal))
            assert chained[0] == HI_READY
            for c in range(LO_CUTS):
                cut = slice(c * NT // LO_CUTS, (c + 1) * NT // LO_CUTS)
                route(dve.tensor_tensor(hot_lo[:, cut, :], bcast(iota[:, :], 1, NT // LO_CUTS),
                                        bcast(r_lo[:, cut], 2, P), ALU.is_equal))
            assert chained[0] == LO_READY
            dve.wait_ge(ro_a, 1)
            route(dve.tensor_copy(gate_3[:, 0, :], r_gate))
            route(dve.tensor_tensor(gate_rest[:, 0, :], r_gate, gate_3[:, 0, :], ALU.subtract))
            route(dve.tensor_copy(gate_3[:, 1, :], gate_rest[:, 0, :]))
            route(dve.tensor_tensor(gate_rest[:, 1, :], gate_rest[:, 0, :], gate_3[:, 1, :], ALU.subtract))
            route(dve.tensor_copy(gate_3[:, 2, :], gate_rest[:, 1, :]))
            dve.wait_ge(ro_p, 4)
            route(dve.tensor_copy(inv_2, banks[5][:, 0:2 * SLOTS].rearrange("p (v k) -> p v k", v=2)))
            route(dve.scalar_tensor_tensor(inv[:, 0, :], inv_2[:, 0, :], float(P), inv_2[:, 1, :], ALU.mult, ALU.add))
            route(dve.tensor_scalar(idx_i[:, 0, :], inv[:, 0, :], -float(P), 0.0, ALU.add, ALU.max))
            route(dve.tensor_scalar(idx_f[:, 1, :], inv[:, 0, :], 0.0, float(FAR), ALU.is_equal, ALU.mult))
            route(dve.scalar_tensor_tensor(idx_i[:, 1, :], idx_f[:, 1, :], -float(P), inv[:, 0, :], ALU.add, ALU.add))
            assert chained[0] == INDEX_READY
            cmp = r_cmp[0:1, 0:SLOTS * E].rearrange("p (k e) -> p k e", k=SLOTS)
            route(dve.tensor_tensor(cmp, bcast(iota[0:1, 0:SLOTS], 2, E), bcast(end_t[0:1, :], 1, SLOTS), ALU.is_ge))
            route(dve.tensor_reduce(ek_f[:, 1, :], cmp, AX.X, ALU.add))
            route(dve.tensor_scalar(ek_f[:, 0, :], ek_f[:, 1, :], float(E - 1), None, ALU.min))
            route(dve.tensor_copy(tile_tab[:, EXPERT, :], ek_f[:, 0, :]))
            route(dve.tensor_scalar(tile_tab[:, PLACE, :], tile_tab[:, EXPERT, :], 1, None, ALU.bitwise_and))
            route(dve.tensor_scalar(tile_tab[:, OTHER, :], tile_tab[:, PLACE, :], 0, None, ALU.is_equal))
            route(dve.tensor_tensor(ek_f[:, 1, 1:], ek_f[:, 0, 1:], ek_f[:, 0, 0:SLOTS - 1], ALU.subtract))
            route(dve.tensor_scalar(ek_f[:, 0, :], ek_f[:, 0, :], float(E - 1), None, ALU.is_lt))
            route(dve.tensor_scalar(tile_tab[:, PART, 0:1], tile_tab[:, EXPERT, 0:1], 0, None, ALU.mult))
            route(dve.tensor_tensor(tile_tab[:, PART, 1:], ek_f[:, 1, 1:], ek_f[:, 0, 1:], ALU.mult))
            assert chained[0] == TABLE_READY

            def hT_low(k):
                dve.wait_ge(hT_hi, k.n + 1)
                dve.tensor_tensor(hT[:, k.place % 2, 1, :], banks[0][:, 0:D], hT[:, k.place % 2, 0, :].bitcast(F32),
                                  ALU.subtract).then_inc(hT_lo, 1)

            def hidT_low(k):
                for h in range(2):
                    dve.wait_ge(hidT_hi, 2 * k.n + h + 1)
                    dve.tensor_tensor(hidT[:, 1, 512 * h:512 * h + 512], banks[5 + h][:, :],
                                      hidT[:, 0, 512 * h:512 * h + 512].bitcast(F32), ALU.subtract).then_inc(hidT_lo, 1)

            def part(k, h):
                with dve.If(lookup(dve, PART, k) > 0):
                    e, other = lookup(dve, EXPERT, k), lookup(dve, OTHER, k)
                    dve.wait_ge(w_hi, 2 * e + 3 + h)
                    dve.tensor_tensor(at(w_parts[:, :, 1, h * WE:(h + 1) * WE], other),
                                      at(raw[:, :, h * WE:(h + 1) * WE], other),
                                      at(w_parts[:, :, 0, h * WE:(h + 1) * WE].bitcast(F32), other),
                                      ALU.subtract).then_inc(w_lo, 1)

            def finish(k):
                dve.wait_ge(f2_ps, k.n + 1)
                dve.scalar_tensor_tensor(res[:, k.place, :], banks[7][:, 0:D], inv[:, 1, bass.ds(k.n, 1)],
                                         rows[:, k.place, 2 * D:], ALU.mult, ALU.mult).then_inc(gated, 1)
                dve.wait_ge(gated, AHEAD + k.n + 1)
                dve.tensor_tensor(res[:, k.place, :], res[:, k.place, :], rows[:, k.place, D:2 * D],
                                  ALU.add).then_inc(res_done, 1)

            hT_low(FIRST_TILE)
            hT_low(FIRST_TILE + 1)
            for v in range(3):
                route(dve.tensor_tensor(hot[:, 3 + v], hot_hi, bcast(gate_3[:, v, :], 2, SLOTS), ALU.mult))
            assert chained[0] == GATES_READY
            dve.wait_ge(ro_p, 5)
            route(dve.tensor_copy(inv[:, 1, :], banks[6][:, 0:SLOTS]))

            def tile(k):
                hidT_low(k + -1)
                if not is_last(k):
                    hT_low(k + 1)
                part(k + -1, 1)
                part(k, 0)
                finish(k + -1)
            tiles(dve, tile)
            hidT_low(LAST_TILE)
            before = LAST_TILE + -Tile.TURN
            dve.wait_ge(put[before.place], 16 * (before.turn + 1))
            finish(LAST_TILE)

        @block.tensor
        def _(pe):
            def matmul_parts(bank, xT, w, start, stop=False):
                pe.matmul(bank, xT[0], w[0], start=start, stop=False)
                pe.matmul(bank, xT[0], w[1], start=False, stop=False)
                return pe.matmul(bank, xT[1], w[0], start=False, stop=stop)

            start_ahead(pe, h2_trans, t2_ps)
            pe.wait_ge(su_d, 1)
            for v in range(NM // 2):
                for k in range(KD):
                    mm = pe.matmul(banks[v][0:B, :], silc[:, 0, k, :], wmod_sb[:, k, v * 512:(v + 1) * 512],
                                   start=(k == 0), stop=(k == KD - 1))
                mm.then_inc(su_m, 1)
            pe.wait_ge(ld_small, 16 * 12)
            for c in range(KD):
                for k in range(KC):
                    mm = pe.matmul(banks[3][:, c * NS:(c + 1) * NS], wx_nat[:, k, c * P:(c + 1) * P], bmT[:, k, :],
                                   start=(k == 0), stop=(k == KC - 1))
            mm.then_inc(su_p, 1)
            at_pow = [powers[:, 0, j * NS:(j + 1) * NS] for j in range(CH + 1)]
            a_pow = [powers[:, 1, j * NS:(j + 1) * NS] for j in range(CH)]
            for k in range(2, CH + 1):
                pe.wait_ge(su_w, k)
                pe.matmul(banks[4][0:NS, 0:NS], a_pow[CH - 1], at_pow[CH - k + 1], start=True, stop=True)
                pe.matmul(banks[4][0:NS, NS:2 * NS], at_pow[CH - 1], a_pow[CH - k + 1],
                          start=True, stop=True).then_inc(su_p, 1)
            pe.wait_ge(su_d, MOD_READY)
            pe.wait_ge(ld_w, 32)
            pe.wait_ge(ld_cm, 16 * CH)
            pe.wait_ge(cst, N_CONST)

            def xn_transpose(b, first):
                for k in range(KD):
                    if k == 1 and not first:
                        pe.wait_ge(x1_done, 2 * (b + -1).n)
                    for j in range(JT):
                        if k == 0:
                            pe.wait_ge(xn_done, JT * b.n + j + 1)
                        tr = pe.transpose(banks[TR[k]][:, j * P:(j + 1) * P], xn_sb[:, j, k * P:(k + 1) * P], ident[:, :])
                    tr.then_inc(xn_trans, 1)

            def state_inputs(b):
                pe.wait_ge(xnT_done, KD * (b.n + 1))
                for k in range(KD):
                    mm = pe.matmul(banks[TR[1]][0:NS, :], g_in[:, k, :], xnT[:, k, :], start=(k == 0), stop=(k == KD - 1))
                mm.then_inc(v_ps, 1)

            def local_states(b):
                pe.wait_ge(v_done, b.n + 1)
                for s in range(CH):
                    mm = pe.matmul(state_ps[:, 0:NC], powers[:, 0, (s + 1) * NS:(s + 1) * NS + P], v_sb[:, s::CH],
                                   start=(s == 0), stop=(s == CH - 1))
                mm.then_inc(loc_ps, 1)

            def project(b, j, is_x):
                c = j * P + (0 if is_x else DI)
                if j == 0 and not is_x:
                    pe.wait_ge(xn_lo, b.n + 1)
                for k in range(KD):
                    mm = matmul_parts(rot[j], [w_in_parts[:, v, k, c:c + P] for v in range(2)],
                                      [xnT_parts[:, v, k, :] for v in range(2)], k == 0, k == KD - 1)
                mm.then_inc(xz_ps, 1)

            def double(i, lv):
                m = 1 << lv
                hold(pe, scan_done, SCAN * i.n + 2 + lv)
                pe.matmul(state_ps[0:NS, NC:2 * NC - m], dbl[:, lv, 0], e_state[:, 0:NC - m],
                          start=True, stop=True).then_inc(scan_ps, 1)

            def carry_states(i):
                pe.wait_ge(scan_done, SCAN * i.n + 2 + LEVELS)
                pe.matmul(state_ps[:, 2 * NC:3 * NC - 1], powers[:, 0, 0:CH * NS], e_state[:, 0:NC - 1],
                          start=True, stop=True).then_inc(scan_ps, 1)

            def state_out(i, j):
                if j == 0:
                    pe.wait_ge(scan_done, SCAN * (i.n + 1))
                pe.wait_ge(conv_done, 3 * KC * i.n + 3 * j + 3)
                pe.matmul(rot[j], cm_t[:, j * P:(j + 1) * P], spread, start=True, stop=True).then_inc(so_ps, 1)

            def project_out(b, j):
                if j == 0:
                    pe.wait_ge(y_done, KC * (b.n + 1))
                    pe.wait_ge(w_ga_done, b.n + 1)
                    pe.wait_ge(lg_done, AHEAD + b.n)
                for k in range(KC):
                    mm = pe.matmul(banks[OUT0 + j // 2][:, (j % 2) * D:(j % 2 + 1) * D],
                                   y_sb[:, k, j * P:(j + 1) * P], w_ga[:, k, :], start=(k == 0), stop=(k == KC - 1))
                if j % 2 == 1:
                    mm.then_inc(op_ps, 1)

            def h2_transpose(b, v_left):
                for k in range(KD):
                    if k == 1:
                        pe.wait_ge(v_done, v_left)
                    for j in range(JT):
                        if k == 0:
                            pe.wait_ge(h2_done, 2 * JT * b.n + JT + j + 1)
                        tr = pe.transpose(banks[TR[k]][:, j * P:(j + 1) * P], rec[:, j, k * P:(k + 1) * P], ident[:, :])
                    tr.then_inc(h2_trans, 1)

            def router(b):
                pe.wait_ge(h2T_done, KD * (b.n + 1))
                for j in range(JT):
                    for k in range(KD):
                        mm = pe.matmul(banks[OUT0][:, j * E:(j + 1) * E], h2T[:, k, j * P:(j + 1) * P], wr_sb[:, k, :],
                                       start=(k == 0), stop=(k == KD - 1))
                mm.then_inc(lg_ps, 1)

            for lv in range(1, LEVELS):
                pe.wait_ge(su_w, CH + 1 + lv)
                pe.matmul(banks[4][0:NS, 0:NS], dbl[:, lv - 1, 1], dbl[:, lv - 1, 0], start=True, stop=True)
                pe.matmul(banks[4][0:NS, NS:2 * NS], dbl[:, lv - 1, 0], dbl[:, lv - 1, 1],
                          start=True, stop=True).then_inc(su_p, 1)
            xn_transpose(Batch(0, 0), True)
            pe.wait_ge(su_w, POWERS_READY)
            state_inputs(Batch(0, 0))
            pe.wait_ge(w_in_lo, 1)
            local_states(Batch(0, 0))

            def step(i, first, last):
                def project_x(j):
                    pe.wait_ge(zg_done, KC * i.n + j + 1)
                    project(i, j, True)

                for j in range(KC):
                    if not first:
                        pe.wait_ge(t_done, KC * (i + -1).n + j + 1)
                    project(i, j, False)
                    if j >= 1:
                        double(i, j - 1)
                for j in range(2):
                    project_x(j)
                    double(i, j + 3)
                for j in range(JT):
                    if not first:
                        project_out(i + -1, j)
                    if j == 0:
                        double(i, LEVELS - 1)
                    if j == 1:
                        carry_states(i)
                for j in range(2, KC):
                    project_x(j)
                if not last:
                    xn_transpose(i + 1, first)
                state_out(i, 0)
                state_out(i, 1)
                state_out(i, 2)
                if not last:
                    state_inputs(i + 1)
                if not first:
                    h2_transpose(i + -1, i.n + (1 if last else 2))
                if not last:
                    local_states(i + 1)
                state_out(i, 3)
                if not first:
                    router(i + -1)
            batches(pe, step)
            for j in range(JT):
                project_out(Batch(B // 2 - 1, 1), j)
            h2_transpose(Batch(B // 2 - 1, 1), B)
            router(Batch(B // 2 - 1, 1))

            pe.wait_ge(ro_d, HOT_READY)
            for c in range(2):
                mm = pe.matmul(banks[2][:, c:c + 1], onehot[:, c * P:(c + 1) * P], ones_bf[:, 0:1], start=True, stop=True)
            mm.then_inc(ro_p, 1)
            pe.wait_ge(ro_d, CNTB_READY)
            for c in range(2):
                mm = pe.matmul(banks[3][:, 0:2 * P], r_cntb[:, c, :], lt_et[:, c, :], start=(c == 0), stop=(c == 1))
            mm.then_inc(ro_p, 1)
            pe.matmul(banks[4][:, 0:2 * P], lt_tok[:, :], onehot, start=True, stop=False)
            for c in range(2):
                mm = pe.matmul(banks[4][:, 0:2 * P], r_cntb[:, c, :], lt_et[:, c, :], start=False, stop=(c == 1))
            mm.then_inc(ro_p, 1)
            for t in range(NT):
                if t == 0:
                    pe.wait_ge(ro_a, 2)
                    pe.wait_ge(hot_done, 1)
                if t % (NT // LO_CUTS) == 0:
                    pe.wait_ge(ro_d, LO_READY - LO_CUTS + 1 + t // (NT // LO_CUTS))
                mm = pe.matmul(banks[5][:, 0:2 * SLOTS], hot_lo[:, t, :], hot[:, 1:3, t, :], start=(t == 0), stop=(t == NT - 1))
            mm.then_inc(ro_p, 1)

            pe.wait_ge(ld_bias, 16)
            pe.wait_ge(ro_d, TABLE_READY)

            def turn_in(k):
                if k is not FIRST_TILE:
                    pe.wait_ge(hT_lo, k.n)
                pe.wait_ge(got[k.place], 16 * (k.turn + 1))
                for c in range(KD):
                    tr = pe.transpose(banks[0][:, c * P:(c + 1) * P], rows[:, k.place, c * P:(c + 1) * P], ident[:, :])
                tr.then_inc(t1_ps, 1)

            def up(k):
                e, place = lookup(pe, EXPERT, k), lookup(pe, PLACE, k)
                if k is not FIRST_TILE:
                    pe.wait_ge(hid_done, AHEAD + 2 * (k + -1).n)
                hold(pe, w_lo, 2 * e + 1)
                pe.wait_ge(hT_lo, k.n + 1)
                bw = bias1[:, bass.ds(e, 1), :].rearrange("p o n -> p (o n)")
                for h in range(2):
                    bank = banks[1 + 2 * (k.place % 2) + h][:, :]
                    for c in range(KD):
                        cut = slice(c * FF + 512 * h, c * FF + 512 * h + 512)
                        matmul_parts(bank, [hT[:, k.place % 2, v, c * P:(c + 1) * P] for v in range(2)],
                                     [at(w_parts[:, :, v, cut], place) for v in range(2)], c == 0)
                    pe.matmul(bank, ones_bf[0:3, :], bw[:, 512 * h:512 * h + 512],
                              start=False, stop=True).then_inc(f1_ps, 1)

            def turn_hidden(k):
                hold(pe, hid_done, AHEAD + 2 * (k.n + 1))
                for i in range(KF):
                    tr = pe.transpose(banks[5 + i // 4][:, (i % 4) * P:(i % 4 + 1) * P],
                                      hid[:, k.place % 2, i * P:(i + 1) * P], ident[:, :])
                    if i % 4 == 3:
                        tr.then_inc(t2_ps, 1)

            def down(k):
                e, place = lookup(pe, EXPERT, k), lookup(pe, PLACE, k)
                hold(pe, gated, AHEAD + k.n)
                hold(pe, w_lo, 2 * e + 2)
                pe.wait_ge(hidT_lo, 2 * k.n + 2)
                bw = bias2[:, bass.ds(e, 1), :].rearrange("p o n -> p (o n)")
                for i in range(KF):
                    matmul_parts(banks[7][:, 0:D], [hidT[:, v, i * P:(i + 1) * P] for v in range(2)],
                                 [at(w_parts[:, :, v, WE + i * D:WE + (i + 1) * D], place) for v in range(2)], i == 0)
                pe.matmul(banks[7][:, 0:D], ones_bf[0:3, :], bw, start=False, stop=True).then_inc(f2_ps, 1)

            turn_in(FIRST_TILE)
            turn_in(FIRST_TILE + 1)
            up(FIRST_TILE)
            pe.wait_ge(ro_d, GATES_READY)
            for t in range(NT):
                for v in range(3):
                    mm = pe.matmul(banks[6][:, 0:SLOTS], hot_lo[:, t, :], hot[:, 3 + v, t, :],
                                   start=(t == 0 and v == 0), stop=(t == NT - 1 and v == 2))
            mm.then_inc(ro_p, 1)
            pe.wait_ge(ro_d, GATES_READY + 1)

            def tile(k):
                turn_hidden(k + -1)
                if not is_last(k):
                    turn_in(k + 1)
                up(k)
                down(k + -1)
            tiles(pe, tile)
            turn_hidden(LAST_TILE)
            down(LAST_TILE)


_INS = ['x', 'ln_gamma', 'ln_beta', 'W_in', 'W_inT', 'conv_w', 'conv_b', 'W_outT', 'A', 'AT', 'BmT', 'Cm',
        'w1', 'b1', 'w2', 'b2', 'wr', 'br', 'cT', 'wmod']
_OUTS = [((8, 512, 256), 'float32')]


def kernel(**inputs):
    import numpy as _np
    import concourse.bacc as _bacc
    from concourse import mybir as _mybir
    from concourse.bass_utils import run_bass_kernel_spmd as _run

    given = {n.replace('L0_attn_', '').replace('L0_ffn_', '').replace('L0_', ''): _np.asarray(a)
             for n, a in inputs.items()}
    for name, of in (('W_inT', 'W_in'), ('W_outT', 'W_out'), ('AT', 'A'), ('BmT', 'Bm'), ('cT', 'c')):
        given[name] = given[of].T
    for name in ('ln_gamma', 'ln_beta', 'conv_b', 'conv_w'):
        a = given[name]
        given[name] = a.reshape((a.shape[0] // P, P) + a.shape[2:]).swapaxes(0, 1)
    nc = _bacc.Bacc("TRN2", target_bir_lowering=False, num_devices=1)
    arrays, args = {}, []
    for name in _INS:
        a = _np.ascontiguousarray(given[name])
        arrays[f"in_{name}_dram"] = a
        args.append(nc.dram_tensor(f"in_{name}_dram", a.shape, _mybir.dt.from_np(a.dtype), kind="ExternalInput").ap())
    for i, (shape, dtype) in enumerate(_OUTS):
        dt = _mybir.dt.from_np(_np.dtype(dtype))
        args.append(nc.dram_tensor(f"out_{i}_dram", shape, dt, kind="ExternalOutput").ap())
    adaln_mamba_moe(nc, *args)
    r = _run(nc, [arrays], core_ids=[0])
    return r.results[0]["out_0_dram"]
```
